# Optimizing a Trainium2 kernel written in Bass

```python
import numpy as np
import jax
import jax.numpy as jnp

def _softmax(x, axis=-1):
    return jax.nn.softmax(x, axis=axis)

def _gelu(x):
    return jax.nn.gelu(x, approximate=True)

def _silu(x):
    return jax.nn.silu(x)

def _sigmoid(x):
    return jax.nn.sigmoid(x)

def _layernorm(x, axis=-1, eps=1e-05):
    m = jnp.mean(x, axis=axis, keepdims=True)
    v = jnp.var(x, axis=axis, keepdims=True)
    return (x - m) / jnp.sqrt(v + eps)

def _scatter_add(tgt, idx, src, axis=0):
    return tgt.at[idx].add(src)

def _segment_sum(src, seg, n):
    return jax.ops.segment_sum(src, seg, n)
kernel_name = 'mk_decoder_preln_d1_seqx_r4_97deeb'

def setup_inputs(seed: int=0):
    np.random.seed(seed)
    _w = jnp.asarray

    def _rec_inputs():
        import jax
        import jax.numpy as jnp
        _rk = jax.random.key(seed)
        x = -0.0002928 + 1 * jax.random.normal(jax.random.fold_in(_rk, 1), (16, 128, 256), jnp.float32)
        _lenS = 128 - jax.random.randint(jax.random.fold_in(_rk, 7), (16,), 0, max(1, 128 // 4) + 1, jnp.int32)
        _lenS2 = 128 - jax.random.randint(jax.random.fold_in(_rk, 8), (16,), 0, max(1, 128 // 4) + 1, jnp.int32)
        _ctx_1024P = jax.random.normal(jax.random.fold_in(_rk, 11), (16, 16, 256), jnp.float32)
        _ctx_1024c = jax.random.dirichlet(jax.random.fold_in(_rk, 511), 0.3 * jnp.ones((16,), jnp.float32), (16, 128))
        _ctx_1024t = jnp.einsum('bsk,bkd->bsd', _ctx_1024c, _ctx_1024P)
        _ctx_1024t = _ctx_1024t * jax.lax.rsqrt(jnp.mean(jnp.square(_ctx_1024t)) + 1e-12) * 0.953939
        ctx_1024 = -1.39393e-06 + 0.999914 * (_ctx_1024t + 0.3 * jax.random.normal(jax.random.fold_in(_rk, 611), (16, 128, 256), jnp.float32))
        return (x, ctx_1024)
    x, ctx_1024 = _rec_inputs()

    def _L0_attn_setup():
        import jax, jax.numpy as jnp
        import numpy as np
        from jax import lax
        H = 256
        EXPAND = 2
        I = EXPAND * H
        N = 16
        K = 4
        R = 64
        EPS = 1e-06
        B_SZ, L = (2, 256)

        def rmsnorm(x, w):
            v = jnp.mean(x.astype(jnp.float32) ** 2, axis=-1, keepdims=True)
            return w * (x * jax.lax.rsqrt(v + EPS)).astype(x.dtype)
        key = jax.random.key(seed)
        ks = jax.random.split(key, 10)
        s = 0.02
        inp = {'hidden_states': jax.random.normal(ks[0], (B_SZ, L, H), jnp.float32), 'in_proj_w': jax.random.normal(ks[1], (2 * I, H), jnp.float32) * s, 'conv_w': jax.random.normal(ks[2], (I, 1, K), jnp.float32) * s, 'conv_b': jnp.zeros((I,), jnp.float32), 'x_proj_w': jax.random.normal(ks[3], (R + 2 * N, I), jnp.float32) * s, 'dt_proj_w': jax.random.normal(ks[4], (I, R), jnp.float32) * s, 'dt_proj_b': jax.random.normal(ks[5], (I,), jnp.float32) * 0.1, 'dt_ln_w': jnp.ones((R,), jnp.float32), 'b_ln_w': jnp.ones((N,), jnp.float32), 'c_ln_w': jnp.ones((N,), jnp.float32), 'A_log': jnp.log(jnp.broadcast_to(jnp.arange(1, N + 1, dtype=jnp.float32)[None, :], (I, N))), 'D': jnp.ones((I,), jnp.float32), 'out_proj_w': jax.random.normal(ks[6], (H, I), jnp.float32) * s}
        return inp
    _L0_attn_all = _L0_attn_setup()
    _L0_attn_in = {k: v for k, v in _L0_attn_all.items() if k in ('in_proj_w', 'conv_w', 'conv_b', 'x_proj_w', 'dt_proj_w', 'dt_proj_b', 'dt_ln_w', 'b_ln_w', 'c_ln_w', 'A_log', 'D', 'out_proj_w')}
    del _L0_attn_all

    def _L0_xattn_setup():
        import jax, jax.numpy as jnp
        import numpy as np
        B, S, H, NH = (2, 512, 256, 4)
        DH = H // NH
        EPS_BACKEND = 1e-06
        EPS_LN = 1e-06

        def _mlstm_parallel_stabilized(q, k, v, igate_preact, fgate_preact):
            b, nh, s, dh = q.shape
            log_fg = jax.nn.log_sigmoid(fgate_preact)
            cs = jnp.concatenate([jnp.zeros((b, nh, 1), q.dtype), jnp.cumsum(log_fg[..., 0], axis=2)], axis=2)
            fg_matrix = cs[:, :, :, None] - cs[:, :, None, :]
            fg_matrix = fg_matrix[:, :, 1:, 1:]
            causal = jnp.tril(jnp.ones((s, s), dtype=bool))
            log_fg_matrix = jnp.where(causal, fg_matrix, -jnp.inf)
            log_D = log_fg_matrix + jnp.swapaxes(igate_preact, -2, -1)
            max_log_D = jnp.max(log_D, axis=-1, keepdims=True)
            D = jnp.exp(log_D - max_log_D)
            qk = jnp.einsum('bhsd,bhtd->bhst', q, k) / jnp.sqrt(jnp.asarray(dh, q.dtype))
            C = qk * D
            normalizer = jnp.maximum(jnp.abs(jnp.sum(C, axis=-1, keepdims=True)), jnp.exp(-max_log_D))
            C_norm = C / (normalizer + EPS_BACKEND)
            return jnp.einsum('bhst,bhtd->bhsd', C_norm, v)

        def _multihead_layernorm(x, scale):
            mean = jnp.mean(x, axis=-1, keepdims=True)
            var = jnp.var(x, axis=-1, keepdims=True)
            xn = (x - mean) * jax.lax.rsqrt(var + EPS_LN)
            return xn * scale.reshape(NH, 1, DH)
        key = jax.random.key(seed)
        kq, kk, kv, kib = jax.random.split(key, 4)
        q = jax.random.normal(kq, (B, S, H), dtype=jnp.float32)
        k = jax.random.normal(kk, (B, S, H), dtype=jnp.float32)
        v = jax.random.normal(kv, (B, S, H), dtype=jnp.float32)
        igate_kernel = jnp.zeros((3 * H, NH), dtype=jnp.float32)
        igate_bias = 0.1 * jax.random.normal(kib, (NH,), dtype=jnp.float32)
        fgate_kernel = jnp.zeros((3 * H, NH), dtype=jnp.float32)
        fgate_bias = jnp.linspace(3.0, 6.0, NH, dtype=jnp.float32)
        outnorm_scale = jnp.ones((H,), dtype=jnp.float32)
        return {'q': q, 'k': k, 'v': v, 'igate_kernel': igate_kernel, 'igate_bias': igate_bias, 'fgate_kernel': fgate_kernel, 'fgate_bias': fgate_bias, 'outnorm_scale': outnorm_scale}
    _L0_xattn_all = _L0_xattn_setup()
    _L0_xattn_in = {k: v for k, v in _L0_xattn_all.items() if k in ('igate_kernel', 'igate_bias', 'fgate_kernel', 'fgate_bias', 'outnorm_scale')}
    del _L0_xattn_all

    def _L0_ffn_setup():
        import jax, jax.numpy as jnp
        import numpy as np
        NUM_NOD = 6
        MAX_PREV = 5
        NUM_EDGE = 20
        D = 256
        H = 8
        LN_EPS = 1e-06

        def _layernorm(x, g, b):
            mu = jnp.mean(x, axis=-1, keepdims=True)
            var = jnp.mean(jnp.square(x - mu), axis=-1, keepdims=True)
            return (x - mu) * jax.lax.rsqrt(var + LN_EPS) * g + b

        def _mha(q, k, v, wq, wk, wv, wo):
            B, S, d = q.shape
            dh = d // H
            qh = (q @ wq).reshape(B, S, H, dh)
            kh = (k @ wk).reshape(B, S, H, dh)
            vh = (v @ wv).reshape(B, S, H, dh)
            scores = jnp.einsum('bqhd,bkhd->bhqk', qh, kh) / jnp.sqrt(jnp.asarray(dh, q.dtype))
            attn = jax.nn.softmax(scores, axis=-1)
            ctx = jnp.einsum('bhqk,bkhd->bqhd', attn, vh).reshape(B, S, d)
            return ctx @ wo
        key = jax.random.key(seed)
        ks = jax.random.split(key, 12)
        B, S = (8, 256)
        scale = 1.0 / np.sqrt(D)
        return {'inputs': jax.random.normal(ks[0], (B, S, D), jnp.float32), 'ew': jax.random.uniform(ks[1], (NUM_NOD, 3), jnp.float32), 'act_w': jax.random.uniform(ks[2], (NUM_NOD,), jnp.float32), 'We': jax.random.normal(ks[3], (NUM_EDGE, D, D), jnp.float32) * scale, 'be': jnp.zeros((NUM_EDGE, D), jnp.float32), 'Wq': jax.random.normal(ks[4], (NUM_NOD, D, D), jnp.float32) * scale, 'Wk': jax.random.normal(ks[5], (NUM_NOD, D, D), jnp.float32) * scale, 'Wv': jax.random.normal(ks[6], (NUM_NOD, D, D), jnp.float32) * scale, 'Wo': jax.random.normal(ks[7], (NUM_NOD, D, D), jnp.float32) * scale, 'ln_g': jnp.ones((D,), jnp.float32), 'ln_b': jnp.zeros((D,), jnp.float32)}
    _L0_ffn_all = _L0_ffn_setup()
    _L0_ffn_in = {k: v for k, v in _L0_ffn_all.items() if k in ('ew', 'act_w', 'We', 'be', 'Wq', 'Wk', 'Wv', 'Wo', 'ln_g', 'ln_b')}
    del _L0_ffn_all
    return {'x': x, 'ctx_1024': ctx_1024, 'L0_attn_in_proj_w': _L0_attn_in['in_proj_w'], 'L0_attn_conv_w': _L0_attn_in['conv_w'], 'L0_attn_conv_b': _L0_attn_in['conv_b'], 'L0_attn_x_proj_w': _L0_attn_in['x_proj_w'], 'L0_attn_dt_proj_w': _L0_attn_in['dt_proj_w'], 'L0_attn_dt_proj_b': _L0_attn_in['dt_proj_b'], 'L0_attn_dt_ln_w': _L0_attn_in['dt_ln_w'], 'L0_attn_b_ln_w': _L0_attn_in['b_ln_w'], 'L0_attn_c_ln_w': _L0_attn_in['c_ln_w'], 'L0_attn_A_log': _L0_attn_in['A_log'], 'L0_attn_D': _L0_attn_in['D'], 'L0_attn_out_proj_w': _L0_attn_in['out_proj_w'], 'L0_xattn_igate_kernel': _L0_xattn_in['igate_kernel'], 'L0_xattn_igate_bias': _L0_xattn_in['igate_bias'], 'L0_xattn_fgate_kernel': _L0_xattn_in['fgate_kernel'], 'L0_xattn_fgate_bias': _L0_xattn_in['fgate_bias'], 'L0_xattn_outnorm_scale': _L0_xattn_in['outnorm_scale'], 'L0_ffn_ew': _L0_ffn_in['ew'], 'L0_ffn_act_w': _L0_ffn_in['act_w'], 'L0_ffn_We': _L0_ffn_in['We'], 'L0_ffn_be': _L0_ffn_in['be'], 'L0_ffn_Wq': _L0_ffn_in['Wq'], 'L0_ffn_Wk': _L0_ffn_in['Wk'], 'L0_ffn_Wv': _L0_ffn_in['Wv'], 'L0_ffn_Wo': _L0_ffn_in['Wo'], 'L0_ffn_ln_g': _L0_ffn_in['ln_g'], 'L0_ffn_ln_b': _L0_ffn_in['ln_b']}

def reference(x, ctx_1024, L0_attn_in_proj_w, L0_attn_conv_w, L0_attn_conv_b, L0_attn_x_proj_w, L0_attn_dt_proj_w, L0_attn_dt_proj_b, L0_attn_dt_ln_w, L0_attn_b_ln_w, L0_attn_c_ln_w, L0_attn_A_log, L0_attn_D, L0_attn_out_proj_w, L0_xattn_igate_kernel, L0_xattn_igate_bias, L0_xattn_fgate_kernel, L0_xattn_fgate_bias, L0_xattn_outnorm_scale, L0_ffn_ew, L0_ffn_act_w, L0_ffn_We, L0_ffn_be, L0_ffn_Wq, L0_ffn_Wk, L0_ffn_Wv, L0_ffn_Wo, L0_ffn_ln_g, L0_ffn_ln_b):
    import jax
    import jax.numpy as jnp

    def _L0_attn_ref(hidden_states, in_proj_w, conv_w, conv_b, x_proj_w, dt_proj_w, dt_proj_b, dt_ln_w, b_ln_w, c_ln_w, A_log, D, out_proj_w):
        import jax, jax.numpy as jnp
        import numpy as np
        from jax import lax
        H = 256
        EXPAND = 2
        I = EXPAND * H
        N = 16
        K = 4
        R = 64
        EPS = 1e-06
        B_SZ, L = (2, 256)

        def rmsnorm(x, w):
            v = jnp.mean(x.astype(jnp.float32) ** 2, axis=-1, keepdims=True)
            return w * (x * jax.lax.rsqrt(v + EPS)).astype(x.dtype)
        b, l, _ = hidden_states.shape
        proj = hidden_states @ in_proj_w.T
        hs, gate = (proj[..., :I], proj[..., I:])
        x = jnp.transpose(hs, (0, 2, 1))
        x = lax.conv_general_dilated(x, conv_w, (1,), [(1, 2)], feature_group_count=I, dimension_numbers=('NCH', 'OIH', 'NCH'))
        x = x + conv_b[None, :, None]
        u = jax.nn.silu(jnp.transpose(x, (0, 2, 1)))
        x_dbl = u @ x_proj_w.T
        dt = rmsnorm(x_dbl[..., :R], dt_ln_w)
        Bm = rmsnorm(x_dbl[..., R:R + N], b_ln_w)
        Cm = rmsnorm(x_dbl[..., R + N:], c_ln_w)
        dt = jax.nn.softplus(dt @ dt_proj_w.T + dt_proj_b)
        A = -jnp.exp(A_log)
        dA = jnp.exp(dt[..., None] * A)
        dBu = (dt * u)[..., None] * Bm[:, :, None, :]

        def step(h, inp):
            dA_t, dBu_t = inp
            h = dA_t * h + dBu_t
            return (h, h)
        h0 = jnp.zeros((b, I, N), jnp.float32)
        _, h_seq = lax.scan(step, h0, (jnp.transpose(dA, (1, 0, 2, 3)), jnp.transpose(dBu, (1, 0, 2, 3))))
        y = jnp.einsum('lbin,bln->bli', h_seq, Cm)
        y = y + u * D
        y = y * jax.nn.silu(gate)
        return y @ out_proj_w.T

    def _L0_xattn_ref(q, k, v, igate_kernel, igate_bias, fgate_kernel, fgate_bias, outnorm_scale):
        import jax, jax.numpy as jnp
        import numpy as np
        B, S, H, NH = (2, 512, 256, 4)
        DH = H // NH
        EPS_BACKEND = 1e-06
        EPS_LN = 1e-06

        def _mlstm_parallel_stabilized(q, k, v, igate_preact, fgate_preact):
            b, nh, s, dh = q.shape
            log_fg = jax.nn.log_sigmoid(fgate_preact)
            cs = jnp.concatenate([jnp.zeros((b, nh, 1), q.dtype), jnp.cumsum(log_fg[..., 0], axis=2)], axis=2)
            fg_matrix = cs[:, :, :, None] - cs[:, :, None, :]
            fg_matrix = fg_matrix[:, :, 1:, 1:]
            causal = jnp.tril(jnp.ones((s, s), dtype=bool))
            log_fg_matrix = jnp.where(causal, fg_matrix, -jnp.inf)
            log_D = log_fg_matrix + jnp.swapaxes(igate_preact, -2, -1)
            max_log_D = jnp.max(log_D, axis=-1, keepdims=True)
            D = jnp.exp(log_D - max_log_D)
            qk = jnp.einsum('bhsd,bhtd->bhst', q, k) / jnp.sqrt(jnp.asarray(dh, q.dtype))
            C = qk * D
            normalizer = jnp.maximum(jnp.abs(jnp.sum(C, axis=-1, keepdims=True)), jnp.exp(-max_log_D))
            C_norm = C / (normalizer + EPS_BACKEND)
            return jnp.einsum('bhst,bhtd->bhsd', C_norm, v)

        def _multihead_layernorm(x, scale):
            mean = jnp.mean(x, axis=-1, keepdims=True)
            var = jnp.var(x, axis=-1, keepdims=True)
            xn = (x - mean) * jax.lax.rsqrt(var + EPS_LN)
            return xn * scale.reshape(NH, 1, DH)
        b, s, h = q.shape
        gate_in = jnp.concatenate([q, k, v], axis=-1)
        ig = gate_in @ igate_kernel + igate_bias
        fg = gate_in @ fgate_kernel + fgate_bias
        ig = jnp.transpose(ig, (0, 2, 1))[..., None]
        fg = jnp.transpose(fg, (0, 2, 1))[..., None]
        qh = jnp.transpose(q.reshape(b, s, NH, DH), (0, 2, 1, 3))
        kh = jnp.transpose(k.reshape(b, s, NH, DH), (0, 2, 1, 3))
        vh = jnp.transpose(v.reshape(b, s, NH, DH), (0, 2, 1, 3))
        hs = _mlstm_parallel_stabilized(qh, kh, vh, ig, fg)
        hn = _multihead_layernorm(hs, outnorm_scale)
        return jnp.transpose(hn, (0, 2, 1, 3)).reshape(b, s, h)

    def _L0_ffn_ref(inputs, ew, act_w, We, be, Wq, Wk, Wv, Wo, ln_g, ln_b):
        import jax, jax.numpy as jnp
        import numpy as np
        NUM_NOD = 6
        MAX_PREV = 5
        NUM_EDGE = 20
        D = 256
        H = 8
        LN_EPS = 1e-06

        def _layernorm(x, g, b):
            mu = jnp.mean(x, axis=-1, keepdims=True)
            var = jnp.mean(jnp.square(x - mu), axis=-1, keepdims=True)
            return (x - mu) * jax.lax.rsqrt(var + LN_EPS) * g + b

        def _mha(q, k, v, wq, wk, wv, wo):
            B, S, d = q.shape
            dh = d // H
            qh = (q @ wq).reshape(B, S, H, dh)
            kh = (k @ wk).reshape(B, S, H, dh)
            vh = (v @ wv).reshape(B, S, H, dh)
            scores = jnp.einsum('bqhd,bkhd->bhqk', qh, kh) / jnp.sqrt(jnp.asarray(dh, q.dtype))
            attn = jax.nn.softmax(scores, axis=-1)
            ctx = jnp.einsum('bhqk,bkhd->bqhd', attn, vh).reshape(B, S, d)
            return ctx @ wo
        nodes = {-1: inputs}
        lind = 0
        for c in range(NUM_NOD):
            nsrc = min(c + 1, MAX_PREV)
            snode = c - nsrc
            eq, ek, ev = (lind + nsrc - 1, lind, lind + nsrc // 2)
            in_q, in_k, in_v = (c - 1, snode, snode + nsrc // 2)
            q = ew[c, 0] * (nodes[in_q] @ We[eq] + be[eq])
            k = ew[c, 1] * (nodes[in_k] @ We[ek] + be[ek])
            v = ew[c, 2] * (nodes[in_v] @ We[ev] + be[ev])
            o = _mha(q, k, v, Wq[c], Wk[c], Wv[c], Wo[c])
            nodes[c] = act_w[c] * o + q
            lind += nsrc
        out = nodes[NUM_NOD - 1]
        return _layernorm(out, ln_g, ln_b)
    x = x + _L0_attn_ref(_layernorm(x, axis=-1), L0_attn_in_proj_w, L0_attn_conv_w, L0_attn_conv_b, L0_attn_x_proj_w, L0_attn_dt_proj_w, L0_attn_dt_proj_b, L0_attn_dt_ln_w, L0_attn_b_ln_w, L0_attn_c_ln_w, L0_attn_A_log, L0_attn_D, L0_attn_out_proj_w)
    x = x + _L0_xattn_ref(_layernorm(x, axis=-1), ctx_1024, ctx_1024, L0_xattn_igate_kernel, L0_xattn_igate_bias, L0_xattn_fgate_kernel, L0_xattn_fgate_bias, L0_xattn_outnorm_scale)
    x = x + _L0_ffn_ref(_layernorm(x, axis=-1), L0_ffn_ew, L0_ffn_act_w, L0_ffn_We, L0_ffn_be, L0_ffn_Wq, L0_ffn_Wk, L0_ffn_Wv, L0_ffn_Wo, L0_ffn_ln_g, L0_ffn_ln_b)
    return x

_drawn_inputs = setup_inputs


def setup_inputs(seed=0):
    import zlib

    import numpy as np

    out = dict(_drawn_inputs(seed))
    spreads = {'L0_attn_conv_b': (0.0, 0.1),
     'L0_attn_dt_ln_w': (1.0, 0.2),
     'L0_attn_b_ln_w': (1.0, 0.2),
     'L0_attn_c_ln_w': (1.0, 0.2),
     'L0_attn_D': (1.0, 0.2),
     'L0_xattn_igate_kernel': (0.0, 0.1),
     'L0_xattn_fgate_kernel': (0.0, 0.1),
     'L0_xattn_outnorm_scale': (1.0, 0.2),
     'L0_ffn_be': (0.0, 0.1),
     'L0_ffn_ln_g': (1.0, 0.2),
     'L0_ffn_ln_b': (0.0, 0.1)}
    factors = {}
    for name, (base, spread) in spreads.items():
        noise = np.random.default_rng([zlib.crc32(name.encode()), seed]).standard_normal(out[name].shape)
        drawn = base * np.exp(spread * noise) if base else spread * noise
        out[name] = jnp.asarray(drawn.astype(out[name].dtype))
    for name, factor in factors.items():
        out[name] = (out[name] * factor).astype(out[name].dtype)
    return out
```

```python
from contextlib import ExitStack

import concourse.bass as bass
from concourse import mybir

F32 = mybir.dt.float32
F32R = mybir.dt.float32r
BF16 = mybir.dt.bfloat16
ALU = mybir.AluOpType
ACT = mybir.ActivationFunctionType
AX = mybir.AxisListType

P = 128
B, L, H = 16, 128, 256
GB = 2
T = GB * L
NG = B // GB
HC = H // P
I = 2 * H
IC = I // P
NS = 16
R = 64
XH, XD = 4, 64
XP = XD + 1
NODES, EDGES = 6, 20
FH, FD = 8, 32
HPC = P // FD
BIG = 1e30
LN_EPS, RMS_EPS, HEAD_EPS, OUT_EPS = 1e-5, 1e-6, 1e-6, 1e-6

PAIRS = NS // 4
UNITS = 2 * IC * PAIRS
STEPS = GB * HC

GRAPH = []
_lind = 0
for _c in range(NODES):
    _n = min(_c + 1, 5)
    GRAPH.append(dict(q=_c - 1, k=_c - _n, v=_c - _n + _n // 2,
                      eq=_lind + _n - 1, ek=_lind, ev=_lind + _n // 2))
    _lind += _n

V_CONVB, V_DTB, V_D, V_CONVW, V_ALOG = 0, 4, 8, 12, 28
V_NORM = V_ALOG + IC * NS
V_GBI, V_GBF = V_NORM + 1, V_NORM + 2
V_BE = V_GBF + 1
V_EW = V_BE + EDGES * HC
V_ACTW = V_EW + NODES * 3
NV = V_ACTW + NODES
C_ID, C_MEAN, C_SEL, C_LO, C_CAUSAL = 0, P, 2 * P, 2 * P + 2 * NS, 2 * P + 2 * NS + 1
NC_ = C_CAUSAL + P

PER = dict(
    x_loaded=32,
    out_stored=16,
    ln1_rows=1, xnT_ps=1, xnT_ready=1,
    inproj_ps=4, inproj_read=4,
    tanh_u=1, tanh_g=1,
    conv_done=1, u_ready=1,
    xproj_ps=1, xsq=1, meansq_ps=1, rms_rstd=1, xdn_ready=1,
    dt_ps=2, dt_read=1, sp_tail=1, dt_ready=1, dtu_ready=1, split_ready=1,
    bc_ps=16, bc_read=16,
    decay=UNITS, inflow=UNITS, state=UNITS, outflow=UNITS, ysum=UNITS,
    y_read=8, y_ready=4,
    outproj_ps=1, x1_ready=1, ln_var2=1, ln_rstd2=1, ln2_rows=1,
    ctxT_ps=1, ctxT_ready=1, qT_ps=1, qT_ready=1, qpad_clear=1, qpad_ready=1, vaug_ready=1,
    gate_ps=1, gate_read=1, gate_tail=1, gates_ready=1, gates_ps=1, gates_rows=1,
    dbc_ps=2, sT_ps=2, dT_ready=2, cT_ready=2, h_ps=2, h_read=2, em_ready=1,
    ln_var1=1, ln_rstd1=1, hvar=1, hrstd=1,
    x2_ready=1, ln_var3=1, ln_rstd3=1, ln3_rows=1, n0T_ps=1, n0T_ready=1,
    q_ps=NODES, k_ps=NODES, v_ps=NODES, qk_read=2 * NODES, qk_max_ready=NODES, qhead_ready=NODES, v_ready=NODES,
    smax_ps=NODES * STEPS, smax_read=NODES * STEPS, maxT_ps=NODES, maxT_ready=NODES,
    score_ps=NODES * STEPS, prob=NODES * STEPS, attn_ps=NODES * STEPS,
    den_inv=NODES, attn_ready=NODES, node_ps=NODES, node_ready=NODES,
    rows_ps=1, ln_var4=1, ln_rstd4=1, out_ready=1,
    vec_m=44, vec_f=7, act_m=9, act_f=7,
)
CREDIT = ("x2_ready", "out_ready", "out_stored", "outproj_ps")
PRE = ["stats_seen", "const_loaded", "consts_made", "prep_ps", "prep_read", "prep_vec", "prep_bias_ps", "prep_bias",
       "w_loaded", "w_used", "a_made", "setup_act", "prep_made"]


def build(nc, x, ctx_in, consts, vecs, rowvecs, w_in, w_x, w_dt, w_out, w_gate, w_edge, w_edgeT, w_node, out):
    with ExitStack() as es:
        def sb(name, shape, dt=F32):
            return es.enter_context(nc.sbuf_tensor(name, shape, dt))

        sig = {n: es.enter_context(nc.semaphore(n)) for n in [*PER, *PRE]}

        cst = sb("cst", [P, NC_])
        vec = sb("vec", [P, NV])
        rowv = sb("rowv", [P, 3, H])
        ident = cst[:, C_ID:C_ID + P]
        ident_bf = sb("ident_bf", [P, P], BF16)
        negid_bf = sb("negid_bf", [P, 16], BF16)
        negid = sb("negid", [P, XH])
        sel = sb("sel", [P, 2 * NS], F32R)
        causal = sb("causal", [P, P], BF16)
        ones = sb("ones", [P, L])
        win = sb("win", [P, HC, 2 * I])
        wx = sb("wx", [P, IC, P])
        wdt = sb("wdt", [R, I])
        wout = sb("wout", [P, IC, H])
        wgate = sb("wgate", [P, 3 * HC, 2, XH])
        a_neg = sb("a_neg", [P, IC * NS])
        convh = sb("convh", [P, 20])
        wq_f = [sb(f"wq_f{c}", [P, HC, H]) for c in range(NODES)]
        wk_f = [sb(f"wk_f{c}", [P, HC, H]) for c in range(NODES)]
        wv_f = [sb(f"wv_f{c}", [P, HC, H]) for c in range(NODES)]
        we_f = [sb(f"we_f{c}", [P, HC, H]) for c in range(NODES)]
        wo_f = [sb(f"wo_f{c}", [P, HC, H]) for c in range(NODES)]
        fb = sb("fb", [P, NODES, 8])

        xr = sb("xr", [P, GB, H])
        cr = sb("cr", [P, GB, H])
        rows = sb("rows", [P, GB, H])
        bn = sb("bn", [P, GB, 6])
        mv = sb("mv", [P, GB, 2])
        rstd = sb("rstd", [P, GB])
        xnT = sb("xnT", [P, HC, T])
        ctxT = sb("ctxT", [P, HC, T])
        hs_pad = sb("hs_pad", [P, IC, GB, L + 3])
        u = sb("u", [P, IC, T])
        th = sb("th", [P, IC, T])
        gate = sb("gate", [P, IC, T])
        dt = sb("dt", [P, IC, T])
        dtu = hs_pad[:, :, :, 1:L + 1]
        xsq, xrs = rows[:, 0, :], rows[:, 1, :]
        xdn = sb("xdn", [P, T])
        bhi = sb("bhi", [P, T], F32R)
        bcr = sb("bcr", [P, T], F32R)
        bs = sb("bs", [P, PAIRS, 2, T])
        cs = sb("cs", [P, PAIRS, 2, T])
        dec = [sb(f"dec{j}", [P, 2, GB, L]) for j in range(2)]
        inf = [sb(f"inf{j}", [P, 2, T]) for j in range(2)]
        hst = [sb(f"hst{j}", [P, 2, T]) for j in range(3)]
        prd = [sb(f"prd{j}", [P, 2, T]) for j in range(2)]
        qpad = th[:].rearrange("p c (x t) -> p (c x t)", x=GB).rearrange("p (c a b t) -> p c a b t", c=HC, a=2, b=GB)
        vaug = sb("vaug", [P, GB, XH, XP])
        gfa, gfm = (dt[0:XH, x, :] for x in range(2))
        grow, gcum, gmax, gtop = (u[0:XH, x, :] for x in range(4))
        rm = sb("rm", [P, 2, GB * XH])
        free = bs[:].rearrange("p q a n -> p (q a n)").rearrange("p (x n) -> p x n", x=4)
        dT, cT = (free[:, x].rearrange("p (a b t) -> p a b t", a=2, b=GB) for x in (0, 1))
        hn, hsq = (free[:, x].rearrange("p (n d) -> p n d", d=XD) for x in (2, 3))
        hrow = sb("hrow", [P, GB, XH, XP])
        em = sb("em", [P, GB * XH])
        den = sb("den", [P, GB * XH])
        hmu = sb("hmu", [P, GB * XH])
        hva = sb("hva", [P, GB * XH])

        node = [sb(f"node{j}", [P, HC, T]) for j in range(5)]
        SLOT = {-1: 0, 0: 1, 1: 2, 2: 3, 3: 4, 4: 2, 5: 4}
        res = sb("res", [P, GB, H])
        qT = sb("qT", [P, HC, T])
        kT = sb("kT", [P, HC, T])
        qhead = sb("qhead", [P, STEPS, HPC, L])
        qheadr = sb("qheadr", [P, STEPS, HPC, L], F32R)
        kTr = sb("kTr", [P, HC, T], F32R)
        vrow = sb("vrow", [P, GB, H])
        bias_t = sb("bias_t", [P, HC])
        mx = sb("mx", [P, GB * FH])
        mxT = sb("mxT", [P, P], BF16)
        pr = [sb(f"pr{j}", [P, HPC, L]) for j in range(2)]
        dinv = sb("dinv", [P, HC, T])
        aT = sb("aT", [P, HC, T])
        fbn = sb("fbn", [P, GB, 6])
        fmv = sb("fmv", [P, GB, 2])
        frstd = sb("frstd", [P, GB])
        orow = sb("orow", [P, GB, H])

        ps = [es.enter_context(nc.psum_tensor(f"ps{j}", [P, 512], F32)) for j in range(8)]
        MA, MB, MY, FP, FQ, FX, FY, FV = ps
        stage = {n: t[:, :, :].rearrange("p a b -> p (a b)").rearrange("p (a b) -> p a b", a=HC)
                 for n, t in (("eqT", node[0]), ("ekT", node[1]), ("evT", node[2]), ("e", node[3]),
                              ("q", node[4]), ("k", qT), ("v", kT), ("o", aT))}

        block = es.enter_context(nc.Block())

        def after(eng, name, i, n):
            value = i * PER[name] + n + (name in CREDIT)
            if not (isinstance(value, int) and value <= 0):
                eng.wait_ge(sig[name], value)

        class Chain:

            def __init__(self, eng, name):
                self.eng, self.name, self.i, self.n = eng, name, 0, 0

            def start(self, i):
                self.i, self.n = i, 0

            def mark(self, ins):
                ins.then_inc(sig[self.name], 1)
                self.n += 1
                return self.n

            def wait(self, n):
                after(self.eng, self.name, self.i, n)

            def link(self, ins):
                self.wait(self.mark(ins))

            def end(self):
                assert self.n == PER[self.name], (self.name, self.n)

        @block.sync
        def _(sp):
            def load(dst, src):
                sp.dma_start(dst, src).then_inc(sig["const_loaded"], 16)

            for name in CREDIT:
                sp.sem_inc(sig[name], 1)
            load(cst[:], consts)
            load(vec[:], vecs)
            load(rowv[:], rowvecs.partition_broadcast(P))
            load(win[:], w_in)
            load(wx[:], w_x)
            load(wdt[:], w_dt)
            load(wout[:], w_out)
            load(wgate[:], w_gate)
            for c, g in enumerate(GRAPH):
                if c >= 1:
                    sp.wait_ge(sig["w_used"], c)
                for n, src in (("eqT", w_edgeT[g["eq"]]), ("ekT", w_edgeT[g["ek"]]), ("evT", w_edgeT[g["ev"]]),
                               ("e", w_edge[g["eq"]]), ("q", w_node[0, c]), ("k", w_node[1, c]),
                               ("v", w_node[2, c]), ("o", w_node[3, c])):
                    sp.dma_start(stage[n], src).then_inc(sig["w_loaded"], 16)

            with sp.Fori(0, NG) as i:
                after(sp, "x2_ready", i, 0)
                sp.dma_start(xr[:], x[bass.ds(i * GB, GB)].rearrange("b t h -> t b h")).then_inc(sig["x_loaded"], 16)
                sp.dma_start(cr[:], ctx_in[bass.ds(i * GB, GB)].rearrange("b t h -> t b h")).then_inc(sig["x_loaded"], 16)
                after(sp, "out_ready", i, 1)
                sp.dma_start(out[bass.ds(i * GB, GB)].rearrange("b t h -> t b h"), orow[:]).then_inc(sig["out_stored"], 16)
            sp.wait_ge(sig["out_stored"], 16 * NG + 1)

        @block.tensor
        def _(pe):
            mm, tr = nc.tensor.matmul, nc.tensor.transpose

            def prep(c):
                pe.wait_ge(sig["w_loaded"], 16 * 8 * (c + 1))
                for j, (e, w) in enumerate((("eqT", "q"), ("ekT", "k"), ("evT", "v"))):
                    bank = (FP, FQ, FX)[j]
                    if c >= 1:
                        pe.wait_ge(sig["prep_read"], 3 * (c - 1) + j + 1)
                    for a in range(HC):
                        for k in range(HC):
                            last = mm(bank[:, a * H:(a + 1) * H], stage[e][:, k, a * P:(a + 1) * P],
                                      stage[w][:, k, :], start=(k == 0), stop=(k == HC - 1))
                    last.then_inc(sig["prep_ps"], 1)
                if c >= 1:
                    pe.wait_ge(sig["prep_bias"], 2 * c)
                for j, (w, e) in enumerate((("q", "eq"), ("k", "ek"), ("v", "ev"))):
                    for a in range(HC):
                        for k in range(HC):
                            last = mm(FY[:, 2 * j + a:2 * j + a + 1], stage[w][:, k, a * P:(a + 1) * P],
                                      vec[:, V_BE + GRAPH[c][e] * HC + k:V_BE + GRAPH[c][e] * HC + k + 1],
                                      start=(k == 0), stop=(k == HC - 1))
                last.then_inc(sig["prep_bias_ps"], 1)
                pe.wait_ge(sig["prep_bias"], 2 * c + 1)
                for a in range(HC):
                    for k in range(HC):
                        last = mm(FY[:, 8 + a:9 + a], stage["o"][:, k, a * P:(a + 1) * P], fb[:, c, 4 + k:5 + k],
                                  start=(k == 0), stop=(k == HC - 1))
                last.then_inc(sig["prep_bias_ps"], 1)

            def rows_to_T(bank, src):
                for a in range(HC):
                    for b in range(GB):
                        last = tr(bank[:, a * T + b * L:a * T + (b + 1) * L], src[:, b, a * P:(a + 1) * P], ident)
                return last

            def mamba_in(i):
                after(pe, "ln1_rows", i, 1)
                rows_to_T(MA, rows).then_inc(sig["xnT_ps"], 1)
                after(pe, "xnT_ready", i, 1)
                for j in range(4):
                    bank = (MB, MA)[j % 2]
                    if j >= 2:
                        after(pe, "inproj_read", i, j - 1)
                    for a in range(2):
                        m = 2 * j + a
                        for k in range(HC):
                            last = mm(bank[:, a * T:(a + 1) * T], win[:, k, m * P:(m + 1) * P], xnT[:, k, :],
                                      start=(k == 0), stop=(k == HC - 1))
                    last.then_inc(sig["inproj_ps"], 1)
                after(pe, "inproj_read", i, 4)
                after(pe, "u_ready", i, 1)
                for k in range(IC):
                    last = mm(MA[:, 0:T], wx[:, k, :], u[:, k, :], start=(k == 0), stop=(k == IC - 1))
                last.then_inc(sig["xproj_ps"], 1)
                after(pe, "xsq", i, 1)
                mm(MB[:, 0:T], cst[:, C_MEAN:C_MEAN + P], xsq, start=True, stop=True).then_inc(sig["meansq_ps"], 1)
                after(pe, "xdn_ready", i, 1)
                for j in range(2):
                    bank = (MA, MB)[j]
                    for a in range(2):
                        m = 2 * j + a
                        last = mm(bank[:, a * T:(a + 1) * T], wdt[:, m * P:(m + 1) * P], xdn[0:R, :],
                                  start=True, stop=True)
                    last.then_inc(sig["dt_ps"], 1)

            def spread(i, n):
                if n == 0:
                    after(pe, "split_ready", i, 1)
                    after(pe, "dt_read", i, 1)
                bank = MA
                for j in range(2):
                    if 2 * n + j >= 1:
                        after(pe, "bc_read", i, 2 * n + j)
                    for a in range(2):
                        s = 2 * n + a
                        last = mm(bank[:, a * T:(a + 1) * T],
                                  sel[:, j * NS + s:j * NS + s + 1].broadcast_to([P, P]), bcr[:], start=True, stop=True)
                    last.then_inc(sig["bc_ps"], 1)

            def sum_states(i, k):
                m, q = k // PAIRS, k % PAIRS
                after(pe, "outflow", i, k + 1)
                if q == 0 and m >= 2:
                    after(pe, "y_read", i, m - 1)
                for a in range(2):
                    last = mm((MY, MB)[m % 2][:, 0:T], ident, prd[k % 2][:, a, :],
                              start=(q == 0 and a == 0), stop=(q == PAIRS - 1 and a == 1))
                last.then_inc(sig["ysum"], 1)

            def units(i, k0, k1):
                for k in range(k0, k1):
                    if k == 0:
                        for n in range(PAIRS):
                            spread(i, n)
                    if k >= UNITS // 2 - PAIRS + 2 and k < UNITS // 2 + 2:
                        spread(i, k - (UNITS // 2 - PAIRS + 2) + PAIRS)
                    sum_states(i, k)

            def mlstm(i):
                after(pe, "bc_read", i, 16)
                after(pe, "y_ready", i, 4)
                for b in range(GB):
                    for k in range(IC):
                        last = mm(MA[:, b * H:(b + 1) * H], gate[:, k, b * L:(b + 1) * L], wout[:, k, :],
                                  start=(k == 0), stop=(k == IC - 1))
                last.then_inc(sig["outproj_ps"], 1)
                rows_to_T(MB, cr).then_inc(sig["ctxT_ps"], 1)
                after(pe, "ln2_rows", i, 1)
                rows_to_T(MA, rows).then_inc(sig["qT_ps"], 1)
                after(pe, "ctxT_ready", i, 1)
                after(pe, "qT_ready", i, 1)
                for gsel in range(2):
                    for k in range(3 * HC):
                        src = xnT if k < HC else ctxT
                        last = mm(MB[0:XH, gsel * T:(gsel + 1) * T], wgate[:, k, gsel, :], src[:, k % HC, :],
                                  start=(k == 0), stop=(k == 3 * HC - 1))
                last.then_inc(sig["gate_ps"], 1)
                after(pe, "gates_ready", i, 1)
                after(pe, "qpad_ready", i, 1)
                for hp in range(2):
                    if hp:
                        after(pe, "dT_ready", i, 1)
                    for a in range(2):
                        h = 2 * hp + a
                        mm(MA[:, a * T:(a + 1) * T], negid[0:XH, h:h + 1].broadcast_to([XH, P]), gmax,
                           start=True, stop=False)
                        last = mm(MA[:, a * T:(a + 1) * T], ident_bf[:],
                                  causal[:].unsqueeze(1).broadcast_to([P, GB, L]), start=False, stop=True)
                    last.then_inc(sig["dbc_ps"], 1)
                    if hp == 0:
                        for j, src in enumerate((grow, gtop)):
                            for b in range(GB):
                                last = tr(MY[:, (j * GB + b) * XH:(j * GB + b + 1) * XH], src[:, b * L:(b + 1) * L],
                                          cst[0:XH, C_ID:C_ID + XH])
                        last.then_inc(sig["gates_ps"], 1)
                    if hp:
                        after(pe, "cT_ready", i, 1)
                    for b in range(GB):
                        last = mm(MB[:].rearrange("p (a b t) -> p a b t", a=2, b=GB)[:, :, b, :],
                                  ctxT[:, hp, b * L:(b + 1) * L], qpad[:, hp, :, b, :], start=True, stop=True)
                    last.then_inc(sig["sT_ps"], 1)
                    after(pe, "cT_ready", i, hp + 1)
                    if hp == 0:
                        after(pe, "vaug_ready", i, 1)
                        after(pe, "gates_rows", i, 1)
                    else:
                        after(pe, "h_read", i, 1)
                    for b in range(GB):
                        for a in range(2):
                            j = b * 2 + a
                            last = mm(MY[:, j * XP:(j + 1) * XP], cT[:, a, b, :], vaug[:, b, 2 * hp + a, :],
                                      start=True, stop=True)
                    last.then_inc(sig["h_ps"], 1)

            def mlstm_out(i):
                after(pe, "ln3_rows", i, 1)
                rows_to_T(MA, rows).then_inc(sig["n0T_ps"], 1)

            def node_proj(i, c):
                g = GRAPH[c]
                if c == 0:
                    after(pe, "n0T_ready", i, 1)
                    after(pe, "out_ready", i, 0)
                else:
                    after(pe, "node_ready", i, c)
                for bank, w, src, s in ((FP, wq_f, g["q"], "q_ps"), (FQ, wk_f, g["k"], "k_ps")):
                    for a in range(HC):
                        for k in range(HC):
                            last = mm(bank[:, a * T:(a + 1) * T], w[c][:, k, a * P:(a + 1) * P],
                                      node[SLOT[src]][:, k, :], start=(k == 0), stop=(k == HC - 1))
                    last.then_inc(sig[s], 1)
                for b in range(GB):
                    for k in range(HC):
                        last = mm(FV[:, b * H:(b + 1) * H], node[SLOT[g["v"]]][:, k, b * L:(b + 1) * L],
                                  wv_f[c][:, k, :], start=(k == 0), stop=(k == HC - 1))
                last.then_inc(sig["v_ps"], 1)

            def node_max(i, c):
                after(pe, "qk_max_ready", i, c + 1)
                for s in range(STEPS):
                    b, m = s // HC, s % HC
                    bank = (FX, FY)[s % 2]
                    if s >= 2:
                        after(pe, "smax_read", i, c * STEPS + s - 1)
                    elif c >= 1:
                        after(pe, "prob", i, c * STEPS)
                    for h in range(HPC):
                        last = mm(bank[:, h * L:(h + 1) * L], qheadr[:, s, h, :], kTr[:, m, b * L:(b + 1) * L],
                                  start=True, stop=True)
                    last.then_inc(sig["smax_ps"], 1)
                after(pe, "smax_read", i, (c + 1) * STEPS)
                after(pe, "v_ready", i, c + 1)
                tr(FV[0:GB * FH, 0:P], mx[:], ident).then_inc(sig["maxT_ps"], 1)

            def node_scores(i, c, s):
                b, m = s // HC, s % HC
                bank = (FX, FY)[s % 2]
                if s == 0:
                    after(pe, "maxT_ready", i, c + 1)
                    after(pe, "qhead_ready", i, c + 1)
                if s >= 2:
                    after(pe, "prob", i, c * STEPS + s - 1)
                mm(bank[:], kT[:, m, b * L:(b + 1) * L], qhead[:, s].rearrange("p h t -> p (h t)"),
                   start=True, stop=False, skip_group_check=True)
                for h in range(HPC):
                    j = s * HPC + h
                    last = mm(bank[:, h * L:(h + 1) * L], negid_bf[:, j:j + 1].broadcast_to([P, P]),
                              mxT[:], start=False, stop=(h == HPC - 1), skip_group_check=True)
                last.then_inc(sig["score_ps"], 1)

            def node_attend(i, c, s):
                b, m = s // HC, s % HC
                after(pe, "prob", i, c * STEPS + s + 1)
                for h in range(HPC):
                    r0 = FD * h
                    at = (m * GB + b) * L
                    mm(FP[r0:r0 + FD, at:at + L], vrow[:, b, m * P + r0:m * P + r0 + FD], pr[s % 2][:, h, :],
                       start=True, stop=True, tile_position=(0, r0))
                    last = mm(FQ[r0:r0 + FD, at:at + L], ones[:, 0:FD], pr[s % 2][:, h, :],
                              start=True, stop=True, tile_position=(0, r0))
                last.then_inc(sig["attn_ps"], 1)

            def node_out(i, c):
                after(pe, "attn_ready", i, c + 1)
                src = node[SLOT[GRAPH[c]["q"]]]
                for a in range(HC):
                    for k in range(HC):
                        mm(FV[:, a * T:(a + 1) * T], we_f[c][:, k, a * P:(a + 1) * P], src[:, k, :],
                           start=(k == 0), stop=False)
                    for k in range(HC):
                        last = mm(FV[:, a * T:(a + 1) * T], wo_f[c][:, k, a * P:(a + 1) * P], aT[:, k, :],
                                  start=False, stop=(k == HC - 1))
                last.then_inc(sig["node_ps"], 1)

            def ffn_out(i):
                after(pe, "node_ready", i, NODES)
                for b in range(GB):
                    for a in range(HC):
                        last = tr(FP[:, b * H + a * P:b * H + (a + 1) * P],
                                  node[SLOT[NODES - 1]][:, a, b * L:(b + 1) * L], ident)
                last.then_inc(sig["rows_ps"], 1)

            pe.wait_ge(sig["const_loaded"], 16 * 8)
            for c in range(NODES):
                prep(c)
            pe.wait_ge(sig["prep_made"], 1)
            pe.wait_ge(sig["setup_act"], 1)
            with pe.Fori(0, NG) as i:
                mamba_in(i)
                units(i, 0, UNITS)
                mlstm(i)
                mlstm_out(i)
                for c in range(NODES):
                    node_proj(i, c)
                    node_max(i, c)
                    node_scores(i, c, 0)
                    node_scores(i, c, 1)
                    for s in range(STEPS):
                        node_attend(i, c, s)
                        if s + 2 < STEPS:
                            node_scores(i, c, s + 2)
                    node_out(i, c)
                ffn_out(i)

        @block.scalar
        def _(act):
            fn = nc.scalar.activation

            m_chain, f_chain = Chain(act, "act_m"), Chain(act, "act_f")

            def rstd_of(chain, var_sig, done_sig, i, dst):
                after(act, var_sig, i, 1)
                chain.link(fn(dst, dst, ACT.Ln))
                fn(dst, dst, ACT.Exp, scale=-0.5).then_inc(sig[done_sig], 1)

            def prep(c):
                for j, (w, e) in enumerate(((wq_f, 0), (wk_f, 1), (wv_f, 2))):
                    act.wait_ge(sig["prep_ps"], 3 * c + j + 1)
                    bank = (FP, FQ, FX)[j]
                    fn(w[c][:].rearrange("p a b -> p (a b)"), bank[:], ACT.Copy,
                       scale=vec[:, V_EW + 3 * c + e:V_EW + 3 * c + e + 1]).then_inc(sig["prep_read"], 1)

            def mamba_in(i):
                m_chain.start(i)
                rstd_of(m_chain, "ln_var1", "ln_rstd1", i, rstd[:])
                after(act, "xnT_ps", i, 1)
                fn(xnT[:].rearrange("p a b -> p (a b)"), MA[:], ACT.Copy).then_inc(sig["xnT_ready"], 1)
                for j in range(2):
                    after(act, "inproj_ps", i, j + 1)
                    bank = (MB, MA)[j % 2]
                    for a in range(2):
                        last = fn(hs_pad[:, 2 * j + a, :, 1:L + 1],
                                  bank[:, a * T:(a + 1) * T].rearrange("p (b t) -> p b t", b=GB), ACT.Copy)
                    last.then_inc(sig["inproj_read"], 1)
                for j in range(2, 4):
                    after(act, "inproj_ps", i, j + 1)
                    bank = (MB, MA)[j % 2]
                    if j == 2:
                        after(act, "outproj_ps", i, 0)
                    fn(gate[:, 2 * j - 4:2 * j - 2, :].rearrange("p a b -> p (a b)"), bank[:], ACT.Copy,
                       scale=0.5).then_inc(sig["inproj_read"], 1)
                after(act, "inproj_read", i, 4)
                fn(dt[:], gate[:], ACT.Tanh).then_inc(sig["tanh_g"], 1)
                after(act, "conv_done", i, 1)
                fn(th[:], u[:], ACT.Tanh).then_inc(sig["tanh_u"], 1)
                act.preload_act_table_set("natural_log_exp_and_others")
                after(act, "xproj_ps", i, 1)
                fn(xsq, MA[:, 0:T], ACT.Square).then_inc(sig["xsq"], 1)
                after(act, "meansq_ps", i, 1)
                m_chain.link(fn(xrs, MB[:, 0:T], ACT.Ln, bias=RMS_EPS))
                fn(xrs, xrs, ACT.Exp, scale=-0.5).then_inc(sig["rms_rstd"], 1)
                for c in range(IC):
                    if c % 2 == 0:
                        after(act, "dt_ps", i, c // 2 + 1)
                    last = fn(dt[:, c, :], (MA, MB)[c // 2][:, (c % 2) * T:(c % 2 + 1) * T], ACT.Identity,
                              bias=vec[:, V_DTB + c:V_DTB + c + 1])
                last.then_inc(sig["dt_read"], 1)
                after(act, "dt_read", i, 1)
                m_chain.link(fn(th[:], dt[:], ACT.Abs))
                m_chain.link(fn(th[:], th[:], ACT.Exp, scale=-1.0))
                fn(th[:], th[:], ACT.Ln, bias=1.0).then_inc(sig["sp_tail"], 1)

            def copies(i, n):
                q = n % PAIRS
                for j, dst in enumerate((bs, cs)):
                    after(act, "bc_ps", i, 2 * n + j + 1)
                    if n >= PAIRS:
                        after(act, ("inflow", "outflow")[j], i, UNITS // 2 - PAIRS + q + 1)
                    fn(dst[:, q].rearrange("p a b -> p (a b)"), MA[:], ACT.Copy).then_inc(sig["bc_read"], 1)

            def units(i, k0, k1):
                for k in range(k0, k1):
                    hf, c, q = k // (UNITS // 2), k // PAIRS % IC, k % PAIRS
                    if k == 0:
                        after(act, "dt_ready", i, 1)
                        for n in range(PAIRS):
                            copies(i, n)
                    if k >= 2:
                        after(act, "state", i, k - 1)
                    for a in range(2):
                        s = hf * (NS // 2) + 2 * q + a
                        last = fn(dec[k % 2][:, a, :, 1:L],
                                  dt[:, c, :].rearrange("p (b t) -> p b t", b=GB)[:, :, 1:L], ACT.Exp,
                                  scale=a_neg[:, c * NS + s:c * NS + s + 1])
                    last.then_inc(sig["decay"], 1)
                    if k >= UNITS // 2 - PAIRS + 2 and k < UNITS // 2 + 2:
                        copies(i, k - (UNITS // 2 - PAIRS + 2) + PAIRS)

            def mlstm(i):
                rstd_of(m_chain, "ln_var2", "ln_rstd2", i, rstd[:])
                after(act, "ctxT_ps", i, 1)
                fn(ctxT[:].rearrange("p a b -> p (a b)"), MB[:], ACT.Copy).then_inc(sig["ctxT_ready"], 1)
                after(act, "qT_ps", i, 1)
                fn(xnT[:].rearrange("p a b -> p (a b)"), MA[:], ACT.Copy).then_inc(sig["qT_ready"], 1)
                after(act, "qpad_clear", i, 1)
                for a in range(2):
                    rs = slice(XD * a, XD * (a + 1))
                    last = fn(qpad[rs, :, a, :, :].rearrange("p c b t -> p c (b t)"),
                              MA[rs, :].rearrange("p (c n) -> p c n", c=HC), ACT.Copy)
                last.then_inc(sig["qpad_ready"], 1)
                after(act, "gate_ps", i, 1)
                fn(grow, MB[0:XH, 0:T], ACT.Identity, bias=vec[0:XH, V_GBI:V_GBI + 1])
                fn(gfm, MB[0:XH, T:2 * T], ACT.Identity, bias=vec[0:XH, V_GBF:V_GBF + 1]).then_inc(sig["gate_read"], 1)
                after(act, "gate_read", i, 1)
                m_chain.link(fn(gfa, gfm, ACT.Abs))
                m_chain.link(fn(gfa, gfa, ACT.Exp, scale=-1.0))
                fn(gfa, gfa, ACT.Ln, bias=1.0).then_inc(sig["gate_tail"], 1)
                after(act, "gates_ps", i, 1)
                fn(rm[:].rearrange("p a b -> p (a b)"), MY[:, 0:2 * GB * XH], ACT.Copy).then_inc(sig["gates_rows"], 1)
                after(act, "gates_rows", i, 1)
                fn(em[:], rm[:, 1, :], ACT.Exp, scale=-1.0).then_inc(sig["em_ready"], 1)
                for hp in range(2):
                    after(act, "dbc_ps", i, hp + 1)
                    if hp:
                        after(act, "cT_ready", i, 1)
                    for a in range(2):
                        for b in range(GB):
                            h = 2 * hp + a
                            last = fn(dT[:, a, b, :], MA[:, a * T + b * L:a * T + (b + 1) * L], ACT.Exp,
                                      bias=rm[:, 0, b * XH + h:b * XH + h + 1])
                    last.then_inc(sig["dT_ready"], 1)
                rstd_of(m_chain, "hvar", "hrstd", i, hva[:])

            def mlstm_out(i):
                rstd_of(m_chain, "ln_var3", "ln_rstd3", i, rstd[:])
                after(act, "n0T_ps", i, 1)
                fn(node[0][:].rearrange("p a b -> p (a b)"), MA[:], ACT.Copy).then_inc(sig["n0T_ready"], 1)
                m_chain.end()

            def node_proj(i, c):
                after(act, "q_ps", i, c + 1)
                for a in range(HC):
                    last = fn(qT[:, a, :], FP[:, a * T:(a + 1) * T], ACT.Identity, bias=fb[:, c, a:a + 1])
                last.then_inc(sig["qk_read"], 1)
                after(act, "k_ps", i, c + 1)
                for a in range(HC):
                    last = fn(kT[:, a, :], FQ[:, a * T:(a + 1) * T], ACT.Identity, bias=fb[:, c, 2 + a:3 + a])
                last.then_inc(sig["qk_read"], 1)
                after(act, "v_ps", i, c + 1)
                fn(vrow[:].rearrange("p a b -> p (a b)"), FV[:], ACT.Copy).then_inc(sig["v_ready"], 1)

            def node_max(i, c):
                after(act, "maxT_ps", i, c + 1)
                fn(mxT[0:GB * FH, :], FV[0:GB * FH, 0:P], ACT.Copy).then_inc(sig["maxT_ready"], 1)

            def node_prob(i, c, s):
                after(act, "score_ps", i, c * STEPS + s + 1)
                if s >= 2:
                    after(act, "attn_ps", i, c * STEPS + s - 1)
                fn(pr[s % 2][:].rearrange("p a b -> p (a b)"), (FX, FY)[s % 2][:], ACT.Exp,
                   scale=FD ** -0.5).then_inc(sig["prob"], 1)

            def node_den(i, c):
                after(act, "attn_ps", i, (c + 1) * STEPS)
                f_chain.link(fn(dinv[:].rearrange("p a b -> p (a b)"), FQ[:], ACT.Ln))
                fn(dinv[:], dinv[:], ACT.Exp, scale=-1.0).then_inc(sig["den_inv"], 1)

            def node_out(i, c):
                after(act, "node_ps", i, c + 1)
                for a in range(HC):
                    last = fn(node[SLOT[c]][:, a, :], FV[:, a * T:(a + 1) * T], ACT.Identity,
                              bias=fb[:, c, 6 + a:7 + a])
                last.then_inc(sig["node_ready"], 1)

            act.wait_ge(sig["const_loaded"], 16 * 8)
            act.preload_act_table_set("natural_log_exp_and_others")
            fn(a_neg[:], vec[:, V_ALOG:V_ALOG + IC * NS], ACT.Exp).then_inc(sig["setup_act"], 1)
            for c in range(NODES):
                prep(c)
            act.wait_ge(sig["prep_made"], 1)
            with act.Fori(0, NG) as i:
                act.preload_act_table_set("natural_log_exp_and_others")
                mamba_in(i)
                units(i, 0, UNITS)
                mlstm(i)
                mlstm_out(i)
                f_chain.start(i)
                for c in range(NODES):
                    node_proj(i, c)
                    node_max(i, c)
                    for s in range(STEPS):
                        node_prob(i, c, s)
                    node_den(i, c)
                    node_out(i, c)
                rstd_of(f_chain, "ln_var4", "ln_rstd4", i, frstd[:])
                f_chain.end()

        @block.vector
        def _(dve):
            v = nc.vector
            m_chain, f_chain = Chain(dve, "vec_m"), Chain(dve, "vec_f")

            def col(n):
                return vec[:, n:n + 1]

            def setup():
                dve.wait_ge(sig["const_loaded"], 16 * 8)
                v.tensor_copy(ident_bf[:], ident)
                v.tensor_scalar(negid_bf[:], cst[:, C_ID:C_ID + GB * FH], -1.0, None, ALU.mult)
                v.tensor_scalar(negid[:], cst[:, C_ID:C_ID + XH], -1.0, None, ALU.mult)
                v.tensor_copy(sel[:], cst[:, C_SEL:C_SEL + 2 * NS])
                v.tensor_copy(causal[:], cst[:, C_CAUSAL:C_CAUSAL + P])
                v.tensor_scalar(convh[:, 0:4], vec[:, V_CONVB:V_CONVB + 4], 0.5, None, ALU.mult)
                v.tensor_scalar(convh[:, 4:20], vec[:, V_CONVW:V_CONVW + 16], 0.5, None, ALU.mult)
                dve.wait_ge(sig["setup_act"], 1)
                v.tensor_scalar(a_neg[:], a_neg[:], -1.0, None, ALU.mult)

            def prep(c):
                g = GRAPH[c]
                ew0, ew1, ew2 = (col(V_EW + 3 * c + j) for j in range(3))
                dve.wait_ge(sig["w_loaded"], 16 * 8 * (c + 1))
                v.tensor_scalar(we_f[c][:], stage["e"], ew0, None, ALU.mult)
                v.tensor_scalar(wo_f[c][:], stage["o"], col(V_ACTW + c), None, ALU.mult)
                dve.wait_ge(sig["prep_bias_ps"], 2 * c + 1)
                for j, e in enumerate((ew0, ew1, ew2)):
                    last = v.tensor_scalar(fb[:, c, 2 * j:2 * j + 2], FY[:, 2 * j:2 * j + 2], e, None, ALU.mult)
                last.then_inc(sig["prep_bias"], 1)
                v.tensor_scalar(bias_t[:], vec[:, V_BE + g["eq"] * HC:V_BE + (g["eq"] + 1) * HC], ew0, None,
                                ALU.mult).then_inc(sig["prep_vec"], 1)
                dve.wait_ge(sig["prep_bias_ps"], 2 * c + 2)
                dve.wait_ge(sig["prep_vec"], c + 1)
                v.scalar_tensor_tensor(fb[:, c, 6:8], FY[:, 8:10], col(V_ACTW + c), bias_t[:], ALU.mult,
                                       ALU.add).then_inc(sig["prep_bias"], 1)
                dve.wait_ge(sig["prep_bias"], 2 * c + 2)
                dve.sem_inc(sig["w_used"], 1)

            def layer_norm(i, chain, n, src, mean_var, stats, inv, eps, dst):
                for b in range(GB):
                    m = chain.mark(v.bn_stats(stats[:, b, :], src(b)))
                chain.wait(m)
                dve.sem_inc(sig["stats_seen"], 1)
                for b in range(GB):
                    m = chain.mark(v.bn_aggr(mean_var[:, b, :], stats[:, b, :]))
                chain.wait(m)
                v.tensor_scalar(inv[:], mean_var[:, :, 1], eps, None, ALU.add).then_inc(sig[f"ln_var{n}"], 1)
                after(dve, f"ln_rstd{n}", i, 1)
                for b in range(GB):
                    last = v.tensor_scalar(dst[:, b, :], src(b), mean_var[:, b, 0:1], inv[:, b:b + 1],
                                           ALU.subtract, ALU.mult)
                return last

            def mamba_in(i):
                m_chain.start(i)
                after(dve, "x_loaded", i, 32)
                layer_norm(i, m_chain, 1, lambda b: xr[:, b, :], mv, bn, rstd, LN_EPS, rows).then_inc(sig["ln1_rows"], 1)
                after(dve, "inproj_read", i, 2)
                marks = [m_chain.mark(v.tensor_scalar(u[:, c, :].rearrange("p (b t) -> p b t", b=GB),
                                                      hs_pad[:, c, :, 0:L], convh[:, 4 + c * 4:5 + c * 4],
                                                      convh[:, c:c + 1], ALU.mult, ALU.add)) for c in range(IC)]
                for k in range(1, 4):
                    for c in range(IC):
                        m_chain.wait(marks[c])
                        uc = u[:, c, :].rearrange("p (b t) -> p b t", b=GB)
                        ins = v.scalar_tensor_tensor(uc, hs_pad[:, c, :, k:k + L],
                                                     convh[:, 4 + c * 4 + k:5 + c * 4 + k], uc, ALU.mult, ALU.add)
                        if k < 3:
                            marks[c] = m_chain.mark(ins)
                ins.then_inc(sig["conv_done"], 1)
                after(dve, "tanh_g", i, 1)
                m_chain.mark(v.scalar_tensor_tensor(gate[:], dt[:], 1.0, gate[:], ALU.add, ALU.mult))
                after(dve, "tanh_u", i, 1)
                v.scalar_tensor_tensor(u[:], th[:], 1.0, u[:], ALU.add, ALU.mult).then_inc(sig["u_ready"], 1)
                after(dve, "rms_rstd", i, 1)
                v.scalar_tensor_tensor(xdn[:], MA[:, 0:T], col(V_NORM), xrs, ALU.mult,
                                       ALU.mult).then_inc(sig["xdn_ready"], 1)
                after(dve, "xdn_ready", i, 1)
                m_chain.link(v.tensor_copy(bhi[:], xdn[:]))
                v.scalar_tensor_tensor(bcr[:], bhi[:].bitcast(F32), cst[:, C_LO:C_LO + 1], xdn[:],
                                       ALU.mult, ALU.add).then_inc(sig["split_ready"], 1)
                after(dve, "sp_tail", i, 1)
                v.scalar_tensor_tensor(dt[:], dt[:], 0.0, th[:], ALU.max, ALU.add).then_inc(sig["dt_ready"], 1)
                after(dve, "dt_ready", i, 1)
                v.tensor_tensor(dtu, dt[:].rearrange("p c (b t) -> p c b t", b=GB),
                                u[:].rearrange("p c (b t) -> p c b t", b=GB), ALU.mult).then_inc(sig["dtu_ready"], 1)

            def scan(i, k):
                after(dve, "decay", i, k + 1)
                after(dve, "inflow", i, k + 1)
                if k >= 3:
                    after(dve, "outflow", i, k - 2)
                v.tensor_tensor_scan(hst[k % 3][:].rearrange("p a b -> p (a b)"),
                                     dec[k % 2][:].rearrange("p a b t -> p (a b t)"),
                                     inf[k % 2][:].rearrange("p a b -> p (a b)"), 0.0, ALU.mult,
                                     ALU.add).then_inc(sig["state"], 1)

            def weigh(i, k):
                q = k % PAIRS
                after(dve, "state", i, k + 1)
                if k >= 2:
                    after(dve, "ysum", i, k - 1)
                after(dve, "bc_read", i, 2 * (k // (UNITS // 2) * PAIRS + q) + 2)
                v.tensor_tensor(prd[k % 2][:], hst[k % 3][:], cs[:, q], ALU.mult).then_inc(sig["outflow"], 1)

            def gather(i, m):
                hf, c = m // IC, m % IC
                after(dve, "ysum", i, (m + 1) * PAIRS)
                src = (MY, MB)[m % 2][:, 0:T]
                if hf == 0:
                    v.scalar_tensor_tensor(u[:, c, :], u[:, c, :], col(V_D + c), src, ALU.mult,
                                           ALU.add).then_inc(sig["y_read"], 1)
                else:
                    v.tensor_tensor(u[:, c, :], u[:, c, :], src, ALU.add).then_inc(sig["y_read"], 1)
                    after(dve, "y_read", i, m + 1)
                    v.tensor_tensor(gate[:, c, :], gate[:, c, :], u[:, c, :], ALU.mult).then_inc(sig["y_ready"], 1)

            def units(i, k0, k1):
                for k in range(k0, k1):
                    scan(i, k)
                    if k >= 1:
                        weigh(i, k - 1)
                    if k % PAIRS == 2 and k > PAIRS:
                        gather(i, k // PAIRS - 1)
                if k1 == UNITS:
                    weigh(i, UNITS - 1)
                    gather(i, 2 * IC - 1)

            def mlstm(i):
                after(dve, "outproj_ps", i, 1)
                v.tensor_tensor(xr[:].rearrange("p a b -> p (a b)"), xr[:].rearrange("p a b -> p (a b)"), MA[:],
                                ALU.add).then_inc(sig["x1_ready"], 1)
                after(dve, "x1_ready", i, 1)
                layer_norm(i, m_chain, 2, lambda b: xr[:, b, :], mv, bn, rstd, LN_EPS, rows).then_inc(sig["ln2_rows"], 1)
                after(dve, "gate_tail", i, 1)
                m_chain.link(v.scalar_tensor_tensor(gfm, gfm, 0.0, gfa, ALU.min, ALU.subtract))
                for b in range(GB):
                    m = m_chain.mark(v.tensor_tensor_scan(gcum[:, b * L:(b + 1) * L], ones[0:XH, 0:L],
                                                          gfm[:, b * L:(b + 1) * L], 0.0, ALU.mult, ALU.add))
                m_chain.wait(m)
                m_chain.link(v.tensor_tensor(grow, grow, gcum, ALU.subtract))
                for b in range(GB):
                    m = m_chain.mark(v.tensor_tensor_scan(gmax[:, b * L:(b + 1) * L], grow[:, b * L:(b + 1) * L],
                                                          grow[:, b * L:(b + 1) * L], -BIG, ALU.max, ALU.max))
                m_chain.wait(m)
                v.tensor_tensor(gtop, gcum, gmax, ALU.add).then_inc(sig["gates_ready"], 1)
                for hp in range(2):
                    after(dve, "sT_ps", i, hp + 1)
                    after(dve, "dT_ready", i, hp + 1)
                    if hp:
                        after(dve, "h_ps", i, 1)
                    v.scalar_tensor_tensor(cT.rearrange("p a b t -> p (a b t)"), MB[:], XD ** -0.5,
                                           dT.rearrange("p a b t -> p (a b t)"), ALU.mult,
                                           ALU.mult).then_inc(sig["cT_ready"], 1)
                    after(dve, "h_ps", i, hp + 1)
                    v.tensor_copy(hrow[:, :, 2 * hp:2 * hp + 2, :],
                                  MY[:, 0:2 * GB * XP].rearrange("p (b a d) -> p b a d", b=GB, a=2)
                                  ).then_inc(sig["h_read"], 1)
                after(dve, "h_read", i, 2)
                after(dve, "em_ready", i, 1)
                hall = hrow[:].rearrange("p b h d -> p (b h) d")
                wide = [P, GB * XH, XD]
                m_chain.link(v.scalar_tensor_tensor(den[:], hall[:, :, XD], -1.0, hall[:, :, XD], ALU.mult, ALU.max))
                m_chain.link(v.tensor_tensor(den[:], den[:], em[:], ALU.max))
                m_chain.link(v.tensor_scalar(den[:], den[:], HEAD_EPS, None, ALU.add))
                m_chain.link(v.reciprocal(den[:], den[:]))
                m_chain.link(v.tensor_tensor(hn, hall[:, :, 0:XD], den[:].unsqueeze(2).broadcast_to(wide), ALU.mult))
                m_chain.link(v.tensor_reduce(hmu[:], hn, AX.X, ALU.add))
                m_chain.link(v.tensor_scalar(hmu[:], hmu[:], 1.0 / XD, None, ALU.mult))
                m_chain.link(v.tensor_tensor(hn, hn, hmu[:].unsqueeze(2).broadcast_to(wide), ALU.subtract))
                m_chain.link(v.tensor_tensor(hsq, hn, hn, ALU.mult))
                m_chain.link(v.tensor_reduce(hva[:], hsq, AX.X, ALU.add))
                v.tensor_scalar(hva[:], hva[:], 1.0 / XD, HEAD_EPS, ALU.mult, ALU.add).then_inc(sig["hvar"], 1)
                after(dve, "hrstd", i, 1)
                m_chain.link(v.tensor_tensor(hn, hn, hva[:].unsqueeze(2).broadcast_to(wide), ALU.mult))
                hb = hn.rearrange("p (b h) d -> p b (h d)", b=GB)
                m_chain.link(v.tensor_tensor(hb, hb, rowv[:, 0:1, :].broadcast_to([P, GB, H]), ALU.mult))

            def mlstm_out(i):
                after(dve, "out_ready", i, 0)
                v.tensor_tensor(res[:].rearrange("p a b -> p (a b)"), xr[:].rearrange("p a b -> p (a b)"),
                                hn.rearrange("p a b -> p (a b)"), ALU.add).then_inc(sig["x2_ready"], 1)
                after(dve, "x2_ready", i, 1)
                layer_norm(i, m_chain, 3, lambda b: res[:, b, :], mv, bn, rstd, LN_EPS, rows).then_inc(sig["ln3_rows"], 1)
                m_chain.end()

            def node_proj(i, c):
                after(dve, "qk_read", i, 2 * c + 1)
                for h in range(HPC):
                    rs = slice(FD * h, FD * (h + 1))
                    v.tensor_copy(qheadr[rs, :, h, :].rearrange("p (b m) t -> p b m t", b=GB),
                                  qT[rs].rearrange("p m (b t) -> p b m t", b=GB))
                after(dve, "qk_read", i, 2 * c + 2)
                v.tensor_copy(kTr[:], kT[:]).then_inc(sig["qk_max_ready"], 1)
                for h in range(HPC):
                    rs = slice(FD * h, FD * (h + 1))
                    last = v.tensor_copy(qhead[rs, :, h, :].rearrange("p (b m) t -> p b m t", b=GB),
                                         qT[rs].rearrange("p m (b t) -> p b m t", b=GB))
                last.then_inc(sig["qhead_ready"], 1)

            def node_max(i, c):
                for s in range(STEPS):
                    after(dve, "smax_ps", i, c * STEPS + s + 1)
                    v.tensor_reduce(mx[:, s * HPC:(s + 1) * HPC],
                                    (FX, FY)[s % 2][:].rearrange("p (h k) -> p h k", h=HPC), AX.X,
                                    ALU.max).then_inc(sig["smax_read"], 1)

            def node_attn(i, c):
                after(dve, "den_inv", i, c + 1)
                v.tensor_tensor(aT[:].rearrange("p a b -> p (a b)"), FP[:], dinv[:].rearrange("p a b -> p (a b)"),
                                ALU.mult).then_inc(sig["attn_ready"], 1)

            def ffn_out(i):
                f_chain.start(i)
                after(dve, "rows_ps", i, 1)
                after(dve, "out_stored", i, 0)
                f_chain.link(layer_norm(i, f_chain, 4, lambda b: FP[:, b * H:(b + 1) * H], fmv, fbn, frstd, OUT_EPS,
                                        orow))
                f_chain.link(v.tensor_tensor(orow[:], orow[:], rowv[:, 1:2, :].broadcast_to([P, GB, H]), ALU.mult))
                f_chain.link(v.tensor_tensor(orow[:], orow[:], rowv[:, 2:3, :].broadcast_to([P, GB, H]), ALU.add))
                v.tensor_tensor(orow[:], orow[:], res[:], ALU.add).then_inc(sig["out_ready"], 1)
                f_chain.end()

            setup()
            for c in range(NODES):
                prep(c)
            dve.wait_ge(sig["consts_made"], 1)
            dve.wait_ge(sig["prep_read"], 3 * NODES)
            dve.drain()
            dve.sem_inc(sig["prep_made"], 1)
            with dve.Fori(0, NG) as i:
                mamba_in(i)
                units(i, 0, UNITS)
                mlstm(i)
                mlstm_out(i)
                for c in range(NODES):
                    node_proj(i, c)
                    node_max(i, c)
                    node_attn(i, c)
                ffn_out(i)

        @block.gpsimd
        def _(pool):
            g = nc.gpsimd
            g.memset(ones[:], 1.0)
            g.memset(hs_pad[:].rearrange("p a b t -> p (a b t)"), 0.0)
            for j in range(2):
                g.memset(dec[j][:].rearrange("p a b t -> p (a b t)"), 0.0)
            g.memset(qhead[:].rearrange("p s h t -> p (s h t)"), 0.0)
            g.memset(qheadr[:].rearrange("p s h t -> p (s h t)").bitcast(F32), 0.0)
            g.memset(mxT[:], 0.0)
            g.memset(vaug[:].rearrange("p b h d -> p (b h d)"), 1.0).then_inc(sig["consts_made"], 1)

            def units(i, k0, k1):
                for k in range(k0, k1):
                    hf, c, q = k // (UNITS // 2), k // PAIRS % IC, k % PAIRS
                    if k == 0:
                        after(pool, "dtu_ready", i, 1)
                    after(pool, "bc_read", i, 2 * (hf * PAIRS + q) + 1)
                    if k >= 2:
                        after(pool, "state", i, k - 1)
                    g.tensor_tensor(inf[k % 2][:].rearrange("p a (b t) -> p a b t", b=GB),
                                    dtu[:, c:c + 1, :, :].broadcast_to([P, 2, GB, L]),
                                    bs[:, q].rearrange("p a (b t) -> p a b t", b=GB), ALU.mult).then_inc(sig["inflow"], 1)

            def mlstm(i):
                g.memset(th[:].rearrange("p c n -> p (c n)"), 0.0).then_inc(sig["qpad_clear"], 1)
                g.tensor_copy(vaug[:, :, :, 0:XD], cr[:].rearrange("p b (h d) -> p b h d", h=XH)
                              ).then_inc(sig["vaug_ready"], 1)

            pool.wait_ge(sig["prep_made"], 1)
            with pool.Fori(0, NG) as i:
                units(i, 0, UNITS)
                mlstm(i)


def kernel(**inputs):
    import numpy as np
    import concourse.bacc as bacc
    from concourse.bass_utils import run_bass_kernel_spmd

    a = {k: np.asarray(v) for k, v in inputs.items()}

    def chunks(w):
        return np.ascontiguousarray(w.reshape(-1, P, w.shape[-1]).transpose(1, 0, 2))

    def cols(w):
        return w.reshape(w.shape[0] // P, P, -1).transpose(1, 0, 2).reshape(P, -1)

    consts = np.zeros((P, NC_), np.float32)
    consts[:, C_ID:C_ID + P] = np.eye(P)
    consts[0:R, C_MEAN:C_MEAN + R] = 1.0 / R
    for part, base in enumerate((R, R + 32)):
        consts[base:base + NS, C_MEAN + base:C_MEAN + base + 32] = 1.0 / NS
        for s in range(NS):
            consts[[base + s, base + NS + s], C_SEL + part * NS + s] = 1.0
        consts[base + NS:base + 32, C_LO] = -1.0
    consts[:, C_CAUSAL:C_CAUSAL + P] = np.where(np.arange(P)[:, None] <= np.arange(P)[None, :], 0.0, -BIG)

    bn_w, cn_w = a["L0_attn_b_ln_w"], a["L0_attn_c_ln_w"]
    norm = np.concatenate([a["L0_attn_dt_ln_w"], bn_w, bn_w, cn_w, cn_w])
    gbias = np.zeros((P, 2), np.float32)
    gbias[0:XH, 0], gbias[0:XH, 1] = a["L0_xattn_igate_bias"], a["L0_xattn_fgate_bias"]
    vecs = np.concatenate([
        cols(a["L0_attn_conv_b"]), cols(a["L0_attn_dt_proj_b"]), cols(a["L0_attn_D"]),
        cols(a["L0_attn_conv_w"]), cols(a["L0_attn_A_log"]), norm[:, None], gbias,
        a["L0_ffn_be"].reshape(EDGES, HC, P).transpose(2, 0, 1).reshape(P, -1),
        np.broadcast_to(a["L0_ffn_ew"].reshape(1, -1), (P, NODES * 3)),
        np.broadcast_to(a["L0_ffn_act_w"].reshape(1, -1), (P, NODES))], axis=1)
    rowvecs = np.stack([a["L0_xattn_outnorm_scale"], a["L0_ffn_ln_g"], a["L0_ffn_ln_b"]])
    xp = a["L0_attn_x_proj_w"]
    w_x = np.concatenate([xp[0:R], xp[R:R + NS], xp[R:R + NS], xp[R + NS:], xp[R + NS:]])
    gk = np.stack([a["L0_xattn_igate_kernel"], a["L0_xattn_fgate_kernel"]], axis=1)
    we = a["L0_ffn_We"]

    def many(w):
        return np.ascontiguousarray(np.swapaxes(w.reshape(*w.shape[:-2], HC, P, H), -3, -2))

    arrays = dict(
        x=a["x"], ctx_in=a["ctx_1024"], consts=consts, vecs=np.ascontiguousarray(vecs), rowvecs=rowvecs,
        w_in=chunks(a["L0_attn_in_proj_w"].T), w_x=chunks(w_x.T),
        w_dt=np.ascontiguousarray(a["L0_attn_dt_proj_w"].T), w_out=chunks(a["L0_attn_out_proj_w"].T),
        w_gate=chunks(gk.reshape(3 * H, -1)).reshape(P, 3 * HC, 2, XH),
        w_edge=many(we), w_edgeT=many(np.swapaxes(we, 1, 2)),
        w_node=many(np.stack([a["L0_ffn_Wq"], a["L0_ffn_Wk"], a["L0_ffn_Wv"], a["L0_ffn_Wo"]])))
    nc = bacc.Bacc("TRN2", target_bir_lowering=False, num_devices=1)
    args = {n: nc.dram_tensor(f"in_{n}", w.shape, mybir.dt.from_np(w.dtype), kind="ExternalInput").ap()
            for n, w in arrays.items()}
    out = nc.dram_tensor("out_dram", (B, L, H), F32, kind="ExternalOutput").ap()
    build(nc, **args, out=out)
    r = run_bass_kernel_spmd(nc, [{f"in_{n}": np.ascontiguousarray(w) for n, w in arrays.items()}], core_ids=[0])
    return r.results[0]["out_dram"]
```

```python
from contextlib import ExitStack

import concourse.bass as bass
from concourse import mybir

F32 = mybir.dt.float32
F32R = mybir.dt.float32r
BF16 = mybir.dt.bfloat16
ALU = mybir.AluOpType
ACT = mybir.ActivationFunctionType
AX = mybir.AxisListType

P = 128
B, L, H = 16, 128, 256
GB = 2
T = GB * L
NG = B // GB
HC = H // P
I = 2 * H
IC = I // P
NS = 16
R = 64
XH, XD = 4, 64
XP = XD + 1
NODES, EDGES = 6, 20
FH, FD = 8, 32
HPC = P // FD
BIG = 1e30
LN_EPS, RMS_EPS, HEAD_EPS, OUT_EPS = 1e-5, 1e-6, 1e-6, 1e-6

PAIRS = NS // 4
UNITS = 2 * IC * PAIRS
STEPS = GB * HC

GRAPH = []
_lind = 0
for _c in range(NODES):
    _n = min(_c + 1, 5)
    GRAPH.append(dict(q=_c - 1, k=_c - _n, v=_c - _n + _n // 2,
                      eq=_lind + _n - 1, ek=_lind, ev=_lind + _n // 2))
    _lind += _n

M_IN = [("m", "in", k) for k in range(8)]
M_UNITS = [("m", "unit", k) for k in range(UNITS)]
M_ML = [("m", "ml", k) for k in range(8)]
M_OUT = [("m", "out", 0)]
F_NODE = [[("f", "proj", c), ("f", "max", c), ("f", "score", c),
           *(("f", "attend", c * STEPS + s) for s in range(STEPS)), ("f", "node", c)] for c in range(NODES)]
F_ALL = [step for n in F_NODE for step in n] + [("f", "out", 0)]
M_ALL = M_IN + M_UNITS + M_ML
BODY = [step for pair in zip(F_ALL, M_ALL) for step in pair] + F_ALL[len(M_ALL):] + M_OUT
FIRST = M_IN[:4]
for _c in range(NODES):
    FIRST = FIRST + [("p", "prep", _c)] + (M_IN[4:] if _c == 0 else M_UNITS[8 * _c - 8:8 * _c])
FIRST = FIRST + M_ML + M_OUT

V_CONVB, V_DTB, V_D, V_CONVW, V_ALOG = 0, 4, 8, 12, 28
V_NORM = V_ALOG + IC * NS
V_GBI, V_GBF = V_NORM + 1, V_NORM + 2
V_BE = V_GBF + 1
V_EW = V_BE + EDGES * HC
V_ACTW = V_EW + NODES * 3
NV = V_ACTW + NODES
C_ID, C_MEAN, C_SEL, C_LO, C_CAUSAL = 0, P, 2 * P, 2 * P + 2 * NS, 2 * P + 2 * NS + 1
NC_ = C_CAUSAL + P

PER = dict(
    x_loaded=32,
    out_stored=16,
    ln1_rows=1, xnT_ps=1, xnT_ready=1,
    inproj_ps=4, inproj_read=4,
    tanh_u=1, tanh_g=1,
    conv_done=1, u_ready=1,
    xproj_ps=1, xsq=1, meansq_ps=1, rms_rstd=1, xdn_ready=1,
    dt_ps=2, dt_read=1, sp_tail=1, dt_ready=1, dtu_ready=1, split_ready=1,
    bc_ps=16, bc_read=16,
    decay=UNITS, inflow=UNITS, state=UNITS, outflow=UNITS, ysum=UNITS,
    y_read=8, y_ready=4,
    outproj_ps=1, x1_ready=1, ln_var2=1, ln_rstd2=1, ln2_rows=1,
    ctxT_ps=1, ctxT_ready=1, qT_ps=1, qT_ready=1, qpad_clear=1, qpad_ready=1, vaug_ready=1,
    gate_ps=1, gate_read=1, gate_tail=1, gates_ready=1, gates_ps=1, gates_rows=1,
    dbc_ps=2, sT_ps=2, dT_ready=2, cT_ready=2, h_ps=2, h_read=2, em_ready=1,
    ln_var1=1, ln_rstd1=1, hvar=1, hrstd=1,
    x2_ready=1, ln_var3=1, ln_rstd3=1, ln3_rows=1, n0T_ps=1, n0T_ready=1,
    q_ps=NODES, k_ps=NODES, v_ps=NODES, qk_read=2 * NODES, qk_max_ready=NODES, qhead_ready=NODES, v_ready=NODES,
    smax_ps=NODES * STEPS, smax_read=NODES * STEPS, maxT_ps=NODES, maxT_ready=NODES,
    score_ps=NODES * STEPS, prob=NODES * STEPS, attn_ps=NODES * STEPS,
    den_inv=NODES, attn_ready=NODES, node_ps=NODES, node_ready=NODES,
    rows_ps=1, ln_var4=1, ln_rstd4=1, out_ready=1,
    vec_m=44, vec_f=7, act_m=9, act_f=7,
)
CREDIT = ("x2_ready", "out_ready", "out_stored", "outproj_ps")
PRE = ["stats_seen", "const_loaded", "pool_consts", "pool_zeros", "vec_consts", "prep_ps", "prep_read", "prep_vec", "prep_bias_ps", "prep_bias",
       "w_loaded", "w_used", "a_made", "setup_act", "prep_made"]


def build(nc, x, ctx_in, consts, vecs, rowvecs, w_in, w_x, w_dt, w_out, w_gate, w_edge, w_edgeT, w_node, out):
    with ExitStack() as es:
        def sb(name, shape, dt=F32):
            return es.enter_context(nc.sbuf_tensor(name, shape, dt))

        sig = {n: es.enter_context(nc.semaphore(n)) for n in [*PER, *PRE]}

        cst = sb("cst", [P, NC_])
        vec = sb("vec", [P, NV])
        rowv = sb("rowv", [P, 3, H])
        ident = cst[:, C_ID:C_ID + P]
        ident_bf = sb("ident_bf", [P, P], BF16)
        negid_bf = sb("negid_bf", [P, 16], BF16)
        negid = sb("negid", [P, XH])
        sel = sb("sel", [P, 2 * NS], F32R)
        causal = sb("causal", [P, P], BF16)
        ones = sb("ones", [P, L])
        win = sb("win", [P, HC, 2 * I])
        wx = sb("wx", [P, IC, P])
        wdt = sb("wdt", [R, I])
        wout = sb("wout", [P, IC, H])
        wgate = sb("wgate", [P, 3 * HC, 2, XH])
        a_neg = sb("a_neg", [P, IC * NS])
        convh = sb("convh", [P, 20])
        wq_f = [sb(f"wq_f{c}", [P, HC, H]) for c in range(NODES)]
        wk_f = [sb(f"wk_f{c}", [P, HC, H]) for c in range(NODES)]
        wv_f = [sb(f"wv_f{c}", [P, HC, H]) for c in range(NODES)]
        we_f = [sb(f"we_f{c}", [P, HC, H]) for c in range(NODES)]
        wo_f = [sb(f"wo_f{c}", [P, HC, H]) for c in range(NODES)]
        fb = sb("fb", [P, NODES, 8])

        xr = sb("xr", [P, GB, H])
        cr = sb("cr", [P, GB, H])
        rows = sb("rows", [P, GB, H])
        bn = sb("bn", [P, GB, 6])
        mv = sb("mv", [P, GB, 2])
        rstd = sb("rstd", [P, GB])
        xnT = sb("xnT", [P, HC, T])
        ctxT = sb("ctxT", [P, HC, T])
        hs_pad = sb("hs_pad", [P, IC, GB, L + 3])
        u = sb("u", [P, IC, T])
        th = sb("th", [P, IC, T])
        gate = sb("gate", [P, IC, T])
        dt = sb("dt", [P, IC, T])
        dtu = hs_pad[:, :, :, 1:L + 1]
        xsq, xrs = rows[:, 0, :], rows[:, 1, :]
        xdn = sb("xdn", [P, T])
        bhi = sb("bhi", [P, T], F32R)
        bcr = sb("bcr", [P, T], F32R)
        bs = sb("bs", [P, PAIRS, 2, T])
        cs = sb("cs", [P, PAIRS, 2, T])
        dec = [sb(f"dec{j}", [P, 2, GB, L]) for j in range(2)]
        inf = [sb(f"inf{j}", [P, 2, T]) for j in range(2)]
        hst = [sb(f"hst{j}", [P, 2, T]) for j in range(3)]
        prd = [sb(f"prd{j}", [P, 2, T]) for j in range(2)]
        qpad = th[:].rearrange("p c (x t) -> p (c x t)", x=GB).rearrange("p (c a b t) -> p c a b t", c=HC, a=2, b=GB)
        vaug = sb("vaug", [P, GB, XH, XP])
        gfa, gfm = (dt[0:XH, x, :] for x in range(2))
        grow, gcum, gmax, gtop = (u[0:XH, x, :] for x in range(4))
        rm = sb("rm", [P, 2, GB * XH])
        free = bs[:].rearrange("p q a n -> p (q a n)").rearrange("p (x n) -> p x n", x=4)
        dT, cT = (free[:, x].rearrange("p (a b t) -> p a b t", a=2, b=GB) for x in (0, 1))
        hn, hsq = (free[:, x].rearrange("p (n d) -> p n d", d=XD) for x in (2, 3))
        hrow = sb("hrow", [P, GB, XH, XP])
        em = sb("em", [P, GB * XH])
        den = sb("den", [P, GB * XH])
        hmu = sb("hmu", [P, GB * XH])
        hva = sb("hva", [P, GB * XH])

        node = [sb(f"node{j}", [P, HC, T]) for j in range(5)]
        SLOT = {-1: 0, 0: 1, 1: 2, 2: 3, 3: 4, 4: 2, 5: 4}
        res = sb("res", [P, GB, H])
        qT = sb("qT", [P, HC, T])
        kT = sb("kT", [P, HC, T])
        qhead = sb("qhead", [P, STEPS, HPC, L])
        qheadr = sb("qheadr", [P, STEPS, HPC, L], F32R)
        kTr = sb("kTr", [P, HC, T], F32R)
        vrow = sb("vrow", [P, GB, H])
        bias_t = sb("bias_t", [P, HC])
        mx = sb("mx", [P, GB * FH])
        mxT = sb("mxT", [P, P], BF16)
        pr = [sb(f"pr{j}", [P, HPC, L]) for j in range(2)]
        dinv = sb("dinv", [P, HC, T])
        aT = sb("aT", [P, HC, T])
        fbn = sb("fbn", [P, GB, 6])
        fmv = sb("fmv", [P, GB, 2])
        frstd = sb("frstd", [P, GB])
        orow = sb("orow", [P, GB, H])

        ps = [es.enter_context(nc.psum_tensor(f"ps{j}", [P, 512], F32)) for j in range(8)]
        MA, MB, MY, FP, FQ, FX, FY, FV = ps
        stage = {n: t[:, :, :].rearrange("p a b -> p (a b)").rearrange("p (a b) -> p a b", a=HC)
                 for n, t in (("eqT", node[0]), ("ekT", node[1]), ("evT", node[2]), ("e", node[3]),
                              ("q", node[4]), ("k", qT), ("v", kT), ("o", aT))}

        block = es.enter_context(nc.Block())

        def after(eng, name, i, n):
            value = i * PER[name] + n + (name in CREDIT)
            if not (isinstance(value, int) and value <= 0):
                eng.wait_ge(sig[name], value)

        def walk(order, steps, f, m):
            for kind, name, n in order:
                if kind + name in steps:
                    steps[kind + name]({"f": f, "m": m, "p": 0}[kind], n)

        class Chain:

            def __init__(self, eng, name):
                self.eng, self.name, self.i, self.n = eng, name, 0, 0

            def start(self, i):
                self.i, self.n = i, 0

            def mark(self, ins):
                ins.then_inc(sig[self.name], 1)
                self.n += 1
                return self.n

            def wait(self, n):
                after(self.eng, self.name, self.i, n)

            def link(self, ins):
                self.wait(self.mark(ins))

            def end(self):
                assert self.n == PER[self.name], (self.name, self.n)

        @block.sync
        def _(sp):
            def load(dst, src):
                sp.dma_start(dst, src).then_inc(sig["const_loaded"], 16)

            for name in CREDIT:
                sp.sem_inc(sig[name], 1)
            def load_group(i):
                after(sp, "x2_ready", i, 0)
                sp.dma_start(xr[:], x[bass.ds(i * GB, GB)].rearrange("b t h -> t b h")).then_inc(sig["x_loaded"], 16)
                sp.dma_start(cr[:], ctx_in[bass.ds(i * GB, GB)].rearrange("b t h -> t b h")).then_inc(sig["x_loaded"], 16)

            def store_group(i):
                after(sp, "out_ready", i, 1)
                sp.dma_start(out[bass.ds(i * GB, GB)].rearrange("b t h -> t b h"), orow[:]).then_inc(sig["out_stored"], 16)

            load_group(0)
            load(cst[:], consts)
            load(vec[:], vecs)
            load(rowv[:], rowvecs.partition_broadcast(P))
            load(win[:], w_in)
            load(wx[:], w_x)
            load(wdt[:], w_dt)
            load(wout[:], w_out)
            load(wgate[:], w_gate)
            for c, g in enumerate(GRAPH):
                if c >= 1:
                    sp.wait_ge(sig["w_used"], c)
                for n, src in (("eqT", w_edgeT[g["eq"]]), ("ekT", w_edgeT[g["ek"]]), ("evT", w_edgeT[g["ev"]]),
                               ("e", w_edge[g["eq"]]), ("q", w_node[0, c]), ("k", w_node[1, c]),
                               ("v", w_node[2, c]), ("o", w_node[3, c])):
                    sp.dma_start(stage[n], src).then_inc(sig["w_loaded"], 16)

            with sp.Fori(0, NG - 1) as i:
                load_group(i + 1)
                store_group(i)
            store_group(NG - 1)
            sp.wait_ge(sig["out_stored"], 16 * NG + 1)

        @block.tensor
        def _(pe):
            mm, tr = nc.tensor.matmul, nc.tensor.transpose

            def prep(_, c):
                pe.wait_ge(sig["w_loaded"], 16 * 8 * (c + 1))
                for j, (e, w) in enumerate((("eqT", "q"), ("ekT", "k"), ("evT", "v"))):
                    bank = (FP, FQ, FX)[j]
                    if c >= 1:
                        pe.wait_ge(sig["prep_read"], 3 * (c - 1) + j + 1)
                    for a in range(HC):
                        for k in range(HC):
                            last = mm(bank[:, a * H:(a + 1) * H], stage[e][:, k, a * P:(a + 1) * P],
                                      stage[w][:, k, :], start=(k == 0), stop=(k == HC - 1))
                    last.then_inc(sig["prep_ps"], 1)
                if c >= 1:
                    pe.wait_ge(sig["prep_bias"], 2 * c)
                for j, (w, e) in enumerate((("q", "eq"), ("k", "ek"), ("v", "ev"))):
                    for a in range(HC):
                        for k in range(HC):
                            last = mm(FY[:, 2 * j + a:2 * j + a + 1], stage[w][:, k, a * P:(a + 1) * P],
                                      vec[:, V_BE + GRAPH[c][e] * HC + k:V_BE + GRAPH[c][e] * HC + k + 1],
                                      start=(k == 0), stop=(k == HC - 1))
                last.then_inc(sig["prep_bias_ps"], 1)
                pe.wait_ge(sig["prep_bias"], 2 * c + 1)
                for a in range(HC):
                    for k in range(HC):
                        last = mm(FY[:, 8 + a:9 + a], stage["o"][:, k, a * P:(a + 1) * P], fb[:, c, 4 + k:5 + k],
                                  start=(k == 0), stop=(k == HC - 1))
                last.then_inc(sig["prep_bias_ps"], 1)

            def rows_to_T(bank, src):
                for a in range(HC):
                    for b in range(GB):
                        last = tr(bank[:, a * T + b * L:a * T + (b + 1) * L], src[:, b, a * P:(a + 1) * P], ident)
                return last

            def mamba_in(i, step):
                if step == 0:
                    after(pe, "ln1_rows", i, 1)
                    rows_to_T(MA, rows).then_inc(sig["xnT_ps"], 1)
                if step in (1, 2):
                    after(pe, "xnT_ready", i, 1)
                    for j in (2 * step - 2, 2 * step - 1):
                        bank = (MB, MA)[j % 2]
                        if j >= 2:
                            after(pe, "inproj_read", i, j - 1)
                        for a in range(2):
                            m = 2 * j + a
                            for k in range(HC):
                                last = mm(bank[:, a * T:(a + 1) * T], win[:, k, m * P:(m + 1) * P], xnT[:, k, :],
                                          start=(k == 0), stop=(k == HC - 1))
                        last.then_inc(sig["inproj_ps"], 1)
                if step == 4:
                    after(pe, "inproj_read", i, 4)
                    after(pe, "u_ready", i, 1)
                    for k in range(IC):
                        last = mm(MA[:, 0:T], wx[:, k, :], u[:, k, :], start=(k == 0), stop=(k == IC - 1))
                    last.then_inc(sig["xproj_ps"], 1)
                if step == 5:
                    after(pe, "xsq", i, 1)
                    mm(MB[:, 0:T], cst[:, C_MEAN:C_MEAN + P], xsq, start=True, stop=True).then_inc(sig["meansq_ps"], 1)
                if step == 6:
                    after(pe, "xdn_ready", i, 1)
                    for j in range(2):
                        bank = (MA, MB)[j]
                        for a in range(2):
                            m = 2 * j + a
                            last = mm(bank[:, a * T:(a + 1) * T], wdt[:, m * P:(m + 1) * P], xdn[0:R, :],
                                      start=True, stop=True)
                        last.then_inc(sig["dt_ps"], 1)
                if step == 7:
                    after(pe, "split_ready", i, 1)
                    after(pe, "dt_read", i, 1)
                    for n in range(PAIRS):
                        spread(i, n)

            def spread(i, n):
                for j in range(2):
                    x = 2 * n + j
                    if n < PAIRS:
                        bank = (MA, MB, MY)[x % 3]
                        if x >= 3:
                            after(pe, "bc_read", i, x - 2)
                    else:
                        bank = MA
                        after(pe, "bc_read", i, x)
                    for a in range(2):
                        s = 2 * n + a
                        last = mm(bank[:, a * T:(a + 1) * T],
                                  sel[:, j * NS + s:j * NS + s + 1].broadcast_to([P, P]), bcr[:], start=True, stop=True)
                    last.then_inc(sig["bc_ps"], 1)

            def sum_states(i, k):
                m, q = k // PAIRS, k % PAIRS
                if k == 0:
                    after(pe, "bc_read", i, 2 * PAIRS)
                after(pe, "outflow", i, k + 1)
                if q == 0 and m >= 2:
                    after(pe, "y_read", i, m - 1)
                for a in range(2):
                    last = mm((MY, MB)[m % 2][:, 0:T], ident, prd[k % 2][:, a, :],
                              start=(q == 0 and a == 0), stop=(q == PAIRS - 1 and a == 1))
                last.then_inc(sig["ysum"], 1)

            def unit(i, k):
                if UNITS // 2 - 2 <= k < UNITS // 2 - 2 + PAIRS:
                    spread(i, k - (UNITS // 2 - 2) + PAIRS)
                if k >= 2:
                    sum_states(i, k - 2)

            def mlstm(i, step):
                if step == 0:
                    sum_states(i, UNITS - 2)
                    sum_states(i, UNITS - 1)
                if step == 1:
                    after(pe, "bc_read", i, 16)
                    after(pe, "y_ready", i, 4)
                    for b in range(GB):
                        for k in range(IC):
                            last = mm(MA[:, b * H:(b + 1) * H], gate[:, k, b * L:(b + 1) * L], wout[:, k, :],
                                      start=(k == 0), stop=(k == IC - 1))
                    last.then_inc(sig["outproj_ps"], 1)
                    rows_to_T(MB, cr).then_inc(sig["ctxT_ps"], 1)
                if step == 2:
                    after(pe, "ln2_rows", i, 1)
                    rows_to_T(MA, rows).then_inc(sig["qT_ps"], 1)
                if step == 3:
                    after(pe, "ctxT_ready", i, 1)
                    after(pe, "qT_ready", i, 1)
                    for gsel in range(2):
                        for k in range(3 * HC):
                            src = xnT if k < HC else ctxT
                            last = mm(MB[0:XH, gsel * T:(gsel + 1) * T], wgate[:, k, gsel, :], src[:, k % HC, :],
                                      start=(k == 0), stop=(k == 3 * HC - 1))
                    last.then_inc(sig["gate_ps"], 1)
                if step == 4:
                    after(pe, "gates_ready", i, 1)
                    after(pe, "qpad_ready", i, 1)
                    decay_rows(i, 0)
                    for j, src in enumerate((grow, gtop)):
                        for b in range(GB):
                            last = tr(MY[:, (j * GB + b) * XH:(j * GB + b + 1) * XH], src[:, b * L:(b + 1) * L],
                                      cst[0:XH, C_ID:C_ID + XH])
                    last.then_inc(sig["gates_ps"], 1)
                    head_scores(i, 0)
                if step == 5:
                    after(pe, "dT_ready", i, 1)
                    decay_rows(i, 1)
                    after(pe, "vaug_ready", i, 1)
                    after(pe, "gates_rows", i, 1)
                    head_values(i, 0)
                    head_scores(i, 1)
                if step == 6:
                    after(pe, "h_read", i, 1)
                    head_values(i, 1)

            def decay_rows(i, hp):
                for a in range(2):
                    h = 2 * hp + a
                    mm(MA[:, a * T:(a + 1) * T], negid[0:XH, h:h + 1].broadcast_to([XH, P]), gmax,
                       start=True, stop=False)
                    last = mm(MA[:, a * T:(a + 1) * T], ident_bf[:],
                              causal[:].unsqueeze(1).broadcast_to([P, GB, L]), start=False, stop=True)
                last.then_inc(sig["dbc_ps"], 1)

            def head_scores(i, hp):
                if hp:
                    after(pe, "cT_ready", i, 1)
                for b in range(GB):
                    last = mm(MB[:].rearrange("p (a b t) -> p a b t", a=2, b=GB)[:, :, b, :],
                              ctxT[:, hp, b * L:(b + 1) * L], qpad[:, hp, :, b, :], start=True, stop=True)
                last.then_inc(sig["sT_ps"], 1)

            def head_values(i, hp):
                after(pe, "cT_ready", i, hp + 1)
                for b in range(GB):
                    for a in range(2):
                        j = b * 2 + a
                        last = mm(MY[:, j * XP:(j + 1) * XP], cT[:, a, b, :], vaug[:, b, 2 * hp + a, :],
                                  start=True, stop=True)
                last.then_inc(sig["h_ps"], 1)

            def mlstm_out(i, _):
                after(pe, "ln3_rows", i, 1)
                rows_to_T(MA, rows).then_inc(sig["n0T_ps"], 1)

            def node_proj(i, c):
                g = GRAPH[c]
                if c == 0:
                    after(pe, "n0T_ready", i, 1)
                    after(pe, "out_ready", i, 0)
                else:
                    after(pe, "node_ready", i, c)
                for bank, w, src, s in ((FP, wq_f, g["q"], "q_ps"), (FQ, wk_f, g["k"], "k_ps")):
                    for a in range(HC):
                        for k in range(HC):
                            last = mm(bank[:, a * T:(a + 1) * T], w[c][:, k, a * P:(a + 1) * P],
                                      node[SLOT[src]][:, k, :], start=(k == 0), stop=(k == HC - 1))
                    last.then_inc(sig[s], 1)
                for b in range(GB):
                    for k in range(HC):
                        last = mm(FV[:, b * H:(b + 1) * H], node[SLOT[g["v"]]][:, k, b * L:(b + 1) * L],
                                  wv_f[c][:, k, :], start=(k == 0), stop=(k == HC - 1))
                last.then_inc(sig["v_ps"], 1)

            def node_max(i, c):
                after(pe, "qk_max_ready", i, c + 1)
                for s in range(STEPS):
                    b, m = s // HC, s % HC
                    bank = (FX, FY)[s % 2]
                    if s >= 2:
                        after(pe, "smax_read", i, c * STEPS + s - 1)
                    elif c >= 1:
                        after(pe, "prob", i, c * STEPS)
                    for h in range(HPC):
                        last = mm(bank[:, h * L:(h + 1) * L], qheadr[:, s, h, :], kTr[:, m, b * L:(b + 1) * L],
                                  start=True, stop=True)
                    last.then_inc(sig["smax_ps"], 1)

            def node_score(i, c):
                after(pe, "smax_read", i, (c + 1) * STEPS)
                after(pe, "v_ready", i, c + 1)
                tr(FV[0:GB * FH, 0:P], mx[:], ident).then_inc(sig["maxT_ps"], 1)
                after(pe, "maxT_ready", i, c + 1)
                after(pe, "qhead_ready", i, c + 1)
                node_scores(i, c, 0)
                node_scores(i, c, 1)

            def node_scores(i, c, s):
                b, m = s // HC, s % HC
                bank = (FX, FY)[s % 2]
                if s >= 2:
                    after(pe, "prob", i, c * STEPS + s - 1)
                mm(bank[:], kT[:, m, b * L:(b + 1) * L], qhead[:, s].rearrange("p h t -> p (h t)"),
                   start=True, stop=False, skip_group_check=True)
                for h in range(HPC):
                    j = s * HPC + h
                    last = mm(bank[:, h * L:(h + 1) * L], negid_bf[:, j:j + 1].broadcast_to([P, P]),
                              mxT[:], start=False, stop=(h == HPC - 1), skip_group_check=True)
                last.then_inc(sig["score_ps"], 1)

            def node_attend(i, cs_):
                c, s = cs_ // STEPS, cs_ % STEPS
                b, m = s // HC, s % HC
                after(pe, "prob", i, c * STEPS + s + 1)
                for h in range(HPC):
                    r0 = FD * h
                    at = (m * GB + b) * L
                    mm(FP[r0:r0 + FD, at:at + L], vrow[:, b, m * P + r0:m * P + r0 + FD], pr[s % 2][:, h, :],
                       start=True, stop=True, tile_position=(0, r0))
                    last = mm(FQ[r0:r0 + FD, at:at + L], ones[:, 0:FD], pr[s % 2][:, h, :],
                              start=True, stop=True, tile_position=(0, r0))
                last.then_inc(sig["attn_ps"], 1)
                if s + 2 < STEPS:
                    node_scores(i, c, s + 2)

            def node_out(i, c):
                after(pe, "attn_ready", i, c + 1)
                src = node[SLOT[GRAPH[c]["q"]]]
                for a in range(HC):
                    for k in range(HC):
                        mm(FV[:, a * T:(a + 1) * T], we_f[c][:, k, a * P:(a + 1) * P], src[:, k, :],
                           start=(k == 0), stop=False)
                    for k in range(HC):
                        last = mm(FV[:, a * T:(a + 1) * T], wo_f[c][:, k, a * P:(a + 1) * P], aT[:, k, :],
                                  start=False, stop=(k == HC - 1))
                last.then_inc(sig["node_ps"], 1)

            def ffn_out(i, _):
                after(pe, "node_ready", i, NODES)
                for b in range(GB):
                    for a in range(HC):
                        last = tr(FP[:, b * H + a * P:b * H + (a + 1) * P],
                                  node[SLOT[NODES - 1]][:, a, b * L:(b + 1) * L], ident)
                last.then_inc(sig["rows_ps"], 1)

            steps = dict(pprep=prep, min=mamba_in, munit=unit, mml=mlstm, mout=mlstm_out, fproj=node_proj,
                         fmax=node_max, fscore=node_score, fattend=node_attend, fnode=node_out, fout=ffn_out)
            pe.wait_ge(sig["const_loaded"], 16 * 8)
            pe.wait_ge(sig["vec_consts"], 1)
            pe.wait_ge(sig["pool_consts"], 1)
            walk(FIRST, steps, None, 0)
            pe.wait_ge(sig["prep_made"], 1)
            pe.wait_ge(sig["pool_zeros"], 1)
            with pe.Fori(0, NG - 1) as i:
                walk(BODY, steps, i, i + 1)
            walk(F_ALL, steps, NG - 1, None)

        @block.scalar
        def _(act):
            fn = nc.scalar.activation

            m_chain, f_chain = Chain(act, "act_m"), Chain(act, "act_f")

            def rstd_of(chain, var_sig, done_sig, i, dst):
                after(act, var_sig, i, 1)
                chain.link(fn(dst, dst, ACT.Ln))
                fn(dst, dst, ACT.Exp, scale=-0.5).then_inc(sig[done_sig], 1)

            def prep(_, c):
                for j, (w, e) in enumerate(((wq_f, 0), (wk_f, 1), (wv_f, 2))):
                    act.wait_ge(sig["prep_ps"], 3 * c + j + 1)
                    bank = (FP, FQ, FX)[j]
                    fn(w[c][:].rearrange("p a b -> p (a b)"), bank[:], ACT.Copy,
                       scale=vec[:, V_EW + 3 * c + e:V_EW + 3 * c + e + 1]).then_inc(sig["prep_read"], 1)

            def mamba_in(i, step):
                if step == 0:
                    m_chain.start(i)
                    rstd_of(m_chain, "ln_var1", "ln_rstd1", i, rstd[:])
                    after(act, "xnT_ps", i, 1)
                    fn(xnT[:].rearrange("p a b -> p (a b)"), MA[:], ACT.Copy).then_inc(sig["xnT_ready"], 1)
                if step == 1:
                    for j in range(2):
                        after(act, "inproj_ps", i, j + 1)
                        bank = (MB, MA)[j % 2]
                        for a in range(2):
                            last = fn(hs_pad[:, 2 * j + a, :, 1:L + 1],
                                      bank[:, a * T:(a + 1) * T].rearrange("p (b t) -> p b t", b=GB), ACT.Copy)
                        last.then_inc(sig["inproj_read"], 1)
                if step == 2:
                    after(act, "outproj_ps", i, 0)
                    for j in range(2, 4):
                        after(act, "inproj_ps", i, j + 1)
                        bank = (MB, MA)[j % 2]
                        fn(gate[:, 2 * j - 4:2 * j - 2, :].rearrange("p a b -> p (a b)"), bank[:], ACT.Copy,
                           scale=0.5).then_inc(sig["inproj_read"], 1)
                if step == 3:
                    after(act, "inproj_read", i, 4)
                    fn(dt[:], gate[:], ACT.Tanh).then_inc(sig["tanh_g"], 1)
                    after(act, "conv_done", i, 1)
                    fn(th[:], u[:], ACT.Tanh).then_inc(sig["tanh_u"], 1)
                    act.preload_act_table_set("natural_log_exp_and_others")
                if step == 4:
                    after(act, "xproj_ps", i, 1)
                    fn(xsq, MA[:, 0:T], ACT.Square).then_inc(sig["xsq"], 1)
                if step == 5:
                    after(act, "meansq_ps", i, 1)
                    m_chain.link(fn(xrs, MB[:, 0:T], ACT.Ln, bias=RMS_EPS))
                    fn(xrs, xrs, ACT.Exp, scale=-0.5).then_inc(sig["rms_rstd"], 1)
                if step == 6:
                    for c in range(IC):
                        if c % 2 == 0:
                            after(act, "dt_ps", i, c // 2 + 1)
                        last = fn(dt[:, c, :], (MA, MB)[c // 2][:, (c % 2) * T:(c % 2 + 1) * T], ACT.Identity,
                                  bias=vec[:, V_DTB + c:V_DTB + c + 1])
                    last.then_inc(sig["dt_read"], 1)
                    after(act, "dt_read", i, 1)
                    m_chain.link(fn(th[:], dt[:], ACT.Abs))
                    m_chain.link(fn(th[:], th[:], ACT.Exp, scale=-1.0))
                    fn(th[:], th[:], ACT.Ln, bias=1.0).then_inc(sig["sp_tail"], 1)
                if step == 7:
                    for n in range(PAIRS):
                        copies(i, n)

            def copies(i, n):
                q = n % PAIRS
                for j, dst in enumerate((bs, cs)):
                    x = 2 * n + j
                    after(act, "bc_ps", i, x + 1)
                    if n >= PAIRS:
                        after(act, ("inflow", "outflow")[j], i, UNITS // 2 - PAIRS + q + 1)
                    bank = (MA, MB, MY)[x % 3] if n < PAIRS else MA
                    fn(dst[:, q].rearrange("p a b -> p (a b)"), bank[:], ACT.Copy).then_inc(sig["bc_read"], 1)

            def unit(i, k):
                hf, c, q = k // (UNITS // 2), k // PAIRS % IC, k % PAIRS
                if k == 0:
                    after(act, "dt_ready", i, 1)
                if k >= 2:
                    after(act, "state", i, k - 1)
                for a in range(2):
                    s = hf * (NS // 2) + 2 * q + a
                    last = fn(dec[k % 2][:, a, :, 1:L],
                              dt[:, c, :].rearrange("p (b t) -> p b t", b=GB)[:, :, 1:L], ACT.Exp,
                              scale=a_neg[:, c * NS + s:c * NS + s + 1])
                last.then_inc(sig["decay"], 1)
                if UNITS // 2 - 2 <= k < UNITS // 2 - 2 + PAIRS:
                    copies(i, k - (UNITS // 2 - 2) + PAIRS)

            def mlstm(i, step):
                if step == 1:
                    rstd_of(m_chain, "ln_var2", "ln_rstd2", i, rstd[:])
                    after(act, "ctxT_ps", i, 1)
                    fn(ctxT[:].rearrange("p a b -> p (a b)"), MB[:], ACT.Copy).then_inc(sig["ctxT_ready"], 1)
                if step == 2:
                    after(act, "qT_ps", i, 1)
                    fn(xnT[:].rearrange("p a b -> p (a b)"), MA[:], ACT.Copy).then_inc(sig["qT_ready"], 1)
                    after(act, "qpad_clear", i, 1)
                    for a in range(2):
                        rs = slice(XD * a, XD * (a + 1))
                        last = fn(qpad[rs, :, a, :, :].rearrange("p c b t -> p c (b t)"),
                                  MA[rs, :].rearrange("p (c n) -> p c n", c=HC), ACT.Copy)
                    last.then_inc(sig["qpad_ready"], 1)
                if step == 3:
                    after(act, "gate_ps", i, 1)
                    fn(grow, MB[0:XH, 0:T], ACT.Identity, bias=vec[0:XH, V_GBI:V_GBI + 1])
                    fn(gfm, MB[0:XH, T:2 * T], ACT.Identity, bias=vec[0:XH, V_GBF:V_GBF + 1]).then_inc(sig["gate_read"], 1)
                    after(act, "gate_read", i, 1)
                    m_chain.link(fn(gfa, gfm, ACT.Abs))
                    m_chain.link(fn(gfa, gfa, ACT.Exp, scale=-1.0))
                    fn(gfa, gfa, ACT.Ln, bias=1.0).then_inc(sig["gate_tail"], 1)
                if step == 4:
                    after(act, "gates_ps", i, 1)
                    fn(rm[:].rearrange("p a b -> p (a b)"), MY[:, 0:2 * GB * XH], ACT.Copy).then_inc(sig["gates_rows"], 1)
                    after(act, "gates_rows", i, 1)
                    fn(em[:], rm[:, 1, :], ACT.Exp, scale=-1.0).then_inc(sig["em_ready"], 1)
                if step in (4, 5):
                    hp = step - 4
                    after(act, "dbc_ps", i, hp + 1)
                    if hp:
                        after(act, "cT_ready", i, 1)
                    for a in range(2):
                        for b in range(GB):
                            h = 2 * hp + a
                            last = fn(dT[:, a, b, :], MA[:, a * T + b * L:a * T + (b + 1) * L], ACT.Exp,
                                      bias=rm[:, 0, b * XH + h:b * XH + h + 1])
                    last.then_inc(sig["dT_ready"], 1)
                if step == 7:
                    rstd_of(m_chain, "hvar", "hrstd", i, hva[:])

            def mlstm_out(i, _):
                rstd_of(m_chain, "ln_var3", "ln_rstd3", i, rstd[:])
                after(act, "n0T_ps", i, 1)
                fn(node[0][:].rearrange("p a b -> p (a b)"), MA[:], ACT.Copy).then_inc(sig["n0T_ready"], 1)
                m_chain.end()

            def node_proj(i, c):
                if c == 0:
                    f_chain.start(i)
                after(act, "q_ps", i, c + 1)
                for a in range(HC):
                    last = fn(qT[:, a, :], FP[:, a * T:(a + 1) * T], ACT.Identity, bias=fb[:, c, a:a + 1])
                last.then_inc(sig["qk_read"], 1)
                after(act, "k_ps", i, c + 1)
                for a in range(HC):
                    last = fn(kT[:, a, :], FQ[:, a * T:(a + 1) * T], ACT.Identity, bias=fb[:, c, 2 + a:3 + a])
                last.then_inc(sig["qk_read"], 1)
                after(act, "v_ps", i, c + 1)
                fn(vrow[:].rearrange("p a b -> p (a b)"), FV[:], ACT.Copy).then_inc(sig["v_ready"], 1)

            def node_score(i, c):
                after(act, "maxT_ps", i, c + 1)
                fn(mxT[0:GB * FH, :], FV[0:GB * FH, 0:P], ACT.Copy).then_inc(sig["maxT_ready"], 1)
                node_prob(i, c, 0)

            def node_attend(i, cs_):
                c, s = cs_ // STEPS, cs_ % STEPS
                if s + 1 < STEPS:
                    node_prob(i, c, s + 1)
                else:
                    node_den(i, c)

            def node_prob(i, c, s):
                after(act, "score_ps", i, c * STEPS + s + 1)
                if s >= 2:
                    after(act, "attn_ps", i, c * STEPS + s - 1)
                fn(pr[s % 2][:].rearrange("p a b -> p (a b)"), (FX, FY)[s % 2][:], ACT.Exp,
                   scale=FD ** -0.5).then_inc(sig["prob"], 1)

            def node_den(i, c):
                after(act, "attn_ps", i, (c + 1) * STEPS)
                f_chain.link(fn(dinv[:].rearrange("p a b -> p (a b)"), FQ[:], ACT.Ln))
                fn(dinv[:], dinv[:], ACT.Exp, scale=-1.0).then_inc(sig["den_inv"], 1)

            def node_out(i, c):
                after(act, "node_ps", i, c + 1)
                for a in range(HC):
                    last = fn(node[SLOT[c]][:, a, :], FV[:, a * T:(a + 1) * T], ACT.Identity,
                              bias=fb[:, c, 6 + a:7 + a])
                last.then_inc(sig["node_ready"], 1)

            def ffn_out(i, _):
                rstd_of(f_chain, "ln_var4", "ln_rstd4", i, frstd[:])
                f_chain.end()

            steps = dict(pprep=prep, min=mamba_in, munit=unit, mml=mlstm, mout=mlstm_out, fproj=node_proj,
                         fscore=node_score, fattend=node_attend, fnode=node_out, fout=ffn_out)
            act.wait_ge(sig["const_loaded"], 16 * 8)
            act.preload_act_table_set("natural_log_exp_and_others")
            fn(a_neg[:], vec[:, V_ALOG:V_ALOG + IC * NS], ACT.Exp).then_inc(sig["setup_act"], 1)
            act.wait_ge(sig["vec_consts"], 1)
            act.wait_ge(sig["pool_consts"], 1)
            walk(FIRST, steps, None, 0)
            act.wait_ge(sig["pool_zeros"], 1)
            act.wait_ge(sig["prep_made"], 1)
            with act.Fori(0, NG - 1) as i:
                act.preload_act_table_set("natural_log_exp_and_others")
                walk(BODY, steps, i, i + 1)
            walk(F_ALL, steps, NG - 1, None)

        @block.vector
        def _(dve):
            v = nc.vector
            m_chain, f_chain = Chain(dve, "vec_m"), Chain(dve, "vec_f")

            def col(n):
                return vec[:, n:n + 1]

            def setup():
                dve.wait_ge(sig["const_loaded"], 16 * 8)
                v.tensor_copy(ident_bf[:], ident)
                v.tensor_scalar(negid_bf[:], cst[:, C_ID:C_ID + GB * FH], -1.0, None, ALU.mult)
                v.tensor_scalar(negid[:], cst[:, C_ID:C_ID + XH], -1.0, None, ALU.mult)
                v.tensor_copy(sel[:], cst[:, C_SEL:C_SEL + 2 * NS])
                v.tensor_copy(causal[:], cst[:, C_CAUSAL:C_CAUSAL + P])
                v.tensor_scalar(convh[:, 0:4], vec[:, V_CONVB:V_CONVB + 4], 0.5, None, ALU.mult)
                v.tensor_scalar(convh[:, 4:20], vec[:, V_CONVW:V_CONVW + 16], 0.5, None, ALU.mult)
                dve.wait_ge(sig["setup_act"], 1)
                v.tensor_scalar(a_neg[:], a_neg[:], -1.0, None, ALU.mult).then_inc(sig["vec_consts"], 1)
                dve.wait_ge(sig["vec_consts"], 1)
                dve.wait_ge(sig["pool_consts"], 1)

            def prep(_, c):
                g = GRAPH[c]
                ew0, ew1, ew2 = (col(V_EW + 3 * c + j) for j in range(3))
                dve.wait_ge(sig["w_loaded"], 16 * 8 * (c + 1))
                v.tensor_scalar(we_f[c][:], stage["e"], ew0, None, ALU.mult)
                v.tensor_scalar(wo_f[c][:], stage["o"], col(V_ACTW + c), None, ALU.mult)
                dve.wait_ge(sig["prep_bias_ps"], 2 * c + 1)
                for j, e in enumerate((ew0, ew1, ew2)):
                    last = v.tensor_scalar(fb[:, c, 2 * j:2 * j + 2], FY[:, 2 * j:2 * j + 2], e, None, ALU.mult)
                last.then_inc(sig["prep_bias"], 1)
                v.tensor_scalar(bias_t[:], vec[:, V_BE + g["eq"] * HC:V_BE + (g["eq"] + 1) * HC], ew0, None,
                                ALU.mult).then_inc(sig["prep_vec"], 1)
                dve.wait_ge(sig["prep_bias_ps"], 2 * c + 2)
                dve.wait_ge(sig["prep_vec"], c + 1)
                v.scalar_tensor_tensor(fb[:, c, 6:8], FY[:, 8:10], col(V_ACTW + c), bias_t[:], ALU.mult,
                                       ALU.add).then_inc(sig["prep_bias"], 1)
                dve.wait_ge(sig["prep_bias"], 2 * c + 2)
                dve.sem_inc(sig["w_used"], 1)

            def layer_norm(i, chain, n, src, mean_var, stats, inv, eps, dst):
                for b in range(GB):
                    m = chain.mark(v.bn_stats(stats[:, b, :], src(b)))
                chain.wait(m)
                dve.sem_inc(sig["stats_seen"], 1)
                for b in range(GB):
                    m = chain.mark(v.bn_aggr(mean_var[:, b, :], stats[:, b, :]))
                chain.wait(m)
                v.tensor_scalar(inv[:], mean_var[:, :, 1], eps, None, ALU.add).then_inc(sig[f"ln_var{n}"], 1)
                after(dve, f"ln_rstd{n}", i, 1)
                for b in range(GB):
                    last = v.tensor_scalar(dst[:, b, :], src(b), mean_var[:, b, 0:1], inv[:, b:b + 1],
                                           ALU.subtract, ALU.mult)
                return last

            def mamba_in(i, step):
                if step == 0:
                    m_chain.start(i)
                    after(dve, "x_loaded", i, 32)
                    layer_norm(i, m_chain, 1, lambda b: xr[:, b, :], mv, bn, rstd, LN_EPS, rows).then_inc(sig["ln1_rows"], 1)
                if step == 2:
                    after(dve, "inproj_read", i, 2)
                    marks = [m_chain.mark(v.tensor_scalar(u[:, c, :].rearrange("p (b t) -> p b t", b=GB),
                                                          hs_pad[:, c, :, 0:L], convh[:, 4 + c * 4:5 + c * 4],
                                                          convh[:, c:c + 1], ALU.mult, ALU.add)) for c in range(IC)]
                    for k in range(1, 4):
                        for c in range(IC):
                            m_chain.wait(marks[c])
                            uc = u[:, c, :].rearrange("p (b t) -> p b t", b=GB)
                            ins = v.scalar_tensor_tensor(uc, hs_pad[:, c, :, k:k + L],
                                                         convh[:, 4 + c * 4 + k:5 + c * 4 + k], uc, ALU.mult, ALU.add)
                            if k < 3:
                                marks[c] = m_chain.mark(ins)
                    ins.then_inc(sig["conv_done"], 1)
                if step == 3:
                    after(dve, "tanh_g", i, 1)
                    m_chain.mark(v.scalar_tensor_tensor(gate[:], dt[:], 1.0, gate[:], ALU.add, ALU.mult))
                    after(dve, "tanh_u", i, 1)
                    v.scalar_tensor_tensor(u[:], th[:], 1.0, u[:], ALU.add, ALU.mult).then_inc(sig["u_ready"], 1)
                if step == 5:
                    after(dve, "rms_rstd", i, 1)
                    v.scalar_tensor_tensor(xdn[:], MA[:, 0:T], col(V_NORM), xrs, ALU.mult,
                                           ALU.mult).then_inc(sig["xdn_ready"], 1)
                    after(dve, "xdn_ready", i, 1)
                    m_chain.link(v.tensor_copy(bhi[:], xdn[:]))
                    v.scalar_tensor_tensor(bcr[:], bhi[:].bitcast(F32), cst[:, C_LO:C_LO + 1], xdn[:],
                                           ALU.mult, ALU.add).then_inc(sig["split_ready"], 1)
                if step == 6:
                    after(dve, "sp_tail", i, 1)
                    v.scalar_tensor_tensor(dt[:], dt[:], 0.0, th[:], ALU.max, ALU.add).then_inc(sig["dt_ready"], 1)
                    after(dve, "dt_ready", i, 1)
                    v.tensor_tensor(dtu, dt[:].rearrange("p c (b t) -> p c b t", b=GB),
                                    u[:].rearrange("p c (b t) -> p c b t", b=GB), ALU.mult).then_inc(sig["dtu_ready"], 1)

            def scan(i, k):
                after(dve, "decay", i, k + 1)
                after(dve, "inflow", i, k + 1)
                if k >= 3:
                    after(dve, "outflow", i, k - 2)
                v.tensor_tensor_scan(hst[k % 3][:].rearrange("p a b -> p (a b)"),
                                     dec[k % 2][:].rearrange("p a b t -> p (a b t)"),
                                     inf[k % 2][:].rearrange("p a b -> p (a b)"), 0.0, ALU.mult,
                                     ALU.add).then_inc(sig["state"], 1)

            def weigh(i, k):
                q = k % PAIRS
                after(dve, "state", i, k + 1)
                if k >= 2:
                    after(dve, "ysum", i, k - 1)
                after(dve, "bc_read", i, 2 * (k // (UNITS // 2) * PAIRS + q) + 2)
                v.tensor_tensor(prd[k % 2][:], hst[k % 3][:], cs[:, q], ALU.mult).then_inc(sig["outflow"], 1)

            def gather(i, m):
                hf, c = m // IC, m % IC
                after(dve, "ysum", i, (m + 1) * PAIRS)
                src = (MY, MB)[m % 2][:, 0:T]
                if hf == 0:
                    v.scalar_tensor_tensor(u[:, c, :], u[:, c, :], col(V_D + c), src, ALU.mult,
                                           ALU.add).then_inc(sig["y_read"], 1)
                else:
                    v.tensor_tensor(u[:, c, :], u[:, c, :], src, ALU.add).then_inc(sig["y_read"], 1)
                    after(dve, "y_read", i, m + 1)
                    v.tensor_tensor(gate[:, c, :], gate[:, c, :], u[:, c, :], ALU.mult).then_inc(sig["y_ready"], 1)

            def unit(i, k):
                scan(i, k)
                if k >= 1:
                    weigh(i, k - 1)
                if k % PAIRS == 2 and k > PAIRS:
                    gather(i, k // PAIRS - 1)

            def head_rows(i, hp):
                after(dve, "h_ps", i, hp + 1)
                v.tensor_copy(hrow[:, :, 2 * hp:2 * hp + 2, :],
                              MY[:, 0:2 * GB * XP].rearrange("p (b a d) -> p b a d", b=GB, a=2)
                              ).then_inc(sig["h_read"], 1)

            def mlstm(i, step):
                if step == 0:
                    weigh(i, UNITS - 1)
                    gather(i, 2 * IC - 1)
                if step == 1:
                    after(dve, "outproj_ps", i, 1)
                    v.tensor_tensor(xr[:].rearrange("p a b -> p (a b)"), xr[:].rearrange("p a b -> p (a b)"), MA[:],
                                    ALU.add).then_inc(sig["x1_ready"], 1)
                    after(dve, "x1_ready", i, 1)
                    layer_norm(i, m_chain, 2, lambda b: xr[:, b, :], mv, bn, rstd, LN_EPS, rows).then_inc(sig["ln2_rows"], 1)
                if step == 3:
                    after(dve, "gate_tail", i, 1)
                    m_chain.link(v.scalar_tensor_tensor(gfm, gfm, 0.0, gfa, ALU.min, ALU.subtract))
                    for b in range(GB):
                        m = m_chain.mark(v.tensor_tensor_scan(gcum[:, b * L:(b + 1) * L], ones[0:XH, 0:L],
                                                              gfm[:, b * L:(b + 1) * L], 0.0, ALU.mult, ALU.add))
                    m_chain.wait(m)
                    m_chain.link(v.tensor_tensor(grow, grow, gcum, ALU.subtract))
                    for b in range(GB):
                        m = m_chain.mark(v.tensor_tensor_scan(gmax[:, b * L:(b + 1) * L], grow[:, b * L:(b + 1) * L],
                                                              grow[:, b * L:(b + 1) * L], -BIG, ALU.max, ALU.max))
                    m_chain.wait(m)
                    v.tensor_tensor(gtop, gcum, gmax, ALU.add).then_inc(sig["gates_ready"], 1)
                if step in (4, 5):
                    hp = step - 4
                    if hp:
                        head_rows(i, 0)
                    after(dve, "sT_ps", i, hp + 1)
                    after(dve, "dT_ready", i, hp + 1)
                    v.scalar_tensor_tensor(cT.rearrange("p a b t -> p (a b t)"), MB[:], XD ** -0.5,
                                           dT.rearrange("p a b t -> p (a b t)"), ALU.mult,
                                           ALU.mult).then_inc(sig["cT_ready"], 1)
                if step == 6:
                    head_rows(i, 1)
                if step == 7:
                    after(dve, "h_read", i, 2)
                    after(dve, "em_ready", i, 1)
                    hall = hrow[:].rearrange("p b h d -> p (b h) d")
                    wide = [P, GB * XH, XD]
                    m_chain.link(v.scalar_tensor_tensor(den[:], hall[:, :, XD], -1.0, hall[:, :, XD], ALU.mult, ALU.max))
                    m_chain.link(v.tensor_tensor(den[:], den[:], em[:], ALU.max))
                    m_chain.link(v.tensor_scalar(den[:], den[:], HEAD_EPS, None, ALU.add))
                    m_chain.link(v.reciprocal(den[:], den[:]))
                    m_chain.link(v.tensor_tensor(hn, hall[:, :, 0:XD], den[:].unsqueeze(2).broadcast_to(wide), ALU.mult))
                    m_chain.link(v.tensor_reduce(hmu[:], hn, AX.X, ALU.add))
                    m_chain.link(v.tensor_scalar(hmu[:], hmu[:], 1.0 / XD, None, ALU.mult))
                    m_chain.link(v.tensor_tensor(hn, hn, hmu[:].unsqueeze(2).broadcast_to(wide), ALU.subtract))
                    m_chain.link(v.tensor_tensor(hsq, hn, hn, ALU.mult))
                    m_chain.link(v.tensor_reduce(hva[:], hsq, AX.X, ALU.add))
                    v.tensor_scalar(hva[:], hva[:], 1.0 / XD, HEAD_EPS, ALU.mult, ALU.add).then_inc(sig["hvar"], 1)
                    after(dve, "hrstd", i, 1)
                    m_chain.link(v.tensor_tensor(hn, hn, hva[:].unsqueeze(2).broadcast_to(wide), ALU.mult))
                    hb = hn.rearrange("p (b h) d -> p b (h d)", b=GB)
                    m_chain.link(v.tensor_tensor(hb, hb, rowv[:, 0:1, :].broadcast_to([P, GB, H]), ALU.mult))

            def mlstm_out(i, _):
                after(dve, "out_ready", i, 0)
                v.tensor_tensor(res[:].rearrange("p a b -> p (a b)"), xr[:].rearrange("p a b -> p (a b)"),
                                hn.rearrange("p a b -> p (a b)"), ALU.add).then_inc(sig["x2_ready"], 1)
                after(dve, "x2_ready", i, 1)
                layer_norm(i, m_chain, 3, lambda b: res[:, b, :], mv, bn, rstd, LN_EPS, rows).then_inc(sig["ln3_rows"], 1)
                m_chain.end()

            def node_proj(i, c):
                after(dve, "qk_read", i, 2 * c + 1)
                for h in range(HPC):
                    rs = slice(FD * h, FD * (h + 1))
                    v.tensor_copy(qheadr[rs, :, h, :].rearrange("p (b m) t -> p b m t", b=GB),
                                  qT[rs].rearrange("p m (b t) -> p b m t", b=GB))
                after(dve, "qk_read", i, 2 * c + 2)
                v.tensor_copy(kTr[:], kT[:]).then_inc(sig["qk_max_ready"], 1)
                for h in range(HPC):
                    rs = slice(FD * h, FD * (h + 1))
                    last = v.tensor_copy(qhead[rs, :, h, :].rearrange("p (b m) t -> p b m t", b=GB),
                                         qT[rs].rearrange("p m (b t) -> p b m t", b=GB))
                last.then_inc(sig["qhead_ready"], 1)

            def node_max(i, c):
                for s in range(STEPS):
                    after(dve, "smax_ps", i, c * STEPS + s + 1)
                    v.tensor_reduce(mx[:, s * HPC:(s + 1) * HPC],
                                    (FX, FY)[s % 2][:].rearrange("p (h k) -> p h k", h=HPC), AX.X,
                                    ALU.max).then_inc(sig["smax_read"], 1)

            def node_attend(i, cs_):
                c, s = cs_ // STEPS, cs_ % STEPS
                if s < STEPS - 1:
                    return
                after(dve, "den_inv", i, c + 1)
                v.tensor_tensor(aT[:].rearrange("p a b -> p (a b)"), FP[:], dinv[:].rearrange("p a b -> p (a b)"),
                                ALU.mult).then_inc(sig["attn_ready"], 1)

            def ffn_out(i, _):
                f_chain.start(i)
                after(dve, "rows_ps", i, 1)
                after(dve, "out_stored", i, 0)
                f_chain.link(layer_norm(i, f_chain, 4, lambda b: FP[:, b * H:(b + 1) * H], fmv, fbn, frstd, OUT_EPS,
                                        orow))
                f_chain.link(v.tensor_tensor(orow[:], orow[:], rowv[:, 1:2, :].broadcast_to([P, GB, H]), ALU.mult))
                f_chain.link(v.tensor_tensor(orow[:], orow[:], rowv[:, 2:3, :].broadcast_to([P, GB, H]), ALU.add))
                v.tensor_tensor(orow[:], orow[:], res[:], ALU.add).then_inc(sig["out_ready"], 1)
                f_chain.end()

            steps = dict(pprep=prep, min=mamba_in, munit=unit, mml=mlstm, mout=mlstm_out, fproj=node_proj,
                         fmax=node_max, fattend=node_attend, fout=ffn_out)
            setup()
            walk(FIRST, steps, None, 0)
            dve.wait_ge(sig["pool_zeros"], 1)
            dve.wait_ge(sig["prep_read"], 3 * NODES)
            dve.wait_ge(sig["prep_bias"], 2 * NODES)
            dve.sem_inc(sig["prep_made"], 1)
            with dve.Fori(0, NG - 1) as i:
                walk(BODY, steps, i, i + 1)
            walk(F_ALL, steps, NG - 1, None)

        @block.gpsimd
        def _(pool):
            g = nc.gpsimd
            g.memset(ones[:], 1.0)
            g.memset(hs_pad[:].rearrange("p a b t -> p (a b t)"), 0.0)
            for j in range(2):
                g.memset(dec[j][:].rearrange("p a b t -> p (a b t)"), 0.0)
            g.memset(vaug[:].rearrange("p b h d -> p (b h d)"), 1.0).then_inc(sig["pool_consts"], 1)
            g.memset(qhead[:].rearrange("p s h t -> p (s h t)"), 0.0)
            g.memset(qheadr[:].rearrange("p s h t -> p (s h t)").bitcast(F32), 0.0)
            g.memset(mxT[:], 0.0).then_inc(sig["pool_zeros"], 1)

            def unit(i, k):
                hf, c, q = k // (UNITS // 2), k // PAIRS % IC, k % PAIRS
                if k == 0:
                    after(pool, "dtu_ready", i, 1)
                after(pool, "bc_read", i, 2 * (hf * PAIRS + q) + 1)
                if k >= 2:
                    after(pool, "state", i, k - 1)
                g.tensor_tensor(inf[k % 2][:].rearrange("p a (b t) -> p a b t", b=GB),
                                dtu[:, c:c + 1, :, :].broadcast_to([P, 2, GB, L]),
                                bs[:, q].rearrange("p a (b t) -> p a b t", b=GB), ALU.mult).then_inc(sig["inflow"], 1)

            def mlstm(i, step):
                if step == 0:
                    g.memset(th[:].rearrange("p c n -> p (c n)"), 0.0).then_inc(sig["qpad_clear"], 1)
                    g.tensor_copy(vaug[:, :, :, 0:XD], cr[:].rearrange("p b (h d) -> p b h d", h=XH)
                                  ).then_inc(sig["vaug_ready"], 1)

            steps = dict(munit=unit, mml=mlstm)
            walk(FIRST, steps, None, 0)
            with pool.Fori(0, NG - 1) as i:
                walk(BODY, steps, i, i + 1)


def kernel(**inputs):
    import numpy as np
    import concourse.bacc as bacc
    from concourse.bass_utils import run_bass_kernel_spmd

    a = {k: np.asarray(v) for k, v in inputs.items()}

    def chunks(w):
        return np.ascontiguousarray(w.reshape(-1, P, w.shape[-1]).transpose(1, 0, 2))

    def cols(w):
        return w.reshape(w.shape[0] // P, P, -1).transpose(1, 0, 2).reshape(P, -1)

    consts = np.zeros((P, NC_), np.float32)
    consts[:, C_ID:C_ID + P] = np.eye(P)
    consts[0:R, C_MEAN:C_MEAN + R] = 1.0 / R
    for part, base in enumerate((R, R + 32)):
        consts[base:base + NS, C_MEAN + base:C_MEAN + base + 32] = 1.0 / NS
        for s in range(NS):
            consts[[base + s, base + NS + s], C_SEL + part * NS + s] = 1.0
        consts[base + NS:base + 32, C_LO] = -1.0
    consts[:, C_CAUSAL:C_CAUSAL + P] = np.where(np.arange(P)[:, None] <= np.arange(P)[None, :], 0.0, -BIG)

    bn_w, cn_w = a["L0_attn_b_ln_w"], a["L0_attn_c_ln_w"]
    norm = np.concatenate([a["L0_attn_dt_ln_w"], bn_w, bn_w, cn_w, cn_w])
    gbias = np.zeros((P, 2), np.float32)
    gbias[0:XH, 0], gbias[0:XH, 1] = a["L0_xattn_igate_bias"], a["L0_xattn_fgate_bias"]
    vecs = np.concatenate([
        cols(a["L0_attn_conv_b"]), cols(a["L0_attn_dt_proj_b"]), cols(a["L0_attn_D"]),
        cols(a["L0_attn_conv_w"]), cols(a["L0_attn_A_log"]), norm[:, None], gbias,
        a["L0_ffn_be"].reshape(EDGES, HC, P).transpose(2, 0, 1).reshape(P, -1),
        np.broadcast_to(a["L0_ffn_ew"].reshape(1, -1), (P, NODES * 3)),
        np.broadcast_to(a["L0_ffn_act_w"].reshape(1, -1), (P, NODES))], axis=1)
    rowvecs = np.stack([a["L0_xattn_outnorm_scale"], a["L0_ffn_ln_g"], a["L0_ffn_ln_b"]])
    xp = a["L0_attn_x_proj_w"]
    w_x = np.concatenate([xp[0:R], xp[R:R + NS], xp[R:R + NS], xp[R + NS:], xp[R + NS:]])
    gk = np.stack([a["L0_xattn_igate_kernel"], a["L0_xattn_fgate_kernel"]], axis=1)
    we = a["L0_ffn_We"]

    def many(w):
        return np.ascontiguousarray(np.swapaxes(w.reshape(*w.shape[:-2], HC, P, H), -3, -2))

    arrays = dict(
        x=a["x"], ctx_in=a["ctx_1024"], consts=consts, vecs=np.ascontiguousarray(vecs), rowvecs=rowvecs,
        w_in=chunks(a["L0_attn_in_proj_w"].T), w_x=chunks(w_x.T),
        w_dt=np.ascontiguousarray(a["L0_attn_dt_proj_w"].T), w_out=chunks(a["L0_attn_out_proj_w"].T),
        w_gate=chunks(gk.reshape(3 * H, -1)).reshape(P, 3 * HC, 2, XH),
        w_edge=many(we), w_edgeT=many(np.swapaxes(we, 1, 2)),
        w_node=many(np.stack([a["L0_ffn_Wq"], a["L0_ffn_Wk"], a["L0_ffn_Wv"], a["L0_ffn_Wo"]])))
    nc = bacc.Bacc("TRN2", target_bir_lowering=False, num_devices=1)
    args = {n: nc.dram_tensor(f"in_{n}", w.shape, mybir.dt.from_np(w.dtype), kind="ExternalInput").ap()
            for n, w in arrays.items()}
    out = nc.dram_tensor("out_dram", (B, L, H), F32, kind="ExternalOutput").ap()
    build(nc, **args, out=out)
    r = run_bass_kernel_spmd(nc, [{f"in_{n}": np.ascontiguousarray(w) for n, w in arrays.items()}], core_ids=[0])
    return r.results[0]["out_dram"]
```

```python
from contextlib import ExitStack

import concourse.bass as bass
from concourse import mybir

F32 = mybir.dt.float32
F32R = mybir.dt.float32r
BF16 = mybir.dt.bfloat16
ALU = mybir.AluOpType
ACT = mybir.ActivationFunctionType
AX = mybir.AxisListType

P = 128
B, L, H = 16, 128, 256
GB = 2
T = GB * L
NG = B // GB
HC = H // P
I = 2 * H
IC = I // P
NS = 16
R = 64
XH, XD = 4, 64
XP = XD + 1
NODES, EDGES = 6, 20
FH, FD = 8, 32
HPC = P // FD
BIG = 1e30
LN_EPS, RMS_EPS, HEAD_EPS, OUT_EPS = 1e-5, 1e-6, 1e-6, 1e-6

PAIRS = NS // 4
GF = 32
GROWS = GF + XH
UNITS = 2 * IC * PAIRS
INFLOW_V = [k for k in range(UNITS) if k % PAIRS == 1]
STEPS = GB * HC

GRAPH = []
_lind = 0
for _c in range(NODES):
    _n = min(_c + 1, 5)
    GRAPH.append(dict(q=_c - 1, k=_c - _n, v=_c - _n + _n // 2,
                      eq=_lind + _n - 1, ek=_lind, ev=_lind + _n // 2))
    _lind += _n

A_IN = [("a", "in", k) for k in range(11)]
M_UNITS = [("m", "unit", k) for k in range(UNITS)]
M_ML = [("m", "ml", k) for k in range(9)]
M_OUT = [("m", "out", 0), ("m", "out", 1)]
M_KEEP = [("m", "keep", 0)]
F_NODE = [[("f", "proj", c), ("f", "max", c), ("f", "score", c),
           *(("f", "attend", c * STEPS + s) for s in range(STEPS)), ("f", "node", c)] for c in range(NODES)]
F_START = F_NODE[0][:1]
F_ALL = [step for n in F_NODE for step in n][1:]
F_OUT = [("f", "out", 0)]
MIX = [step for pair in zip(M_ML + M_OUT[:1], A_IN) for step in pair] + M_OUT[1:] + A_IN[10:]
M_AFTER = [2, 2, 1, 0, 1, 1, 1, 0, 1, 1, 1, 1, 0, 3, 1, 0, 3, 0, 0, 2, 1, 3, 1, 1,
           2, 1, 2, 0, 0, 1, 0, 0, 0, 1, 0, 1, 1, 0, 1, 2, 1, 1, 0, 1, 0, 1, 0, 0, 0]
A_AFTER = [0, 0, 0, 0, 0, 0, 0, 0, 0, 0, 0, 0, 0, 0, 0, 0, 0, 0, 0, 0, 0, 0, 0, 0,
           0, 0, 0, 0, 0, 0, 1, 1, 0, 0, 1, 1, 0, 1, 0, 1, 1, 1, 0, 0, 0, 0, 1, 0, 2]


def beside_f(a_steps):
    order, m, a = [], 0, 0
    for n, step in enumerate(F_ALL + [("g", "proj", 0)] + F_OUT):
        order = order + [step] + (M_UNITS + M_ML + M_OUT)[m:m + M_AFTER[n]] + a_steps[a:a + A_AFTER[n]]
        m, a = m + M_AFTER[n], a + A_AFTER[n]
    return order


BODY = beside_f(A_IN) + M_KEEP
BODY_END = beside_f([]) + M_KEEP
PREP = [[("p", "prep", 3 * c + part) for part in range(3)] for c in range(NODES)]
FIRST_IN = (A_IN[:4] + PREP[0][:1] + A_IN[4:6] + PREP[0][1:2] + A_IN[6:8] + PREP[0][2:] + A_IN[8:])
FIRST = []
for _c in range(1, NODES - 1):
    _u = M_UNITS[8 * (_c - 1):8 * _c]
    FIRST = FIRST + _u[:5] + PREP[_c][:1] + _u[5:6] + PREP[_c][1:2] + _u[6:7] + PREP[_c][2:] + _u[7:]
_p = PREP[NODES - 1]
FIRST = FIRST + MIX[:4] + _p[:1] + MIX[4:6] + _p[1:2] + MIX[6:8] + _p[2:] + MIX[8:] + M_KEEP

V_CONVB, V_DTB, V_D, V_CONVW, V_ALOG = 0, 4, 8, 12, 28
V_NORM = V_ALOG + IC * NS
V_GBI = V_NORM + 1
V_BE = V_GBI + 1
V_EW = V_BE + EDGES * HC
V_ACTW = V_EW + NODES * 3
NV = V_ACTW + NODES
C_ID, C_MEAN, C_SEL, C_LO, C_CAUSAL = 0, P, 2 * P, 2 * P + 2 * NS, 2 * P + 2 * NS + 1
NC_ = C_CAUSAL + P

PER = dict(
    x_loaded=16, c_loaded=16,
    out_stored=16,
    ln1_rows=1, xnT_ps=1, xnT_ready=1,
    inproj_ps=4, inproj_read=4,
    tanh_u=1, tanh_g=1,
    conv_done=1, u_ready=1,
    xproj_ps=1, xsq=1, meansq_ps=1, rms_rstd=1, xdn_ready=1,
    dt_ps=2, dt_read=2, sp_tail=1, dt_ready=1, dtu_ready=1, split_ready=1,
    bc_ps=16, bc_read=16,
    decay=UNITS, inflow=UNITS - len(INFLOW_V), inflow_v=len(INFLOW_V), state=UNITS, outflow=UNITS, ysum=UNITS,
    y_read=8, y_ready=4,
    outproj_ps=1, x_kept=1, x1_ready=1, ln_var2=1, ln_rstd2=1, ln2_rows=1,
    ctxT_ps=1, ctxT_ready=1, qT_ps=1, qT_ready=1, qpad_clear=1, qpad_ready=1, vaug_ready=1,
    gate_ps=1, gate_read=1, gate_tail=1, gates_ready=1, gates_ps=1, gates_rows=1,
    dbc_ps=2, sT_ps=2, dT_ready=2, cT_ready=2, h_ps=2, h_read=2, em_ready=1,
    ln_var1=1, ln_rstd1=1, hvar=1, hrstd=1,
    x2_ready=1, res_ready=1, ln_var3=1, ln_rstd3=1, ln3_rows=1, n0T_ps=1, n0T_ready=1,
    q_ps=NODES, k_ps=NODES, v_ps=NODES, q_read=2 * NODES, k_read=NODES, qk_max_ready=2 * NODES, qhead_ready=NODES,
    v_ready=NODES,
    smax_ps=NODES * STEPS, smax_read=NODES * STEPS, maxT_ps=NODES, maxT_ready=NODES,
    score_ps=NODES * STEPS, prob=NODES * STEPS, attn_ps=NODES * STEPS,
    den_inv=NODES, attn_ready=NODES, node_ps=NODES, node_ready=NODES,
    rows_ps=1, ln_var4=1, ln_rstd4=1, out_ready=1,
    vec_a=17, vec_m=26, vec_f=7, act_a=4, act_m=5, act_f=7,
)
CREDIT = ("out_ready", "out_stored", "outproj_ps")
PRE = ["stats_seen", "ctx_seen", "const_loaded", "pool_consts", "pool_zeros", "vec_consts", "prep_ps", "prep_read", "prep_vec", "prep_bias_ps", "prep_bias",
       "w_loaded", "w_used", "a_made", "setup_act", "prep_made"]


def build(nc, x, ctx_in, consts, vecs, rowvecs, w_in, w_x, w_dt, w_out, w_gate, w_edge, w_edgeT, w_node, out):
    with ExitStack() as es:
        def sb(name, shape, dt=F32):
            return es.enter_context(nc.sbuf_tensor(name, shape, dt))

        sig = {n: es.enter_context(nc.semaphore(n)) for n in [*PER, *PRE]}

        cst = sb("cst", [P, NC_])
        vec = sb("vec", [P, NV])
        rowv = sb("rowv", [P, 3, H])
        ident = cst[:, C_ID:C_ID + P]
        ident_bf = sb("ident_bf", [P, P], BF16)
        negid_bf = sb("negid_bf", [P, 16], BF16)
        negid = sb("negid", [P, XH])
        sel = sb("sel", [P, 2 * NS], F32R)
        causal = sb("causal", [P, P], BF16)
        ones = sb("ones", [P, L])
        win = sb("win", [P, HC, 2 * I])
        wx = sb("wx", [P, IC, P])
        wdt = sb("wdt", [R, I])
        wout = sb("wout", [P, IC, H])
        wgate = sb("wgate", [P, 3 * HC, GROWS])
        a_neg = sb("a_neg", [P, IC * NS])
        convh = sb("convh", [P, 20])
        wq_f = [sb(f"wq_f{c}", [P, HC, H]) for c in range(NODES)]
        wk_f = [sb(f"wk_f{c}", [P, HC, H]) for c in range(NODES)]
        wv_f = [sb(f"wv_f{c}", [P, HC, H]) for c in range(NODES)]
        we_f = [sb(f"we_f{c}", [P, HC, H]) for c in range(NODES)]
        wo_f = [sb(f"wo_f{c}", [P, HC, H]) for c in range(NODES)]
        fb = sb("fb", [P, NODES, 8])

        xin = sb("xin", [P, GB, H])
        xr = sb("xr", [P, GB, H])
        cr = sb("cr", [P, GB, H])
        rows = sb("rows", [P, GB, H])
        bn = sb("bn", [P, GB, 6])
        mv = sb("mv", [P, GB, 2])
        rstd = sb("rstd", [P, GB])
        xnT = sb("xnT", [P, HC, T])
        ctxT = sb("ctxT", [P, HC, T])
        hs_pad = sb("hs_pad", [P, IC, GB, L + 3])
        u = sb("u", [P, IC, T])
        th = sb("th", [P, IC, T])
        gate = sb("gate", [P, IC, T])
        dt = sb("dt", [P, IC, T])
        dtu = hs_pad[:, :, :, 1:L + 1]
        xsq, xrs = rows[:, 0, :], rows[:, 1, :]
        xdn = sb("xdn", [P, T])
        bhi = th[:, 0, :].bitcast(F32R)
        bcr = sb("bcr", [P, T], F32R)
        bs = sb("bs", [P, PAIRS, 2, T])
        cs = sb("cs", [P, PAIRS, 2, T])
        dec = [sb(f"dec{j}", [P, 2, GB, L]) for j in range(2)]
        unit_buf = sb("unit_buf", [P, 8, 2 * T])
        inf, hst, prd = ([unit_buf[:, j].rearrange("p (a n) -> p a n", a=2) for j in slots]
                         for slots in ((0, 1), (2, 3, 4), (5, 6, 7)))
        acc = sb("acc", [P, 2, T])
        ych = [sb(f"ych{j}", [P, T]) for j in range(2)]
        mrow, mqT = (unit_buf[:, j].rearrange("p (a n) -> p a n", a=2) for j in (0, 1))
        qpad = unit_buf[:, 2:4].rearrange("p x n -> p (x n)").rearrange("p (c a b t) -> p c a b t", c=HC, a=2, b=GB)
        vaug = sb("vaug", [P, GB, XH, XP])
        gfa, gfm, grow, gcum, gmax, gtop = (unit_buf[0:XH, 4 + x // 2, x % 2 * T:(x % 2 + 1) * T] for x in range(6))
        mbn = sb("mbn", [P, GB, 6])
        mmv = sb("mmv", [P, GB, 2])
        mrstd = sb("mrstd", [P, GB])
        rm = sb("rm", [P, 2, GB * XH])
        free = bs[:].rearrange("p q a n -> p (q a n)").rearrange("p (x n) -> p x n", x=4)
        dT, cT = (free[:, x].rearrange("p (a b t) -> p a b t", a=2, b=GB) for x in (0, 1))
        hn, hsq = (free[:, x].rearrange("p (n d) -> p n d", d=XD) for x in (2, 3))
        hrow = sb("hrow", [P, GB, XH, XP])
        em = sb("em", [P, GB * XH])
        den = sb("den", [P, GB * XH])
        hmu = sb("hmu", [P, GB * XH])
        hva = sb("hva", [P, GB * XH])

        node = [sb(f"node{j}", [P, HC, T]) for j in range(5)]
        SLOT = {-1: 0, 0: 1, 1: 2, 2: 3, 3: 4, 4: 2, 5: 4}
        res = sb("res", [P, GB, H])
        qT = sb("qT", [P, HC, T])
        kT = sb("kT", [P, HC, T])
        qhead = sb("qhead", [P, STEPS, HPC, L])
        qheadr = sb("qheadr", [P, STEPS, HPC, L], F32R)
        kTr = sb("kTr", [P, HC, T], F32R)
        vrow = sb("vrow", [P, GB, H])
        bias_t = sb("bias_t", [P, HC])
        mx = sb("mx", [P, GB * FH])
        mxT = sb("mxT", [P, P], BF16)
        pr = [sb(f"pr{j}", [P, HPC, L]) for j in range(2)]
        aT = sb("aT", [P, HC, T])
        dinv = aT
        fbn = sb("fbn", [P, GB, 6])
        fmv = sb("fmv", [P, GB, 2])
        frstd = sb("frstd", [P, GB])
        orow = sb("orow", [P, GB, H])

        ps = [es.enter_context(nc.psum_tensor(f"ps{j}", [P, 512], F32)) for j in range(8)]
        MA, MB, MY, FP, FQ, FX, FY, FV = ps
        SMAX = ((0, FX), (2, FV), (1, FP), (3, FQ))
        stage = {n: t[:, :, :].rearrange("p a b -> p (a b)").rearrange("p (a b) -> p a b", a=HC)
                 for n, t in (("eqT", node[0]), ("ekT", node[1]), ("evT", node[2]), ("e", node[3]),
                              ("q", node[4]), ("k", qT), ("v", kT), ("o", aT))}

        block = es.enter_context(nc.Block())

        def after(eng, name, i, n):
            value = i * PER[name] + n + (name in CREDIT)
            if not (isinstance(value, int) and value <= 0):
                eng.wait_ge(sig[name], value)

        def added(k):
            return k // PAIRS * PAIRS + max(k % PAIRS, 1)

        def inflow(on, k):
            c, q = k // PAIRS % IC, k % PAIRS
            return on.tensor_tensor(inf[k % 2][:].rearrange("p a (b t) -> p a b t", b=GB),
                                    dtu[:, c:c + 1, :, :].broadcast_to([P, 2, GB, L]),
                                    bs[:, q].rearrange("p a (b t) -> p a b t", b=GB), ALU.mult)

        def inflow_done(eng, i, k):
            by_v = k in INFLOW_V
            after(eng, "inflow_v" if by_v else "inflow", i,
                  sum((j in INFLOW_V) == by_v for j in range(k + 1)))

        def walk(order, steps, f, m):
            for kind, name, n in order:
                if kind + name in steps:
                    group = {"f": lambda: f, "g": lambda: f + 1, "m": lambda: m, "a": lambda: m + 1,
                             "p": lambda: 0}[kind]()
                    steps[kind + name](group, n)

        class Chain:

            def __init__(self, eng, name):
                self.eng, self.name, self.i, self.n = eng, name, 0, 0

            def start(self, i):
                self.i, self.n = i, 0

            def mark(self, ins):
                ins.then_inc(sig[self.name], 1)
                self.n += 1
                return self.n

            def wait(self, n):
                after(self.eng, self.name, self.i, n)

            def link(self, ins):
                self.wait(self.mark(ins))

            def end(self):
                assert self.n == PER[self.name], (self.name, self.n)

        @block.sync
        def _(sp):
            def load(dst, src):
                sp.dma_start(dst, src).then_inc(sig["const_loaded"], 16)

            for name in CREDIT:
                sp.sem_inc(sig[name], 1)

            def load_x(i):
                after(sp, "x_kept", i - 1, 1)
                sp.dma_start(xin[:], x[bass.ds(i * GB, GB)].rearrange("b t h -> t b h")).then_inc(sig["x_loaded"], 16)

            def load_ctx(i):
                for name in ("vaug_ready", "ctxT_ps"):
                    after(sp, name, i - 1, 1)
                sp.dma_start(cr[:], ctx_in[bass.ds(i * GB, GB)].rearrange("b t h -> t b h")).then_inc(sig["c_loaded"], 16)

            def store_group(i):
                after(sp, "out_ready", i, 1)
                sp.dma_start(out[bass.ds(i * GB, GB)].rearrange("b t h -> t b h"), orow[:]).then_inc(sig["out_stored"], 16)

            load_x(0)
            load(cst[:], consts)
            load(vec[:], vecs)
            load(rowv[:], rowvecs.partition_broadcast(P))
            load(win[:], w_in)
            load(wx[:], w_x)
            load(wdt[:], w_dt)
            load(wout[:], w_out)
            load(wgate[:], w_gate)
            for c, g in enumerate(GRAPH):
                if c >= 1:
                    sp.wait_ge(sig["w_used"], c)
                for n, src in (("eqT", w_edgeT[g["eq"]]), ("ekT", w_edgeT[g["ek"]]), ("evT", w_edgeT[g["ev"]]),
                               ("e", w_edge[g["eq"]]), ("q", w_node[0, c]), ("k", w_node[1, c]),
                               ("v", w_node[2, c]), ("o", w_node[3, c])):
                    sp.dma_start(stage[n], src).then_inc(sig["w_loaded"], 16)

            load_ctx(0)
            load_x(1)
            with sp.Fori(0, NG - 2) as i:
                load_ctx(i + 1)
                load_x(i + 2)
                store_group(i)
            load_ctx(NG - 1)
            store_group(NG - 2)
            store_group(NG - 1)
            sp.wait_ge(sig["out_stored"], 16 * NG + 1)

        @block.tensor
        def _(pe):
            mm, tr = nc.tensor.matmul, nc.tensor.transpose

            def prep(_, n):
                c, part = n // 3, n % 3
                if part == 1:
                    pe.wait_ge(sig["prep_bias"], 2 * c + 1)
                    for a in range(HC):
                        for k in range(HC):
                            last = mm(FY[:, 8 + a:9 + a], stage["o"][:, k, a * P:(a + 1) * P],
                                      fb[:, c, 4 + k:5 + k], start=(k == 0), stop=(k == HC - 1))
                    last.then_inc(sig["prep_bias_ps"], 1)
                if part:
                    return
                pe.wait_ge(sig["w_loaded"], 16 * 8 * (c + 1))
                for j, (e, w) in enumerate((("eqT", "q"), ("ekT", "k"), ("evT", "v"))):
                    bank = (FP, FQ, FX)[j]
                    if c >= 1:
                        pe.wait_ge(sig["prep_read"], 3 * (c - 1) + j + 1)
                    for a in range(HC):
                        for k in range(HC):
                            last = mm(bank[:, a * H:(a + 1) * H], stage[e][:, k, a * P:(a + 1) * P],
                                      stage[w][:, k, :], start=(k == 0), stop=(k == HC - 1))
                    last.then_inc(sig["prep_ps"], 1)
                if c >= 1:
                    pe.wait_ge(sig["prep_bias"], 2 * c)
                for j, (w, e) in enumerate((("q", "eq"), ("k", "ek"), ("v", "ev"))):
                    for a in range(HC):
                        for k in range(HC):
                            last = mm(FY[:, 2 * j + a:2 * j + a + 1], stage[w][:, k, a * P:(a + 1) * P],
                                      vec[:, V_BE + GRAPH[c][e] * HC + k:V_BE + GRAPH[c][e] * HC + k + 1],
                                      start=(k == 0), stop=(k == HC - 1))
                last.then_inc(sig["prep_bias_ps"], 1)

            def rows_to_T(bank, src):
                for a in range(HC):
                    for b in range(GB):
                        last = tr(bank[:, a * T + b * L:a * T + (b + 1) * L], src[:, b, a * P:(a + 1) * P], ident)
                return last

            def mamba_in(i, step):
                if step == 1:
                    after(pe, "ln1_rows", i, 1)
                    rows_to_T(MA, rows).then_inc(sig["xnT_ps"], 1)
                if step in (2, 3, 4, 5):
                    j = step - 2
                    if j == 0:
                        after(pe, "xnT_ready", i, 1)
                    else:
                        after(pe, "inproj_read", i, j)
                    for a in range(2):
                        m = 2 * j + a
                        for k in range(HC):
                            last = mm(MA[:, a * T:(a + 1) * T], win[:, k, m * P:(m + 1) * P], xnT[:, k, :],
                                      start=(k == 0), stop=(k == HC - 1))
                    last.then_inc(sig["inproj_ps"], 1)
                if step == 7:
                    after(pe, "inproj_read", i, 4)
                    after(pe, "u_ready", i, 1)
                    for k in range(IC):
                        last = mm(MA[:, 0:T], wx[:, k, :], u[:, k, :], start=(k == 0), stop=(k == IC - 1))
                    last.then_inc(sig["xproj_ps"], 1)
                if step == 8:
                    after(pe, "xsq", i, 1)
                    mm(MA[:, T:2 * T], cst[:, C_MEAN:C_MEAN + P], xsq, start=True,
                       stop=True).then_inc(sig["meansq_ps"], 1)
                if step == 9:
                    after(pe, "xdn_ready", i, 1)
                    for j in range(2):
                        if j:
                            after(pe, "dt_read", i, 1)
                        for a in range(2):
                            m = 2 * j + a
                            last = mm(MA[:, a * T:(a + 1) * T], wdt[:, m * P:(m + 1) * P], xdn[0:R, :],
                                      start=True, stop=True)
                        last.then_inc(sig["dt_ps"], 1)
                if step == 10:
                    after(pe, "split_ready", i, 1)
                    after(pe, "dt_read", i, 2)
                    after(pe, "n0T_ready", i - 1, 1)
                    for n in range(2):
                        spread(i, n)

            def spread(i, n):
                for j in range(2):
                    x = 2 * n + j
                    bank = (MA, MB, MY)[x % 3]
                    if x >= 3:
                        after(pe, "bc_read", i, x - 2)
                    for a in range(2):
                        s = 2 * n + a
                        last = mm(bank[:, a * T:(a + 1) * T],
                                  sel[:, j * NS + s:j * NS + s + 1].broadcast_to([P, P]), bcr[:], start=True, stop=True)
                    last.then_inc(sig["bc_ps"], 1)

            def unit(i, k):
                if k < PAIRS - 2:
                    spread(i, k + 2)
                if UNITS // 2 - 2 <= k < UNITS // 2 - 2 + PAIRS:
                    spread(i, k - (UNITS // 2 - 2) + PAIRS)

            def mlstm(i, step):
                if step == 1:
                    after(pe, "bc_read", i, 16)
                    after(pe, "y_ready", i, 4)
                    for b in range(GB):
                        for k in range(IC):
                            last = mm(MY[:, b * H:(b + 1) * H], gate[:, k, b * L:(b + 1) * L], wout[:, k, :],
                                      start=(k == 0), stop=(k == IC - 1))
                    last.then_inc(sig["outproj_ps"], 1)
                    after(pe, "c_loaded", i, 16)
                    rows_to_T(MB, cr).then_inc(sig["ctxT_ps"], 1)
                if step == 2:
                    after(pe, "ln2_rows", i, 1)
                    rows_to_T(MY, mrow).then_inc(sig["qT_ps"], 1)
                if step == 3:
                    after(pe, "ctxT_ready", i, 1)
                    after(pe, "qT_ready", i, 1)
                    for k in range(3 * HC):
                        src = mqT if k < HC else ctxT
                        last = mm(MB[0:GROWS, 0:T], wgate[:, k, :], src[:, k % HC, :],
                                  start=(k == 0), stop=(k == 3 * HC - 1))
                    last.then_inc(sig["gate_ps"], 1)
                if step == 4:
                    after(pe, "gates_ready", i, 1)
                    after(pe, "qpad_ready", i, 1)
                    decay_rows(i, 0)
                    for j, src in enumerate((grow, gtop)):
                        for b in range(GB):
                            last = tr(MB[:, (j * GB + b) * XH:(j * GB + b + 1) * XH], src[:, b * L:(b + 1) * L],
                                      cst[0:XH, C_ID:C_ID + XH])
                    last.then_inc(sig["gates_ps"], 1)
                    after(pe, "gates_rows", i, 1)
                    head_scores(i, 0)
                if step == 5:
                    after(pe, "dT_ready", i, 1)
                    decay_rows(i, 1)
                    after(pe, "vaug_ready", i, 1)
                    head_values(i, 0)
                if step == 6:
                    after(pe, "h_read", i, 1)
                    head_scores(i, 1)
                if step == 7:
                    head_values(i, 1)

            def decay_rows(i, hp):
                for a in range(2):
                    h = 2 * hp + a
                    mm(MY[:, a * T:(a + 1) * T], negid[0:XH, h:h + 1].broadcast_to([XH, P]), gmax,
                       start=True, stop=False)
                    last = mm(MY[:, a * T:(a + 1) * T], ident_bf[:],
                              causal[:].unsqueeze(1).broadcast_to([P, GB, L]), start=False, stop=True)
                last.then_inc(sig["dbc_ps"], 1)

            def head_scores(i, hp):
                for b in range(GB):
                    last = mm(MB[:].rearrange("p (a b t) -> p a b t", a=2, b=GB)[:, :, b, :],
                              ctxT[:, hp, b * L:(b + 1) * L], qpad[:, hp, :, b, :], start=True, stop=True)
                last.then_inc(sig["sT_ps"], 1)

            def head_values(i, hp):
                after(pe, "cT_ready", i, hp + 1)
                for b in range(GB):
                    for a in range(2):
                        j = b * 2 + a
                        last = mm(MB[:, j * XP:(j + 1) * XP], cT[:, a, b, :], vaug[:, b, 2 * hp + a, :],
                                  start=True, stop=True)
                last.then_inc(sig["h_ps"], 1)

            def mlstm_out(i, step):
                if step == 0:
                    return
                after(pe, "ln3_rows", i, 1)
                rows_to_T(MB, mrow).then_inc(sig["n0T_ps"], 1)

            def project(bank, w, src, done):
                for a in range(HC):
                    for k in range(HC):
                        last = mm(bank[:, a * T:(a + 1) * T], w[:, k, a * P:(a + 1) * P], src[:, k, :],
                                  start=(k == 0), stop=(k == HC - 1))
                last.then_inc(sig[done], 1)

            def node_proj(i, c):
                g = GRAPH[c]
                if c == 0:
                    after(pe, "n0T_ready", i, 1)
                    project(FX, wk_f[c], node[SLOT[g["k"]]], "k_ps")
                early = c >= 2
                if early:
                    values(c, 0)
                if c >= 1:
                    after(pe, "node_ready", i, c)
                project(FP, wq_f[c], node[SLOT[g["q"]]], "q_ps")
                if not early:
                    values(c, 0)
                values(c, 1).then_inc(sig["v_ps"], 1)

            def values(c, b):
                for k in range(HC):
                    last = mm(FY[:, b * H:(b + 1) * H], node[SLOT[GRAPH[c]["v"]]][:, k, b * L:(b + 1) * L],
                              wv_f[c][:, k, :], start=(k == 0), stop=(k == HC - 1))
                return last

            def node_max(i, c):
                for n, (s, bank) in enumerate(SMAX):
                    b, m = s // HC, s % HC
                    after(pe, "qk_max_ready", i, 2 * c + m + 1)
                    if c == 0 and bank is FQ:
                        after(pe, "out_ready", i, 0)
                    for h in range(HPC):
                        last = mm(bank[:, h * L:(h + 1) * L], qheadr[:, s, h, :], kTr[:, m, b * L:(b + 1) * L],
                                  start=True, stop=True)
                    last.then_inc(sig["smax_ps"], 1)

            def node_score(i, c):
                after(pe, "qhead_ready", i, c + 1)
                after(pe, "smax_read", i, c * STEPS + 1)
                scores(0)
                after(pe, "v_ready", i, c + 1)
                scores(1)
                after(pe, "smax_read", i, (c + 1) * STEPS)
                tr(FV[0:GB * FH, 0:P], mx[:], ident).then_inc(sig["maxT_ps"], 1)
                after(pe, "maxT_ready", i, c + 1)
                for s in range(2):
                    less_max(s)

            def scores(s):
                b, m = s // HC, s % HC
                mm((FX, FY)[s % 2][:], kT[:, m, b * L:(b + 1) * L], qhead[:, s].rearrange("p h t -> p (h t)"),
                   start=True, stop=False, skip_group_check=True)

            def less_max(s):
                bank = (FX, FY)[s % 2]
                for h in range(HPC):
                    j = s * HPC + h
                    last = mm(bank[:, h * L:(h + 1) * L], negid_bf[:, j:j + 1].broadcast_to([P, P]),
                              mxT[:], start=False, stop=(h == HPC - 1), skip_group_check=True)
                last.then_inc(sig["score_ps"], 1)

            def node_attend(i, cs_):
                c, s = cs_ // STEPS, cs_ % STEPS
                b, m = s // HC, s % HC
                after(pe, "prob", i, c * STEPS + s + 1)
                for h in range(HPC):
                    r0 = FD * h
                    at = (m * GB + b) * L
                    mm(FP[r0:r0 + FD, at:at + L], vrow[:, b, m * P + r0:m * P + r0 + FD], pr[s % 2][:, h, :],
                       start=True, stop=True, tile_position=(0, r0))
                    last = mm(FQ[r0:r0 + FD, at:at + L], ones[:, 0:FD], pr[s % 2][:, h, :],
                              start=True, stop=True, tile_position=(0, r0))
                last.then_inc(sig["attn_ps"], 1)
                if s + 2 < STEPS:
                    scores(s + 2)
                    less_max(s + 2)

            def node_out(i, c):
                src = node[SLOT[GRAPH[c]["q"]]]
                for a in range(HC):
                    for k in range(HC):
                        mm(FV[:, a * T:(a + 1) * T], we_f[c][:, k, a * P:(a + 1) * P], src[:, k, :],
                           start=(a == 0 and k == 0), stop=False, skip_group_check=True)
                if c + 1 < NODES:
                    project(FX, wk_f[c + 1], node[SLOT[GRAPH[c + 1]["k"]]], "k_ps")
                after(pe, "attn_ready", i, c + 1)
                for a in range(HC):
                    for k in range(HC):
                        last = mm(FV[:, a * T:(a + 1) * T], wo_f[c][:, k, a * P:(a + 1) * P], aT[:, k, :],
                                  start=False, stop=(k == HC - 1), skip_group_check=True)
                last.then_inc(sig["node_ps"], 1)

            def ffn_out(i, _):
                after(pe, "node_ready", i, NODES)
                for b in range(GB):
                    for a in range(HC):
                        last = tr(FQ[:, b * H + a * P:b * H + (a + 1) * P],
                                  node[SLOT[NODES - 1]][:, a, b * L:(b + 1) * L], ident)
                last.then_inc(sig["rows_ps"], 1)

            steps = dict(pprep=prep, ain=mamba_in, munit=unit, mml=mlstm, mout=mlstm_out, fproj=node_proj, gproj=node_proj,
                         fmax=node_max, fscore=node_score, fattend=node_attend, fnode=node_out, fout=ffn_out)
            pe.wait_ge(sig["const_loaded"], 16 * 8)
            pe.wait_ge(sig["vec_consts"], 1)
            pe.wait_ge(sig["pool_consts"], 1)
            walk(FIRST_IN, steps, None, -1)
            walk(FIRST, steps, None, 0)
            pe.wait_ge(sig["prep_made"], 1)
            pe.wait_ge(sig["pool_zeros"], 1)
            walk(F_START, steps, 0, None)
            with pe.Fori(0, NG - 2) as i:
                walk(BODY, steps, i, i + 1)
            walk(BODY_END, steps, NG - 2, NG - 1)
            walk(F_ALL + F_OUT, steps, NG - 1, None)

        @block.scalar
        def _(act):
            fn = nc.scalar.activation

            a_chain, m_chain, f_chain = Chain(act, "act_a"), Chain(act, "act_m"), Chain(act, "act_f")

            def rstd_of(chain, var_sig, done_sig, i, dst):
                after(act, var_sig, i, 1)
                chain.link(fn(dst, dst, ACT.Ln))
                fn(dst, dst, ACT.Exp, scale=-0.5).then_inc(sig[done_sig], 1)

            def prep(_, n):
                c, part = n // 3, n % 3
                if part:
                    return
                for j, (w, e) in enumerate(((wq_f, 0), (wk_f, 1), (wv_f, 2))):
                    act.wait_ge(sig["prep_ps"], 3 * c + j + 1)
                    bank = (FP, FQ, FX)[j]
                    fn(w[c][:].rearrange("p a b -> p (a b)"), bank[:], ACT.Copy,
                       scale=vec[:, V_EW + 3 * c + e:V_EW + 3 * c + e + 1]).then_inc(sig["prep_read"], 1)

            def mamba_in(i, step):
                if step == 0:
                    a_chain.start(i)
                    rstd_of(a_chain, "ln_var1", "ln_rstd1", i, rstd[:])
                if step == 1:
                    after(act, "xnT_ps", i, 1)
                    fn(xnT[:].rearrange("p a b -> p (a b)"), MA[:], ACT.Copy).then_inc(sig["xnT_ready"], 1)
                if step in (2, 3):
                    j = step - 2
                    after(act, "state", i - 1, UNITS)
                    after(act, "inproj_ps", i, j + 1)
                    for a in range(2):
                        last = fn(hs_pad[:, 2 * j + a, :, 1:L + 1],
                                  MA[:, a * T:(a + 1) * T].rearrange("p (b t) -> p b t", b=GB), ACT.Copy)
                    last.then_inc(sig["inproj_read"], 1)
                if step in (4, 5):
                    j = step - 2
                    after(act, "outproj_ps", i, 0)
                    after(act, "inproj_ps", i, j + 1)
                    fn(gate[:, 2 * j - 4:2 * j - 2, :].rearrange("p a b -> p (a b)"), MA[:], ACT.Copy,
                       scale=0.5).then_inc(sig["inproj_read"], 1)
                if step == 5:
                    after(act, "inproj_read", i, 4)
                    fn(dt[:], gate[:], ACT.Tanh).then_inc(sig["tanh_g"], 1)
                    after(act, "conv_done", i, 1)
                    fn(th[:], u[:], ACT.Tanh).then_inc(sig["tanh_u"], 1)
                    act.preload_act_table_set("natural_log_exp_and_others")
                if step == 7:
                    after(act, "xproj_ps", i, 1)
                    fn(xsq, MA[:, 0:T], ACT.Square).then_inc(sig["xsq"], 1)
                if step == 8:
                    after(act, "meansq_ps", i, 1)
                    a_chain.link(fn(xrs, MA[:, T:2 * T], ACT.Ln, bias=RMS_EPS))
                    fn(xrs, xrs, ACT.Exp, scale=-0.5).then_inc(sig["rms_rstd"], 1)
                if step == 9:
                    for c in range(IC):
                        if c % 2 == 0:
                            after(act, "dt_ps", i, c // 2 + 1)
                        last = fn(dt[:, c, :], MA[:, (c % 2) * T:(c % 2 + 1) * T], ACT.Identity,
                                  bias=vec[:, V_DTB + c:V_DTB + c + 1])
                        if c % 2:
                            last.then_inc(sig["dt_read"], 1)
                    after(act, "dt_read", i, 2)
                    after(act, "split_ready", i, 1)
                    a_chain.link(fn(th[:], dt[:], ACT.Abs))
                    a_chain.link(fn(th[:], th[:], ACT.Exp, scale=-1.0))
                    fn(th[:], th[:], ACT.Ln, bias=1.0).then_inc(sig["sp_tail"], 1)
                    a_chain.end()
                if step == 10:
                    after(act, "x2_ready", i - 1, 1)
                    for n in range(2):
                        copies(i, n)

            def copies(i, n):
                q = n % PAIRS
                for j, dst in enumerate((bs, cs)):
                    x = 2 * n + j
                    after(act, "bc_ps", i, x + 1)
                    if n >= PAIRS:
                        after(act, ("state", "outflow")[j], i, UNITS // 2 - PAIRS + q + 1)
                    bank = (MA, MB, MY)[x % 3]
                    fn(dst[:, q].rearrange("p a b -> p (a b)"), bank[:], ACT.Copy).then_inc(sig["bc_read"], 1)

            def unit(i, k):
                hf, c, q = k // (UNITS // 2), k // PAIRS % IC, k % PAIRS
                if k == 0:
                    m_chain.start(i)
                    after(act, "dt_ready", i, 1)
                if k == PAIRS:
                    after(act, "x_loaded", i, 16)
                    after(act, "ln1_rows", i, 1)
                    after(act, "res_ready", i - 1, 1)
                    fn(xr[:], xin[:], ACT.Copy).then_inc(sig["x_kept"], 1)
                if k >= 2:
                    after(act, "state", i, k - 1)
                for a in range(2):
                    s = hf * (NS // 2) + 2 * q + a
                    last = fn(dec[k % 2][:, a, :, 1:L],
                              dt[:, c, :].rearrange("p (b t) -> p b t", b=GB)[:, :, 1:L], ACT.Exp,
                              scale=a_neg[:, c * NS + s:c * NS + s + 1])
                last.then_inc(sig["decay"], 1)
                if k < PAIRS - 2:
                    copies(i, k + 2)
                if UNITS // 2 - 2 <= k < UNITS // 2 - 2 + PAIRS:
                    copies(i, k - (UNITS // 2 - 2) + PAIRS)

            def mlstm(i, step):
                if step == 1:
                    rstd_of(m_chain, "ln_var2", "ln_rstd2", i, mrstd[:])
                    after(act, "ctxT_ps", i, 1)
                    fn(ctxT[:].rearrange("p a b -> p (a b)"), MB[:], ACT.Copy).then_inc(sig["ctxT_ready"], 1)
                if step == 2:
                    after(act, "qT_ps", i, 1)
                    fn(mqT.rearrange("p a b -> p (a b)"), MY[:], ACT.Copy).then_inc(sig["qT_ready"], 1)
                    after(act, "qpad_clear", i, 1)
                    for a in range(2):
                        rs = slice(XD * a, XD * (a + 1))
                        last = fn(qpad[rs, :, a, :, :].rearrange("p c b t -> p c (b t)"),
                                  MY[rs, :].rearrange("p (c n) -> p c n", c=HC), ACT.Copy)
                    last.then_inc(sig["qpad_ready"], 1)
                if step == 3:
                    after(act, "gate_ps", i, 1)
                    fn(grow, MB[0:XH, 0:T], ACT.Identity, bias=vec[0:XH, V_GBI:V_GBI + 1])
                    fn(gfm, MB[GF:GROWS, 0:T], ACT.Identity, bias=vec[GF:GROWS, V_GBI:V_GBI + 1]).then_inc(sig["gate_read"], 1)
                    after(act, "gate_read", i, 1)
                    m_chain.link(fn(gfa, gfm, ACT.Abs))
                    m_chain.link(fn(gfa, gfa, ACT.Exp, scale=-1.0))
                    fn(gfa, gfa, ACT.Ln, bias=1.0).then_inc(sig["gate_tail"], 1)
                if step == 4:
                    after(act, "gates_ps", i, 1)
                    fn(rm[:].rearrange("p a b -> p (a b)"), MB[:, 0:2 * GB * XH], ACT.Copy).then_inc(sig["gates_rows"], 1)
                    after(act, "gates_rows", i, 1)
                    fn(em[:], rm[:, 1, :], ACT.Exp, scale=-1.0).then_inc(sig["em_ready"], 1)
                if step in (4, 6):
                    hp = (step - 4) // 2
                    after(act, "dbc_ps", i, hp + 1)
                    if hp:
                        after(act, "cT_ready", i, 1)
                    for a in range(2):
                        for b in range(GB):
                            h = 2 * hp + a
                            last = fn(dT[:, a, b, :], MY[:, a * T + b * L:a * T + (b + 1) * L], ACT.Exp,
                                      bias=rm[:, 0, b * XH + h:b * XH + h + 1])
                    last.then_inc(sig["dT_ready"], 1)
                if step == 8:
                    rstd_of(m_chain, "hvar", "hrstd", i, hva[:])

            def mlstm_out(i, step):
                if step == 0:
                    rstd_of(m_chain, "ln_var3", "ln_rstd3", i, mrstd[:])
                    return
                after(act, "n0T_ps", i, 1)
                after(act, "k_ps", i - 1, NODES - 1)
                fn(node[0][:].rearrange("p a b -> p (a b)"), MB[:], ACT.Copy).then_inc(sig["n0T_ready"], 1)
                m_chain.end()

            def keep_x2(i, _):
                after(act, "out_ready", i, 0)
                after(act, "x2_ready", i, 1)
                fn(res[:], xr[:], ACT.Copy).then_inc(sig["res_ready"], 1)

            def node_proj(i, c):
                if c == 0:
                    keys(i, c)
                after(act, "q_ps", i, c + 1)
                for a in range(HC):
                    fn(qT[:, a, :], FP[:, a * T:(a + 1) * T], ACT.Identity,
                       bias=fb[:, c, a:a + 1]).then_inc(sig["q_read"], 1)
                after(act, "q_read", i, 2 * c + 2)
                for h in range(HPC):
                    rs = slice(FD * h, FD * (h + 1))
                    last = fn(qhead[rs, :, h, :].rearrange("p (b m) t -> p b m t", b=GB),
                              qT[rs].rearrange("p m (b t) -> p b m t", b=GB), ACT.Copy)
                last.then_inc(sig["qhead_ready"], 1)
                after(act, "v_ps", i, c + 1)
                fn(vrow[:].rearrange("p a b -> p (a b)"), FY[:], ACT.Copy).then_inc(sig["v_ready"], 1)

            def keys(i, c):
                after(act, "k_ps", i, c + 1)
                for a in range(HC):
                    last = fn(kT[:, a, :], FX[:, a * T:(a + 1) * T], ACT.Identity, bias=fb[:, c, 2 + a:3 + a])
                last.then_inc(sig["k_read"], 1)

            def node_score(i, c):
                if c == 0:
                    f_chain.start(i)
                after(act, "maxT_ps", i, c + 1)
                fn(mxT[0:GB * FH, :], FV[0:GB * FH, 0:P], ACT.Copy).then_inc(sig["maxT_ready"], 1)
                node_prob(i, c, 0)

            def node_attend(i, cs_):
                c, s = cs_ // STEPS, cs_ % STEPS
                if s + 1 < STEPS:
                    node_prob(i, c, s + 1)
                else:
                    node_den(i, c)

            def node_prob(i, c, s):
                after(act, "score_ps", i, c * STEPS + s + 1)
                if s >= 2:
                    after(act, "attn_ps", i, c * STEPS + s - 1)
                fn(pr[s % 2][:].rearrange("p a b -> p (a b)"), (FX, FY)[s % 2][:], ACT.Exp,
                   scale=FD ** -0.5).then_inc(sig["prob"], 1)

            def node_den(i, c):
                after(act, "attn_ps", i, (c + 1) * STEPS)
                f_chain.link(fn(dinv[:].rearrange("p a b -> p (a b)"), FQ[:], ACT.Ln))
                fn(dinv[:], dinv[:], ACT.Exp, scale=-1.0).then_inc(sig["den_inv"], 1)

            def node_out(i, c):
                if c + 1 < NODES:
                    keys(i, c + 1)
                after(act, "node_ps", i, c + 1)
                for a in range(HC):
                    last = fn(node[SLOT[c]][:, a, :], FV[:, a * T:(a + 1) * T], ACT.Identity,
                              bias=fb[:, c, 6 + a:7 + a])
                last.then_inc(sig["node_ready"], 1)

            def ffn_out(i, _):
                rstd_of(f_chain, "ln_var4", "ln_rstd4", i, frstd[:])
                f_chain.end()

            steps = dict(pprep=prep, ain=mamba_in, munit=unit, mml=mlstm, mout=mlstm_out, mkeep=keep_x2, fproj=node_proj, gproj=node_proj,
                         fscore=node_score, fattend=node_attend, fnode=node_out, fout=ffn_out)
            act.wait_ge(sig["const_loaded"], 16 * 8)
            act.preload_act_table_set("natural_log_exp_and_others")
            fn(a_neg[:], vec[:, V_ALOG:V_ALOG + IC * NS], ACT.Exp).then_inc(sig["setup_act"], 1)
            act.wait_ge(sig["vec_consts"], 1)
            act.wait_ge(sig["pool_consts"], 1)
            walk(FIRST_IN, steps, None, -1)
            walk(FIRST, steps, None, 0)
            act.wait_ge(sig["pool_zeros"], 1)
            act.wait_ge(sig["prep_made"], 1)
            walk(F_START, steps, 0, None)
            with act.Fori(0, NG - 2) as i:
                act.preload_act_table_set("natural_log_exp_and_others")
                walk(BODY, steps, i, i + 1)
            walk(BODY_END, steps, NG - 2, NG - 1)
            walk(F_ALL + F_OUT, steps, NG - 1, None)

        @block.vector
        def _(dve):
            v = nc.vector
            a_chain, m_chain, f_chain = Chain(dve, "vec_a"), Chain(dve, "vec_m"), Chain(dve, "vec_f")

            def col(n):
                return vec[:, n:n + 1]

            def setup():
                dve.wait_ge(sig["const_loaded"], 16 * 8)
                v.tensor_copy(ident_bf[:], ident)
                v.tensor_scalar(negid_bf[:], cst[:, C_ID:C_ID + GB * FH], -1.0, None, ALU.mult)
                v.tensor_scalar(negid[:], cst[:, C_ID:C_ID + XH], -1.0, None, ALU.mult)
                v.tensor_copy(sel[:], cst[:, C_SEL:C_SEL + 2 * NS])
                v.tensor_copy(causal[:], cst[:, C_CAUSAL:C_CAUSAL + P])
                v.tensor_scalar(convh[:, 0:4], vec[:, V_CONVB:V_CONVB + 4], 0.5, None, ALU.mult)
                v.tensor_scalar(convh[:, 4:20], vec[:, V_CONVW:V_CONVW + 16], 0.5, None, ALU.mult)
                dve.wait_ge(sig["setup_act"], 1)
                v.tensor_scalar(a_neg[:], a_neg[:], -1.0, None, ALU.mult).then_inc(sig["vec_consts"], 1)
                dve.wait_ge(sig["vec_consts"], 1)
                dve.wait_ge(sig["pool_consts"], 1)

            def prep(_, n):
                c, part = n // 3, n % 3
                g = GRAPH[c]
                ew0, ew1, ew2 = (col(V_EW + 3 * c + j) for j in range(3))
                if part == 0:
                    dve.wait_ge(sig["w_loaded"], 16 * 8 * (c + 1))
                    v.tensor_scalar(we_f[c][:], stage["e"], ew0, None, ALU.mult)
                    v.tensor_scalar(wo_f[c][:], stage["o"], col(V_ACTW + c), None, ALU.mult)
                if part == 1:
                    dve.wait_ge(sig["prep_bias_ps"], 2 * c + 1)
                    for j, e in enumerate((ew0, ew1, ew2)):
                        last = v.tensor_scalar(fb[:, c, 2 * j:2 * j + 2], FY[:, 2 * j:2 * j + 2], e, None, ALU.mult)
                    last.then_inc(sig["prep_bias"], 1)
                    v.tensor_scalar(bias_t[:], vec[:, V_BE + g["eq"] * HC:V_BE + (g["eq"] + 1) * HC], ew0, None,
                                    ALU.mult).then_inc(sig["prep_vec"], 1)
                if part == 2:
                    dve.wait_ge(sig["prep_bias_ps"], 2 * c + 2)
                    dve.wait_ge(sig["prep_vec"], c + 1)
                    v.scalar_tensor_tensor(fb[:, c, 6:8], FY[:, 8:10], col(V_ACTW + c), bias_t[:], ALU.mult,
                                           ALU.add).then_inc(sig["prep_bias"], 1)
                    dve.wait_ge(sig["prep_bias"], 2 * c + 2)
                    dve.sem_inc(sig["w_used"], 1)

            def layer_norm(i, chain, n, src, mean_var, stats, inv, eps, dst):
                for b in range(GB):
                    m = chain.mark(v.bn_stats(stats[:, b, :], src(b)))
                chain.wait(m)
                dve.sem_inc(sig["stats_seen"], 1)
                for b in range(GB):
                    m = chain.mark(v.bn_aggr(mean_var[:, b, :], stats[:, b, :]))
                chain.wait(m)
                v.tensor_scalar(inv[:], mean_var[:, :, 1], eps, None, ALU.add).then_inc(sig[f"ln_var{n}"], 1)
                after(dve, f"ln_rstd{n}", i, 1)
                for b in range(GB):
                    last = v.tensor_scalar(dst[:, b, :], src(b), mean_var[:, b, 0:1], inv[:, b:b + 1],
                                           ALU.subtract, ALU.mult)
                return last

            def mamba_in(i, step):
                if step == 0:
                    a_chain.start(i)
                    after(dve, "x_loaded", i, 16)
                    layer_norm(i, a_chain, 1, lambda b: xin[:, b, :], mv, bn, rstd, LN_EPS, rows).then_inc(sig["ln1_rows"], 1)
                if step == 4:
                    after(dve, "inproj_read", i, 2)
                    marks = [a_chain.mark(v.tensor_scalar(u[:, c, :].rearrange("p (b t) -> p b t", b=GB),
                                                          hs_pad[:, c, :, 0:L], convh[:, 4 + c * 4:5 + c * 4],
                                                          convh[:, c:c + 1], ALU.mult, ALU.add)) for c in range(IC)]
                    for k in range(1, 4):
                        for c in range(IC):
                            a_chain.wait(marks[c])
                            uc = u[:, c, :].rearrange("p (b t) -> p b t", b=GB)
                            ins = v.scalar_tensor_tensor(uc, hs_pad[:, c, :, k:k + L],
                                                         convh[:, 4 + c * 4 + k:5 + c * 4 + k], uc, ALU.mult, ALU.add)
                            if k < 3:
                                marks[c] = a_chain.mark(ins)
                    ins.then_inc(sig["conv_done"], 1)
                if step == 6:
                    after(dve, "tanh_g", i, 1)
                    v.scalar_tensor_tensor(gate[:], dt[:], 1.0, gate[:], ALU.add, ALU.mult)
                    after(dve, "tanh_u", i, 1)
                    v.scalar_tensor_tensor(u[:], th[:], 1.0, u[:], ALU.add, ALU.mult).then_inc(sig["u_ready"], 1)
                if step == 8:
                    after(dve, "rms_rstd", i, 1)
                    v.scalar_tensor_tensor(xdn[:], MA[:, 0:T], col(V_NORM), xrs, ALU.mult,
                                           ALU.mult).then_inc(sig["xdn_ready"], 1)
                    after(dve, "xdn_ready", i, 1)
                    a_chain.link(v.tensor_copy(bhi, xdn[:]))
                    v.scalar_tensor_tensor(bcr[:], th[:, 0, :], cst[:, C_LO:C_LO + 1], xdn[:],
                                           ALU.mult, ALU.add).then_inc(sig["split_ready"], 1)
                if step == 10:
                    after(dve, "sp_tail", i, 1)
                    v.scalar_tensor_tensor(dt[:], dt[:], 0.0, th[:], ALU.max, ALU.add).then_inc(sig["dt_ready"], 1)
                    after(dve, "dt_ready", i, 1)
                    v.tensor_tensor(dtu, dt[:].rearrange("p c (b t) -> p c b t", b=GB),
                                    u[:].rearrange("p c (b t) -> p c b t", b=GB), ALU.mult).then_inc(sig["dtu_ready"], 1)
                    a_chain.end()

            def scan(i, k):
                if k in INFLOW_V:
                    after(dve, "bc_read", i, 2 * (k // (UNITS // 2) * PAIRS + k % PAIRS) + 1)
                    after(dve, "state", i, k - 1)
                    inflow(v, k).then_inc(sig["inflow_v"], 1)
                after(dve, "decay", i, k + 1)
                inflow_done(dve, i, k)
                if k >= 3:
                    after(dve, "outflow", i, k - 2)
                v.tensor_tensor_scan(hst[k % 3][:].rearrange("p a b -> p (a b)"),
                                     dec[k % 2][:].rearrange("p a b t -> p (a b t)"),
                                     inf[k % 2][:].rearrange("p a b -> p (a b)"), 0.0, ALU.mult,
                                     ALU.add).then_inc(sig["state"], 1)

            def weigh(i, k):
                q = k % PAIRS
                after(dve, "state", i, k + 1)
                if k >= 3:
                    after(dve, "ysum", i, added(k - 3))
                after(dve, "bc_read", i, 2 * (k // (UNITS // 2) * PAIRS + q) + 2)
                v.tensor_tensor(prd[k % 3][:], hst[k % 3][:], cs[:, q], ALU.mult).then_inc(sig["outflow"], 1)

            def gather(i, m):
                hf, c = m // IC, m % IC
                after(dve, "ysum", i, (m + 1) * PAIRS)
                if m >= IC:
                    after(dve, "y_read", i, c + 1)
                src = ych[m % 2][:]
                if hf == 0:
                    v.scalar_tensor_tensor(u[:, c, :], u[:, c, :], col(V_D + c), src, ALU.mult,
                                           ALU.add).then_inc(sig["y_read"], 1)
                else:
                    v.tensor_tensor(u[:, c, :], u[:, c, :], src, ALU.add).then_inc(sig["y_read"], 1)
                    after(dve, "y_read", i, m + 1)
                    v.tensor_tensor(gate[:, c, :], gate[:, c, :], u[:, c, :], ALU.mult).then_inc(sig["y_ready"], 1)

            def unit(i, k):
                if k == 0:
                    m_chain.start(i)
                if k >= 1:
                    weigh(i, k - 1)
                scan(i, k)
                if k % PAIRS == 2 and k > PAIRS:
                    gather(i, k // PAIRS - 1)

            def head_rows(i, hp):
                after(dve, "h_ps", i, hp + 1)
                v.tensor_copy(hrow[:, :, 2 * hp:2 * hp + 2, :],
                              MB[:, 0:2 * GB * XP].rearrange("p (b a d) -> p b a d", b=GB, a=2)
                              ).then_inc(sig["h_read"], 1)

            def mlstm(i, step):
                if step == 0:
                    weigh(i, UNITS - 1)
                    gather(i, 2 * IC - 1)
                if step == 1:
                    after(dve, "outproj_ps", i, 1)
                    after(dve, "x_kept", i, 1)
                    v.tensor_tensor(xr[:].rearrange("p a b -> p (a b)"), xr[:].rearrange("p a b -> p (a b)"), MY[:],
                                    ALU.add).then_inc(sig["x1_ready"], 1)
                    after(dve, "x1_ready", i, 1)
                    layer_norm(i, m_chain, 2, lambda b: xr[:, b, :], mmv, mbn, mrstd, LN_EPS, mrow).then_inc(sig["ln2_rows"], 1)
                if step == 3:
                    after(dve, "gate_tail", i, 1)
                    m_chain.link(v.scalar_tensor_tensor(gfm, gfm, 0.0, gfa, ALU.min, ALU.subtract))
                    for b in range(GB):
                        m = m_chain.mark(v.tensor_tensor_scan(gcum[:, b * L:(b + 1) * L], ones[0:XH, 0:L],
                                                              gfm[:, b * L:(b + 1) * L], 0.0, ALU.mult, ALU.add))
                    m_chain.wait(m)
                    m_chain.link(v.tensor_tensor(grow, grow, gcum, ALU.subtract))
                    for b in range(GB):
                        m = m_chain.mark(v.tensor_tensor_scan(gmax[:, b * L:(b + 1) * L], grow[:, b * L:(b + 1) * L],
                                                              grow[:, b * L:(b + 1) * L], -BIG, ALU.max, ALU.max))
                    m_chain.wait(m)
                    v.tensor_tensor(gtop, gcum, gmax, ALU.add).then_inc(sig["gates_ready"], 1)
                if step == 5:
                    head_rows(i, 0)
                if step in (4, 6):
                    hp = (step - 4) // 2
                    after(dve, "sT_ps", i, hp + 1)
                    after(dve, "dT_ready", i, hp + 1)
                    v.scalar_tensor_tensor(cT.rearrange("p a b t -> p (a b t)"), MB[:], XD ** -0.5,
                                           dT.rearrange("p a b t -> p (a b t)"), ALU.mult,
                                           ALU.mult).then_inc(sig["cT_ready"], 1)
                if step == 7:
                    head_rows(i, 1)
                if step == 8:
                    after(dve, "h_read", i, 2)
                    after(dve, "em_ready", i, 1)
                    hall = hrow[:].rearrange("p b h d -> p (b h) d")
                    wide = [P, GB * XH, XD]
                    m_chain.link(v.scalar_tensor_tensor(den[:], hall[:, :, XD], -1.0, hall[:, :, XD], ALU.mult, ALU.max))
                    m_chain.link(v.tensor_tensor(den[:], den[:], em[:], ALU.max))
                    m_chain.link(v.tensor_scalar(den[:], den[:], HEAD_EPS, None, ALU.add))
                    m_chain.link(v.reciprocal(den[:], den[:]))
                    m_chain.link(v.tensor_tensor(hn, hall[:, :, 0:XD], den[:].unsqueeze(2).broadcast_to(wide), ALU.mult))
                    m_chain.link(v.tensor_reduce(hmu[:], hn, AX.X, ALU.add))
                    m_chain.link(v.tensor_scalar(hmu[:], hmu[:], 1.0 / XD, None, ALU.mult))
                    m_chain.link(v.tensor_tensor(hn, hn, hmu[:].unsqueeze(2).broadcast_to(wide), ALU.subtract))
                    m_chain.link(v.tensor_tensor(hsq, hn, hn, ALU.mult))
                    m_chain.link(v.tensor_reduce(hva[:], hsq, AX.X, ALU.add))
                    v.tensor_scalar(hva[:], hva[:], 1.0 / XD, HEAD_EPS, ALU.mult, ALU.add).then_inc(sig["hvar"], 1)
                    after(dve, "hrstd", i, 1)
                    m_chain.link(v.tensor_tensor(hn, hn, hva[:].unsqueeze(2).broadcast_to(wide), ALU.mult))
                    hb = hn.rearrange("p (b h) d -> p b (h d)", b=GB)
                    m_chain.link(v.tensor_tensor(hb, hb, rowv[:, 0:1, :].broadcast_to([P, GB, H]), ALU.mult))

            def mlstm_out(i, step):
                if step == 1:
                    return
                v.tensor_tensor(xr[:].rearrange("p a b -> p (a b)"), xr[:].rearrange("p a b -> p (a b)"),
                                hn.rearrange("p a b -> p (a b)"), ALU.add).then_inc(sig["x2_ready"], 1)
                after(dve, "x2_ready", i, 1)
                layer_norm(i, m_chain, 3, lambda b: xr[:, b, :], mmv, mbn, mrstd, LN_EPS, mrow).then_inc(sig["ln3_rows"], 1)
                m_chain.end()

            def node_proj(i, c):
                after(dve, "k_read", i, c + 1)
                v.tensor_copy(kTr[:], kT[:])
                for m in range(HC):
                    after(dve, "q_read", i, 2 * c + m + 1)
                    for h in range(HPC):
                        rs = slice(FD * h, FD * (h + 1))
                        last = v.tensor_copy(qheadr[rs, :, h, :].rearrange("p (b m) t -> p b m t", b=GB)[:, :, m, :],
                                             qT[rs, m, :].rearrange("p (b t) -> p b t", b=GB))
                    last.then_inc(sig["qk_max_ready"], 1)

            def node_max(i, c):
                for n, (s, bank) in enumerate(SMAX):
                    after(dve, "smax_ps", i, c * STEPS + n + 1)
                    v.tensor_reduce(mx[:, s * HPC:(s + 1) * HPC], bank[:].rearrange("p (h k) -> p h k", h=HPC),
                                    AX.X, ALU.max).then_inc(sig["smax_read"], 1)

            def node_attend(i, cs_):
                c, s = cs_ // STEPS, cs_ % STEPS
                if s < STEPS - 1:
                    return
                after(dve, "den_inv", i, c + 1)
                v.tensor_tensor(aT[:].rearrange("p a b -> p (a b)"), FP[:], dinv[:].rearrange("p a b -> p (a b)"),
                                ALU.mult).then_inc(sig["attn_ready"], 1)

            def ffn_out(i, _):
                f_chain.start(i)
                after(dve, "res_ready", i, 1)
                after(dve, "rows_ps", i, 1)
                after(dve, "out_stored", i, 0)
                f_chain.link(layer_norm(i, f_chain, 4, lambda b: FQ[:, b * H:(b + 1) * H], fmv, fbn, frstd, OUT_EPS,
                                        orow))
                f_chain.link(v.tensor_tensor(orow[:], orow[:], rowv[:, 1:2, :].broadcast_to([P, GB, H]), ALU.mult))
                f_chain.link(v.tensor_tensor(orow[:], orow[:], rowv[:, 2:3, :].broadcast_to([P, GB, H]), ALU.add))
                v.tensor_tensor(orow[:], orow[:], res[:], ALU.add).then_inc(sig["out_ready"], 1)
                f_chain.end()

            steps = dict(pprep=prep, ain=mamba_in, munit=unit, mml=mlstm, mout=mlstm_out, fproj=node_proj, gproj=node_proj,
                         fmax=node_max, fattend=node_attend, fout=ffn_out)
            setup()
            walk(FIRST_IN, steps, None, -1)
            walk(FIRST, steps, None, 0)
            dve.wait_ge(sig["pool_zeros"], 1)
            dve.wait_ge(sig["prep_read"], 3 * NODES)
            dve.wait_ge(sig["prep_bias"], 2 * NODES)
            dve.sem_inc(sig["prep_made"], 1)
            walk(F_START, steps, 0, None)
            with dve.Fori(0, NG - 2) as i:
                walk(BODY, steps, i, i + 1)
            walk(BODY_END, steps, NG - 2, NG - 1)
            walk(F_ALL + F_OUT, steps, NG - 1, None)

        @block.gpsimd
        def _(pool):
            g = nc.gpsimd
            g.memset(ones[:], 1.0)
            g.memset(hs_pad[:].rearrange("p a b t -> p (a b t)"), 0.0)
            for j in range(2):
                g.memset(dec[j][:].rearrange("p a b t -> p (a b t)"), 0.0)
            g.memset(vaug[:].rearrange("p b h d -> p (b h d)"), 1.0).then_inc(sig["pool_consts"], 1)
            g.memset(qhead[:].rearrange("p s h t -> p (s h t)"), 0.0)
            g.memset(qheadr[:].rearrange("p s h t -> p (s h t)").bitcast(F32), 0.0)
            g.memset(mxT[:], 0.0).then_inc(sig["pool_zeros"], 1)

            def unit(i, k):
                if k == 0:
                    after(pool, "dtu_ready", i, 1)
                if k not in INFLOW_V:
                    after(pool, "bc_read", i, 2 * (k // (UNITS // 2) * PAIRS + k % PAIRS) + 1)
                    if k >= 2:
                        after(pool, "state", i, k - 1)
                    inflow(g, k).then_inc(sig["inflow"], 1)
                if k >= 2:
                    add(i, k - 2)

            def add(i, k):
                m, q = k // PAIRS, k % PAIRS
                if q == 0:
                    return
                after(pool, "outflow", i, k + 1)
                if q == 1:
                    if m >= 1:
                        after(pool, "ysum", i, m * PAIRS)
                    g.tensor_tensor(acc[:], prd[(k - 1) % 3][:], prd[k % 3][:], ALU.add).then_inc(sig["ysum"], 1)
                else:
                    after(pool, "ysum", i, m * PAIRS + q - 1)
                    g.tensor_tensor(acc[:], acc[:], prd[k % 3][:], ALU.add).then_inc(sig["ysum"], 1)
                if q == PAIRS - 1:
                    after(pool, "ysum", i, m * PAIRS + q)
                    if m >= 2:
                        after(pool, "y_read", i, m - 1)
                    g.tensor_tensor(ych[m % 2][:], acc[:, 0, :], acc[:, 1, :], ALU.add).then_inc(sig["ysum"], 1)

            def mlstm(i, step):
                if step == 0:
                    add(i, UNITS - 2)
                    add(i, UNITS - 1)
                    g.memset(unit_buf[:, 2:4], 0.0).then_inc(sig["qpad_clear"], 1)
                    after(pool, "c_loaded", i, 16)
                    pool.sem_inc(sig["ctx_seen"], 1)
                    g.tensor_copy(vaug[:, :, :, 0:XD], cr[:].rearrange("p b (h d) -> p b h d", h=XH)
                                  ).then_inc(sig["vaug_ready"], 1)

            steps = dict(munit=unit, mml=mlstm)
            walk(FIRST_IN, steps, None, -1)
            walk(FIRST, steps, None, 0)
            with pool.Fori(0, NG - 2) as i:
                walk(BODY, steps, i, i + 1)
            walk(BODY_END, steps, NG - 2, NG - 1)


def kernel(**inputs):
    import numpy as np
    import concourse.bacc as bacc
    from concourse.bass_utils import run_bass_kernel_spmd

    a = {k: np.asarray(v) for k, v in inputs.items()}

    def chunks(w):
        return np.ascontiguousarray(w.reshape(-1, P, w.shape[-1]).transpose(1, 0, 2))

    def cols(w):
        return w.reshape(w.shape[0] // P, P, -1).transpose(1, 0, 2).reshape(P, -1)

    consts = np.zeros((P, NC_), np.float32)
    consts[:, C_ID:C_ID + P] = np.eye(P)
    consts[0:R, C_MEAN:C_MEAN + R] = 1.0 / R
    for part, base in enumerate((R, R + 32)):
        consts[base:base + NS, C_MEAN + base:C_MEAN + base + 32] = 1.0 / NS
        for s in range(NS):
            consts[[base + s, base + NS + s], C_SEL + part * NS + s] = 1.0
        consts[base + NS:base + 32, C_LO] = -1.0
    consts[:, C_CAUSAL:C_CAUSAL + P] = np.where(np.arange(P)[:, None] <= np.arange(P)[None, :], 0.0, -BIG)

    bn_w, cn_w = a["L0_attn_b_ln_w"], a["L0_attn_c_ln_w"]
    norm = np.concatenate([a["L0_attn_dt_ln_w"], bn_w, bn_w, cn_w, cn_w])
    gbias = np.zeros((P, 1), np.float32)
    gbias[0:XH, 0], gbias[GF:GROWS, 0] = a["L0_xattn_igate_bias"], a["L0_xattn_fgate_bias"]
    vecs = np.concatenate([
        cols(a["L0_attn_conv_b"]), cols(a["L0_attn_dt_proj_b"]), cols(a["L0_attn_D"]),
        cols(a["L0_attn_conv_w"]), cols(a["L0_attn_A_log"]), norm[:, None], gbias,
        a["L0_ffn_be"].reshape(EDGES, HC, P).transpose(2, 0, 1).reshape(P, -1),
        np.broadcast_to(a["L0_ffn_ew"].reshape(1, -1), (P, NODES * 3)),
        np.broadcast_to(a["L0_ffn_act_w"].reshape(1, -1), (P, NODES))], axis=1)
    rowvecs = np.stack([a["L0_xattn_outnorm_scale"], a["L0_ffn_ln_g"], a["L0_ffn_ln_b"]])
    xp = a["L0_attn_x_proj_w"]
    w_x = np.concatenate([xp[0:R], xp[R:R + NS], xp[R:R + NS], xp[R + NS:], xp[R + NS:]])
    gk = np.zeros((3 * H, GROWS), np.float32)
    gk[:, 0:XH], gk[:, GF:GROWS] = a["L0_xattn_igate_kernel"], a["L0_xattn_fgate_kernel"]
    we = a["L0_ffn_We"]

    def many(w):
        return np.ascontiguousarray(np.swapaxes(w.reshape(*w.shape[:-2], HC, P, H), -3, -2))

    arrays = dict(
        x=a["x"], ctx_in=a["ctx_1024"], consts=consts, vecs=np.ascontiguousarray(vecs), rowvecs=rowvecs,
        w_in=chunks(a["L0_attn_in_proj_w"].T), w_x=chunks(w_x.T),
        w_dt=np.ascontiguousarray(a["L0_attn_dt_proj_w"].T), w_out=chunks(a["L0_attn_out_proj_w"].T),
        w_gate=chunks(gk),
        w_edge=many(we), w_edgeT=many(np.swapaxes(we, 1, 2)),
        w_node=many(np.stack([a["L0_ffn_Wq"], a["L0_ffn_Wk"], a["L0_ffn_Wv"], a["L0_ffn_Wo"]])))
    nc = bacc.Bacc("TRN2", target_bir_lowering=False, num_devices=1)
    args = {n: nc.dram_tensor(f"in_{n}", w.shape, mybir.dt.from_np(w.dtype), kind="ExternalInput").ap()
            for n, w in arrays.items()}
    out = nc.dram_tensor("out_dram", (B, L, H), F32, kind="ExternalOutput").ap()
    build(nc, **args, out=out)
    r = run_bass_kernel_spmd(nc, [{f"in_{n}": np.ascontiguousarray(w) for n, w in arrays.items()}], core_ids=[0])
    return r.results[0]["out_dram"]
```
